# Optimizing a Trainium2 kernel written in Bass

```python
import numpy as np
import jax
import jax.numpy as jnp

def _softmax(x, axis=-1):
    return jax.nn.softmax(x, axis=axis)
def _gelu(x):
    return jax.nn.gelu(x, approximate=True)
def _silu(x):
    return jax.nn.silu(x)
def _sigmoid(x):
    return jax.nn.sigmoid(x)
def _layernorm(x, axis=-1, eps=1e-5):
    m = jnp.mean(x, axis=axis, keepdims=True)
    v = jnp.var(x, axis=axis, keepdims=True)
    return (x - m) / jnp.sqrt(v + eps)
def _scatter_add(tgt, idx, src, axis=0):
    return tgt.at[idx].add(src)
def _segment_sum(src, seg, n):
    return jax.ops.segment_sum(src, seg, n)

kernel_name = 'mk_metaformer_d1_conv_nhwc256_08bf8b'

def setup_inputs(seed: int = 0):
    np.random.seed(seed)
    _w = jnp.asarray
    def _rec_inputs():
        import jax
        import jax.numpy as jnp
        _gk = jax.random.key(seed)
        x = 7.22e-05 + 1 * jax.random.normal(jax.random.fold_in(_gk, 1), (8, 64, 64, 256), jnp.float32)
        return x
    x = _rec_inputs()
    def _L0_conv_setup():
        import jax, jax.numpy as jnp
        import numpy as np
        from jax import lax
        NUM_HEADS = 8
        KEY_DIM = 32
        key = jax.random.key(seed)
        ks = jax.random.split(key, 13)
        B, H, W, C = (8, 64, 64, 256)

        def nrm(k, shape, s):
            return jax.random.normal(k, shape, jnp.float32) * s
        return {'x': jax.random.normal(ks[0], (B, H, W, C), jnp.float32), 'mask_h': nrm(ks[1], (NUM_HEADS, H, H), 1.0), 'mask_w': nrm(ks[2], (NUM_HEADS, W, W), 1.0), 'Wq': nrm(ks[3], (C, C), 0.02), 'bq': jnp.zeros((C,), jnp.float32), 'Wk': nrm(ks[4], (C, C), 0.02), 'bk': jnp.zeros((C,), jnp.float32), 'Wv': nrm(ks[5], (C, C), 0.02), 'bv': jnp.zeros((C,), jnp.float32), 'Wlepe': nrm(ks[6], (5, 5, 1, C), 0.05), 'blepe': jnp.zeros((C,), jnp.float32), 'Wo': nrm(ks[7], (C, C), 0.02), 'bo': jnp.zeros((C,), jnp.float32)}
    _L0_conv_all = _L0_conv_setup()
    _L0_conv_in = {k: v for k, v in _L0_conv_all.items() if k in ('mask_h', 'mask_w', 'Wq', 'bq', 'Wk', 'bk', 'Wv', 'bv', 'Wlepe', 'blepe', 'Wo', 'bo', )}
    del _L0_conv_all

    def _L0_ffn_setup():
        import math
        import jax, jax.numpy as jnp
        import numpy as np
        CAPACITY_FACTOR = 1.25
        key = jax.random.key(seed)
        ks = jax.random.split(key, 5)
        B, L, D, F, E = (8, 8192, 256, 1024, 8)
        h = jax.random.normal(ks[0], (B, L, D), dtype=jnp.float32)
        gate_w = jax.random.normal(ks[1], (D, E), dtype=jnp.float32) * 0.02
        gate_b = jnp.zeros((E,), dtype=jnp.float32)
        w1 = jax.random.normal(ks[2], (E, D, F), dtype=jnp.float32) * (1.0 / math.sqrt(D))
        b1 = jnp.zeros((E, F), dtype=jnp.float32)
        w2 = jax.random.normal(ks[3], (E, F, D), dtype=jnp.float32) * (1.0 / math.sqrt(F))
        b2 = jnp.zeros((E, D), dtype=jnp.float32)
        return {'h': h, 'gate_w': gate_w, 'gate_b': gate_b, 'w1': w1, 'b1': b1, 'w2': w2, 'b2': b2}
    _L0_ffn_all = _L0_ffn_setup()
    _L0_ffn_in = {k: v for k, v in _L0_ffn_all.items() if k in ('gate_w', 'gate_b', 'w1', 'b1', 'w2', 'b2', )}
    del _L0_ffn_all

    return {
        "x": x,
        "L0_conv_mask_h": _L0_conv_in["mask_h"],
        "L0_conv_mask_w": _L0_conv_in["mask_w"],
        "L0_conv_Wq": _L0_conv_in["Wq"],
        "L0_conv_bq": _L0_conv_in["bq"],
        "L0_conv_Wk": _L0_conv_in["Wk"],
        "L0_conv_bk": _L0_conv_in["bk"],
        "L0_conv_Wv": _L0_conv_in["Wv"],
        "L0_conv_bv": _L0_conv_in["bv"],
        "L0_conv_Wlepe": _L0_conv_in["Wlepe"],
        "L0_conv_blepe": _L0_conv_in["blepe"],
        "L0_conv_Wo": _L0_conv_in["Wo"],
        "L0_conv_bo": _L0_conv_in["bo"],
        "L0_ffn_gate_w": _L0_ffn_in["gate_w"],
        "L0_ffn_gate_b": _L0_ffn_in["gate_b"],
        "L0_ffn_w1": _L0_ffn_in["w1"],
        "L0_ffn_b1": _L0_ffn_in["b1"],
        "L0_ffn_w2": _L0_ffn_in["w2"],
        "L0_ffn_b2": _L0_ffn_in["b2"],
    }

def reference(x, L0_conv_mask_h, L0_conv_mask_w, L0_conv_Wq, L0_conv_bq, L0_conv_Wk, L0_conv_bk, L0_conv_Wv, L0_conv_bv, L0_conv_Wlepe, L0_conv_blepe, L0_conv_Wo, L0_conv_bo, L0_ffn_gate_w, L0_ffn_gate_b, L0_ffn_w1, L0_ffn_b1, L0_ffn_w2, L0_ffn_b2):
    import jax
    import jax.numpy as jnp
    def _L0_conv_ref(x, mask_h, mask_w, Wq, bq, Wk, bk, Wv, bv, Wlepe, blepe, Wo, bo):
        import jax, jax.numpy as jnp
        import numpy as np
        from jax import lax
        NUM_HEADS = 8
        KEY_DIM = 32
        B, H, W, C = x.shape
        scaling = KEY_DIM ** (-0.5)
        q = x @ Wq.T + bq
        k = (x @ Wk.T + bk) * scaling
        v = x @ Wv.T + bv
        lepe = lax.conv_general_dilated(v, Wlepe, window_strides=(1, 1), padding=((2, 2), (2, 2)), dimension_numbers=('NHWC', 'HWIO', 'NHWC'), feature_group_count=C) + blepe
        qr = q.reshape(B, H, W, NUM_HEADS, KEY_DIM)
        kr = k.reshape(B, H, W, NUM_HEADS, KEY_DIM)
        vr = v.reshape(B, H, W, NUM_HEADS, -1)
        attn_w = jax.nn.softmax(jnp.einsum('bhqnd,bhknd->bhnqk', qr, kr) + mask_w[None, None], axis=-1)
        v1 = jnp.einsum('bhnqk,bhknd->bhqnd', attn_w, vr)
        attn_h = jax.nn.softmax(jnp.einsum('bqwnd,bkwnd->bwnqk', qr, kr) + mask_h[None, None], axis=-1)
        out = jnp.einsum('bwnqk,bkwnd->bqwnd', attn_h, v1)
        out = out.reshape(B, H, W, C) + lepe
        return out @ Wo.T + bo

    def _L0_ffn_ref(h, gate_w, gate_b, w1, b1, w2, b2):
        import math
        import jax, jax.numpy as jnp
        import numpy as np
        CAPACITY_FACTOR = 1.25
        B, L, D = h.shape
        E = gate_w.shape[1]
        T = B * L
        C = max(1, math.ceil(CAPACITY_FACTOR * T / E))
        x = h.reshape(T, D)
        logits = x @ gate_w + gate_b
        probs = jax.nn.softmax(logits, axis=-1)
        idx = jnp.argmax(probs, axis=-1)
        prb = jnp.take_along_axis(probs, idx[:, None], axis=1)[:, 0]
        one_hot = jax.nn.one_hot(idx, E, dtype=jnp.float32)
        pos = (jnp.cumsum(one_hot, axis=0) * one_hot).sum(-1).astype(jnp.int32) - 1
        kept = pos < C
        pos_safe = jnp.where(kept, pos, C)
        buf = jnp.zeros((E, C, D), dtype=h.dtype).at[idx, pos_safe].set(x, mode='drop')
        hmid = jax.nn.relu(jnp.einsum('ecd,edf->ecf', buf, w1) + b1[:, None, :])
        ybuf = jnp.einsum('ecf,efd->ecd', hmid, w2) + b2[:, None, :]
        pos_g = jnp.minimum(pos, C - 1)
        y_tok = ybuf[idx, pos_g] * (prb * kept)[:, None]
        y = y_tok.reshape(B, L, D)
        y = jnp.nan_to_num(y, nan=0.0, posinf=10000.0, neginf=-10000.0)
        return y

    def _gn(v, G=32, eps=1e-5):
        B_, H_, W_, C_ = v.shape
        g = v.reshape(B_, H_, W_, G, C_ // G)
        m = jnp.mean(g, axis=(1, 2, 4), keepdims=True)
        s = jnp.var(g, axis=(1, 2, 4), keepdims=True)
        return ((g - m) / jnp.sqrt(s + eps)).reshape(v.shape)

    def _ln_c(v, eps=1e-6):
        m = jnp.mean(v, axis=-1, keepdims=True)
        s = jnp.var(v, axis=-1, keepdims=True)
        return (v - m) / jnp.sqrt(s + eps)

    def _ln_t(v, eps=1e-5):
        m = jnp.mean(v, axis=-1, keepdims=True)
        s = jnp.var(v, axis=-1, keepdims=True)
        return (v - m) / jnp.sqrt(s + eps)

    def _to_tokens(v):
        B_, H_, W_, C_ = v.shape
        return v.reshape(B_, H_ * W_, C_)
    def _from_tokens(t, like):
        return t.reshape(like.shape)

    x = x + _L0_conv_ref(_ln_c(x), L0_conv_mask_h, L0_conv_mask_w, L0_conv_Wq, L0_conv_bq, L0_conv_Wk, L0_conv_bk, L0_conv_Wv, L0_conv_bv, L0_conv_Wlepe, L0_conv_blepe, L0_conv_Wo, L0_conv_bo)
    t = _to_tokens(x)
    t = t + _L0_ffn_ref(_ln_t(t), L0_ffn_gate_w, L0_ffn_gate_b, L0_ffn_w1, L0_ffn_b1, L0_ffn_w2, L0_ffn_b2)
    x = _from_tokens(t, x)
    return x


_drawn_inputs = setup_inputs


def setup_inputs(seed=0):
    import zlib

    import numpy as np

    out = dict(_drawn_inputs(seed))
    spreads = {'L0_conv_bq': (0.0, 0.8),
     'L0_conv_bk': (0.0, 0.8),
     'L0_conv_bv': (0.0, 0.1),
     'L0_conv_blepe': (0.0, 0.1),
     'L0_conv_bo': (0.0, 0.1),
     'L0_ffn_gate_b': (0.0, 0.1),
     'L0_ffn_b1': (0.0, 0.616),
     'L0_ffn_b2': (0.0, 0.436)}
    factors = {'L0_conv_mask_h': 7.454, 'L0_conv_mask_w': 7.416, 'L0_conv_Wq': 8.0, 'L0_conv_Wk': 8.0}
    for name, (base, spread) in spreads.items():
        noise = np.random.default_rng([zlib.crc32(name.encode()), seed]).standard_normal(out[name].shape)
        drawn = base * np.exp(spread * noise) if base else spread * noise
        out[name] = jnp.asarray(drawn.astype(out[name].dtype))
    for name, factor in factors.items():
        out[name] = (out[name] * factor).astype(out[name].dtype)
    return out
```

```python
import math
from contextlib import ExitStack

import numpy as np
import concourse.bass as bass
from concourse import mybir
from concourse.alu_op_type import AluOpType as ALU

F32 = mybir.dt.float32
I32 = mybir.dt.int32
U32 = mybir.dt.uint32
ACT = mybir.ActivationFunctionType
AX_X = mybir.AxisListType.X

P = 128
HEADS = 8
KEY_DIM = 32
VCOLS = KEY_DIM + 1
LINES = 4
PAD = 2
TAPS = 25
CREDIT = 2
CHUNK = 512
FLT_MAX = 3.4028234663852886e38
NO_TOKEN = 1 << 20


class Step:

    def __init__(self, half, par, inside):
        self.half, self.par, self.inside = half, par, inside

    def plus(self, off):
        total = self.par + off
        return Step(self.half + total // 2, total % 2, self.inside)

    @property
    def index(self):
        return self.half * 2 + self.par

    def valid(self, count):
        return self.inside or 0 <= self.index < count


def run_steps(eng, first, last, lo, hi, emit, before_loop):
    for s in range(first, lo):
        emit(Step(s // 2, s % 2, False))
    before_loop(eng)
    with eng.Fori(lo // 2, hi // 2) as half:
        for par in range(2):
            emit(Step(half, par, True))
    for s in range(hi, last + 1):
        emit(Step(s // 2, s % 2, False))


def done(n):
    return n + (1 + CREDIT)


def freed(n, buffers):
    return n + (1 + CREDIT - buffers)


def metaformer_kernel(nc, x, mask_h, mask_w, wqT, bq, wkT, bk, wvT, bv, wlepe, blepe, woT, bo,
                      gate_w, gate_b, w1, b1, w2, b2, out):
    IMGS, H, W, C = x.shape
    E, _, F = w1.shape
    TOK = IMGS * H * W
    IMG_TOK = H * W
    KC = C // P
    DC = P // HEADS
    STEPS = H // LINES
    ST = LINES * W
    TT = ST // P
    CAP = math.ceil(1.25 * TOK / E)
    CHUNKS = CAP // CHUNK
    SLOTS = E * CAP
    FB = F // P
    CT = CHUNK // P
    PW = W + 2 * PAD
    VROW = HEADS * VCOLS
    RT = IMG_TOK // P
    SCALING = float(KEY_DIM) ** -0.5
    assert H == W == 64 and C == 256 and CAP % (2 * CHUNK) == 0 and E % 2 == 0
    LO, HI = 2, 12

    x_t = x.rearrange("b h w c -> (b h w) c")
    out_t = out.rearrange("b h w c -> (b h w) c")
    v1_t = nc.dram_tensor("v1_rows", [TOK, VROW], F32).ap()
    x2_t = nc.dram_tensor("x2_rows", [TOK, C], F32).ap()
    lg_t = nc.dram_tensor("gate_logits", [TOK, E], F32).ap()
    slot_t = nc.dram_tensor("slot_table", [SLOTS + CHUNK, 2], I32).ap()

    with ExitStack() as ctx:
        def sb(name, shape, dt=F32):
            return ctx.enter_context(nc.sbuf_tensor(name, shape, dt))

        def sem(name):
            return ctx.enter_context(nc.semaphore(name))

        q_img = sb("q_img", [P, KC, IMG_TOK])
        k_img = sb("k_img", [P, KC, IMG_TOK])
        v_pad = sb("v_pad", [P, KC, H + 2 * PAD, PW])
        lepe = sb("lepe", [P, KC, H, W])
        q_st = sb("q_st", [P, 2, KC, ST])
        k_st = sb("k_st", [P, 2, KC, ST])
        v_st = sb("v_st", [P, 2, TT, VCOLS, HEADS])
        sc_sb = sb("sc_sb", [P, 4 * LINES, 64])
        ex_sb = sb("ex_sb", [P, 4 * LINES, 64])
        exT_sb = sb("exT_sb", [P, 8, P])
        mx_sb = sb("mx_sb", [P, 16])
        rec_sb = sb("rec_sb", [P, 16])
        v1_st = sb("v1_st", [P, 2, TT, VCOLS, HEADS])
        x_in = sb("x_in", [P, 2, TT, C])
        xn = sb("xn", [P, 2, TT, C])
        xnT = sb("xnT", [P, KC, ST])
        oT_sb = sb("oT_sb", [P, KC, ST])
        o2 = sb("o2", [P, 2, TT, C])
        x_r, hn = x_in, xn
        x2_st = sb("x2_st", [P, 2, TT, C])
        hT_sb = sb("hT_sb", [P, KC, ST])
        lg_st = sb("lg_st", [P, 2, TT, E])
        masks = sb("masks", [P, 2, 4, 64])
        wq_sb, wk_sb, wv_sb, wo_sb = (sb(n, [P, KC, C]) for n in ("wq_sb", "wk_sb", "wv_sb", "wo_sb"))
        gw_sb = sb("gw_sb", [P, KC, E])
        gb_sb = sb("gb_sb", [P, E])
        bq_sb = sb("bq_sb", [P, KC])
        bk_sb = sb("bk_sb", [P, KC])
        bv_sb = sb("bv_sb", [P, C])
        bo_sb = sb("bo_sb", [P, C])
        wl_sb = sb("wl_sb", [P, KC, TAPS])
        bl_sb = sb("bl_sb", [P, KC])
        ident = sb("ident", [P, P])
        upper = sb("upper", [P, P])
        ones = sb("ones", [P, P])
        stat = sb("stat", [P, 2, 4, 6])
        mv = sb("mv", [P, 2, 4, 2])
        veps = sb("veps", [P, 2, 4])
        rstd = sb("rstd", [P, 2, 4])
        half = sb("half", [P, 4])
        q_flat = q_img[:, :, :].rearrange("p c t -> p (c t)")
        k_flat = k_img[:, :, :].rearrange("p c t -> p (c t)")
        W1N, W2N = KC * F, FB * C
        w1_sb = [(q_flat, k_flat)[h][:, 0:W1N].rearrange("p (c f) -> p c f", c=KC) for h in range(2)]
        w2_sb = [(q_flat, k_flat)[h][:, W1N:W1N + W2N].rearrange("p (c f) -> p c f", c=FB) for h in range(2)]
        b1_sb = [(q_flat, k_flat)[h][:, W1N + W2N:W1N + W2N + FB] for h in range(2)]
        b2_sb = [(q_flat, k_flat)[h][:, W1N + W2N + FB:W1N + W2N + FB + C] for h in range(2)]
        l_flat = lepe[:, :, :, :].rearrange("p c h w -> p (c h w)")
        hm_sb = l_flat[:, 0:FB * CHUNK].rearrange("p (f t) -> p f t", f=FB)
        fT_sb = l_flat[:, FB * CHUNK:FB * CHUNK + KC * CHUNK].rearrange("p (c t) -> p c t", c=KC)
        v_flat = v_pad[:, :, :, :].rearrange("p c h w -> p (c h w)")
        CN = CT * C
        xg = [v_flat[:, n * CN:(n + 1) * CN].rearrange("p (i c) -> p i c", i=CT) for n in range(2)]
        fn = v_flat[:, 2 * CN:3 * CN].rearrange("p (i c) -> p i c", i=CT)
        y_sb = v_flat[:, 3 * CN:4 * CN].rearrange("p (i c) -> p i c", i=CT)
        r_sb = v_flat[:, 4 * CN:5 * CN].rearrange("p (i c) -> p i c", i=CT)
        m_sb = v_flat[:, 5 * CN:6 * CN].rearrange("p (i c) -> p i c", i=CT)
        yo = [v_flat[:, (6 + n) * CN:(7 + n) * CN].rearrange("p (i c) -> p i c", i=CT) for n in range(2)]
        tok_g = sb("tok_g", [P, 2, CT, 2], I32)
        rl = sb("rl", [P, RT, E])
        rp = sb("rp", [P, RT, E])
        r_eq = sb("r_eq", [P, RT, E])
        r_cum = sb("r_cum", [P, RT, E])
        r_oh = sb("r_oh", [P, E, RT])
        r_pos = sb("r_pos", [P, E, RT])
        r_big = sb("r_big", [P, E, RT])
        r_mx = sb("r_mx", [P, RT])
        r_sum = sb("r_sum", [P, RT])
        r_slot = sb("r_slot", [P, RT])
        r_slot_i = sb("r_slot_i", [P, RT], I32)
        r_tok = sb("r_tok", [P, RT])
        r_pair = sb("r_pair", [P, RT, 2], I32)
        r_reset = sb("r_reset", [P, E, RT])
        r_run = sb("r_run", [P, E])
        r_tot = sb("r_tot", [P, E])
        r_base = sb("r_base", [P, E])
        r_first = sb("r_first", [P, E])

        ps_s = ctx.enter_context(nc.psum_tensor("ps_s", [P, 2, 512], F32))
        ps_t = ctx.enter_context(nc.psum_tensor("ps_t", [P, 1024], F32))
        ps_p = [ctx.enter_context(nc.psum_tensor(f"ps_p{n}", [P, 512], F32)) for n in range(4)]
        ps_o = ps_t[:, :].rearrange("p (t n) -> p t n", t=TT)[:, :, 0:VROW].rearrange(
            "p t (n d) -> p t n d", n=HEADS)

        consts = sem("consts_loaded")
        made = sem("constants_made")
        x_load = [sem(f"x_load{n}") for n in range(2)]
        qk_stored = [sem(f"qk_stored{n}") for n in range(2)]
        v1_stored = [sem(f"v1_stored{n}") for n in range(2)]
        v_load = [sem(f"v_load{n}") for n in range(2)]
        xr_load = [sem(f"xr_load{n}") for n in range(2)]
        x2_stored = [sem(f"x2_stored{n}") for n in range(2)]
        lg_stored = [sem(f"lg_stored{n}") for n in range(2)]
        stat1, eps1, rstd1, xn_ready = sem("stat1"), sem("eps1"), sem("rstd1"), sem("xn_ready")
        st_c = sem("stats_chain")
        xT_ready, xnT_sb_ready = sem("xT_ready"), sem("xnT_sb_ready")
        q_ready, k_ready, v_ready = sem("q_ready"), sem("k_ready"), sem("v_ready")
        q_sb, k_sb, v_sb = sem("q_sb"), sem("k_sb"), sem("v_sb")
        vT_ready, vT_sb = sem("vT_ready"), sem("vT_sb")
        tap0, tap1 = sem("taps_chunk0"), sem("taps_chunk1")
        s_ready, sm_done, mx_done, sub_done = sem("s_ready"), sem("sm_done"), sem("mx_done"), sem("sub_done")
        e_ready, eT_ready, eT_sb = sem("e_ready"), sem("eT_ready"), sem("eT_sb")
        o_ready, rec_done, o_sb = sem("o_ready"), sem("rec_done"), sem("o_sb")
        staged, xb_ready = sem("staged"), sem("xb_ready")
        oT_ready, oT_done, y_ready, x2_ready = sem("oT_ready"), sem("oT_done"), sem("y_ready"), sem("x2_ready")
        stat2, eps2, rstd2, hn_ready = sem("stat2"), sem("eps2"), sem("rstd2"), sem("hn_ready")
        st_c2 = sem("stats_chain2")
        hT_ready, hT_done, g_ready, lg_ready = sem("hT_ready"), sem("hT_done"), sem("g_ready"), sem("lg_ready")
        passed = sem("passed")
        table_cleared = sem("table_cleared")
        r_free = sem("r_free")
        rl_load, r_chain, r_exp, r_pe, r_ready, r_scattered = (
            sem(n) for n in ("rl_load", "r_chain", "r_exp", "r_pe", "r_ready", "r_scattered"))
        w_load = [sem(f"w_load{n}") for n in range(2)]
        tok_load = [sem(f"tok_load{n}") for n in range(2)]
        gathered = [sem(f"gathered{n}") for n in range(2)]
        scattered = [sem(f"scattered{n}") for n in range(2)]
        f_stat, f_aggr, f_eps, f_rstd, fn_ready = (sem(n) for n in ("f_stat", "f_aggr", "f_eps", "f_rstd", "fn_ready"))
        fT_ready, fT_done, h_ready, relu_done, f_ready, y_taken, y_chain, yo_ready = (
            sem(n) for n in ("fT_ready", "fT_done", "h_ready", "relu_done", "f_ready", "y_taken", "y_chain", "yo_ready"))

        CONST_DMAS = 5 + 3 + 3 + 1 + 8

        R_TOTALS = 7 + (E - 1) + 3
        R_CHAIN = R_TOTALS + 12
        CLEAR_DMAS = math.ceil((SLOTS + CHUNK) / P / RT)

        block = ctx.enter_context(nc.Block())

        def settle(eng):
            eng.sem_inc(passed, 1)

        def st_of(b, s):
            return b * STEPS + s.index

        def half_of(b, s):
            return b * (STEPS // 2) + s.half

        def tokens_rows(dram, b, s):
            return dram[bass.ds(b * IMG_TOK + s.index * ST, ST), :].rearrange("(t p) c -> p t c", p=P)

        def tokens_cols(dram, b, s, s2):
            img = dram[bass.ds(b * IMG_TOK, IMG_TOK), :].rearrange("(h w) c -> h w c", w=W)
            cols = img[:, bass.ds(s.index * LINES, LINES), :].rearrange("h (t s2) c -> h t s2 c", s2=2)
            return cols[:, :, s2, :]

        @block.sync
        def _(sp):
            for dst, src in ((wq_sb, wqT), (wk_sb, wkT), (wv_sb, wvT), (wo_sb, woT), (gw_sb, gate_w)):
                sp.dma_start(dst[:, :, :], src.rearrange("(c p) n -> p c n", p=P)).then_inc(consts, 16)
            for dst, src in ((bq_sb, bq), (bk_sb, bk), (bl_sb, blepe)):
                sp.dma_start(dst[:, :], src.rearrange("(c p) -> p c", p=P),
                             allow_slow_non_contiguous=True).then_inc(consts, 16)
            for dst, src in ((bv_sb, bv), (bo_sb, bo), (gb_sb, gate_b)):
                sp.dma_start(dst[:, :], src.partition_broadcast(P)).then_inc(consts, 16)
            sp.dma_start(wl_sb[:, :, :], wlepe.rearrange("(c p) k -> p c k", p=P)).then_inc(consts, 16)
            for m, mask in enumerate((mask_w, mask_h)):
                by_head = mask.rearrange("(c i e) q k -> e i q c k", i=2, e=2)
                for e in range(2):
                    for i in range(2):
                        sp.dma_start(masks[64 * e:64 * e + 64, m, 2 * i:2 * i + 2, :],
                                     by_head[e, i]).then_inc(consts, 16)
            for n in range(2):
                sp.sem_inc(v1_stored[n], 16)
                sp.sem_inc(qk_stored[n], 32)
                sp.sem_inc(x2_stored[n], 64)
                sp.sem_inc(lg_stored[n], 32)

            with sp.Fori(0, IMGS) as b:
                def phase1(s):
                    q = s.plus(3)
                    if q.valid(STEPS):
                        sp.wait_ge(xn_ready, freed(st_of(b, q), 2))
                        sp.dma_start(x_in[:, q.par], tokens_rows(x_t, b, q)).then_inc(x_load[q.par], 16)
                    q = s.plus(1)
                    if q.valid(STEPS):
                        if not q.inside and q.index == 0:
                            sp.wait_ge(staged, b * (2 * STEPS) + CREDIT)
                        cols = bass.ds(q.index * ST, ST)
                        sp.wait_ge(q_sb, done(st_of(b, q)))
                        sp.dma_start(q_img[:, :, cols], q_st[:, q.par]).then_inc(qk_stored[q.par], 16)
                        sp.wait_ge(k_sb, done(st_of(b, q)))
                        settle(sp)
                        sp.dma_start(k_img[:, :, cols], k_st[:, q.par]).then_inc(qk_stored[q.par], 16)
                    if s.valid(STEPS):
                        sp.wait_ge(o_sb, done(b * (2 * STEPS) + s.index))
                        sp.dma_start(tokens_rows(v1_t, b, s),
                                     v1_st[:, s.par].rearrange("p t d n -> p t (d n)")).then_inc(v1_stored[s.par], 16)

                run_steps(sp, -3, STEPS - 1, LO, HI, phase1, settle)
                for n in range(2):
                    sp.wait_ge(v1_stored[n], b * (8 * STEPS) + (8 * STEPS + 16))
                    settle(sp)

                def phase2(s):
                    q = s.plus(1)
                    if q.valid(STEPS):
                        sp.wait_ge(o_ready, freed(b * (2 * STEPS) + (q.index + STEPS), 2))
                        for s2 in range(2):
                            sp.dma_start(v_st[64 * s2:64 * s2 + 64, q.par].rearrange("p t d n -> p t (d n)"),
                                         tokens_cols(v1_t, b, q, s2)).then_inc(v_load[q.par], 16)
                    if s.valid(STEPS):
                        sp.wait_ge(x2_ready, freed(st_of(b, s), 2))
                        for s2 in range(2):
                            sp.dma_start(x_r[64 * s2:64 * s2 + 64, s.par], tokens_cols(x_t, b, s, s2)
                                         ).then_inc(xr_load[s.par], 16)
                    q = s.plus(-1)
                    if q.valid(STEPS):
                        sp.wait_ge(x2_ready, done(st_of(b, q)))
                        for s2 in range(2):
                            for dram in (x2_t, out_t):
                                sp.dma_start(tokens_cols(dram, b, q, s2), x2_st[64 * s2:64 * s2 + 64, q.par]
                                             ).then_inc(x2_stored[q.par], 16)
                    q = s.plus(-2)
                    if q.valid(STEPS):
                        sp.wait_ge(lg_ready, done(st_of(b, q)))
                        for s2 in range(2):
                            sp.dma_start(tokens_cols(lg_t, b, q, s2), lg_st[64 * s2:64 * s2 + 64, q.par]
                                         ).then_inc(lg_stored[q.par], 16)

                run_steps(sp, -1, STEPS + 1, LO, HI, phase2, settle)
                for n in range(2):
                    sp.wait_ge(lg_stored[n], b * (16 * STEPS) + (16 * STEPS + 32))
                    settle(sp)
                sp.dma_start(rl[:, :, :], lg_t[bass.ds(b * IMG_TOK, IMG_TOK), :].rearrange(
                    "(p t) e -> p t e", t=RT)).then_inc(rl_load, 16)

            w1_rows = w1.rearrange("e d f -> (e d) f")
            w2_rows = w2.rearrange("e f d -> (e f) d")

            def weights(e, par):
                for dst, src in ((w1_sb[par], w1_rows[bass.ds(e * C, C), :]),
                                 (w2_sb[par], w2_rows[bass.ds(e * F, F), :])):
                    sp.dma_start(dst, src.rearrange("(c p) n -> p c n", p=P)).then_inc(w_load[par], 16)
                sp.dma_start(b1_sb[par], b1[:, bass.ds(e * FB, FB)]).then_inc(w_load[par], 16)
                sp.dma_start(b2_sb[par], b2[bass.ds(e, 1), :].rearrange("a c -> (a c)").partition_broadcast(P)
                             ).then_inc(w_load[par], 16)

            sp.wait_ge(staged, 2 * IMGS * STEPS + CREDIT)
            settle(sp)
            weights(0, 0)
            weights(1, 1)
            with sp.Fori(1, E // 2) as pair:
                for par in range(2):
                    sp.wait_ge(y_taken, pair * (2 * CHUNKS) + ((par - 1) * CHUNKS + CREDIT))
                    settle(sp)
                    weights(pair * 2 + par, par)
            for n in range(2):
                sp.wait_ge(x2_stored[n], 32 * IMGS * STEPS + 64)
                sp.wait_ge(scattered[n], 16 * CT * (E * CHUNKS // 2))

        @block.tensor
        def _(pe):
            for s_ in (xT_ready, q_ready, k_ready, v_ready, vT_ready, s_ready, eT_ready, o_ready,
                       oT_ready, y_ready, hT_ready, g_ready, fT_ready, f_ready):
                pe.sem_inc(s_, CREDIT)
            pe.sem_inc(h_ready, CREDIT)
            pe.wait_ge(consts, 16 * CONST_DMAS)
            pe.wait_ge(made, 5)

            def scores(g, par):
                pe.wait_ge(sm_done, freed(g, 1))
                for c in range(KC):
                    for r in range(LINES):
                        for a in range(4):
                            i, e = a // 2, a % 2
                            rows = slice(32 * a, 32 * a + 32)
                            line = slice(64 * r, 64 * r + 64)
                            col = 256 * c + 64 * r
                            last = nc.tensor.matmul(ps_s[64 * e:64 * e + 64, i, col:col + 64],
                                                    q_st[rows, par, c, line], k_st[rows, par, c, line],
                                                    start=True, stop=True)
                last.then_inc(s_ready, 1)

            def weights_T(g):
                pe.wait_ge(e_ready, done(g))
                pe.wait_ge(o_sb, freed(g, 1))
                for k in range(8):
                    ic, rp_ = k // 2, k % 2
                    src = ex_sb[:, LINES * ic + 2 * rp_:LINES * ic + 2 * rp_ + 2, :].rearrange("p r k -> p (r k)")
                    last = nc.tensor.transpose(ps_t[:, P * k:P * k + P], src, ident[:, :])
                last.then_inc(eT_ready, 1)

            def values(g, par):
                pe.wait_ge(eT_sb, done(g))
                settle(pe)
                for t in range(TT):
                    for c in range(KC):
                        for i in range(2):
                            for e in range(2):
                                for r in range(2):
                                    n = 4 * c + 2 * i + e
                                    rows = slice(64 * r, 64 * r + 64)
                                    last = nc.tensor.matmul(
                                        ps_o[rows, t, n, :], exT_sb[rows, 2 * (2 * i + c) + t, 64 * e:64 * e + 64],
                                        v_st[rows, par, t, :, n], start=True, stop=True)
                last.then_inc(o_ready, 1)

            with pe.Fori(0, IMGS) as b:
                def phase1(s):
                    g = b * (2 * STEPS) + s.index
                    q = s.plus(1)
                    n = st_of(b, q)
                    if s.valid(STEPS):
                        pe.wait_ge(q_sb, done(st_of(b, s)))
                        pe.wait_ge(k_sb, done(st_of(b, s)))
                        scores(g, s.par)
                    if q.valid(STEPS):
                        pe.wait_ge(xn_ready, done(n))
                        pe.wait_ge(vT_sb, freed(n, 1))
                        for c in range(KC):
                            for t in range(TT):
                                last = nc.tensor.transpose(ps_p[0][:, ST * c + P * t:ST * c + P * t + P],
                                                           xn[:, q.par, t, P * c:P * c + P], ident[:, :])
                        last.then_inc(xT_ready, 1)
                        pe.wait_ge(xnT_sb_ready, done(n))
                        for bank, wt, taken, ready in ((1, wq_sb, q_sb, q_ready), (2, wk_sb, k_sb, k_ready)):
                            pe.wait_ge(taken, freed(n, 1))
                            for m in range(KC):
                                for c in range(KC):
                                    last = nc.tensor.matmul(ps_p[bank][:, ST * m:ST * m + ST],
                                                            wt[:, c, P * m:P * m + P], xnT[:, c, :],
                                                            start=(c == 0), stop=(c == KC - 1))
                            last.then_inc(ready, 1)
                        pe.wait_ge(v_sb, freed(n, 1))
                        for t in range(TT):
                            for c in range(KC):
                                last = nc.tensor.matmul(ps_p[3][:, C * t:C * t + C], xnT[:, c, P * t:P * t + P],
                                                        wv_sb[:, c, :], start=(c == 0), stop=(c == KC - 1))
                        last.then_inc(v_ready, 1)
                    if s.valid(STEPS):
                        weights_T(g)
                    if q.valid(STEPS):
                        pe.wait_ge(v_sb, done(n))
                        for c in range(KC):
                            for t in range(TT):
                                last = nc.tensor.transpose(ps_p[0][:, ST * c + P * t:ST * c + P * t + P],
                                                           v_st[:, q.par, t, DC * c:DC * c + DC, :].rearrange("p d n -> p (d n)"),
                                                           ident[:, :])
                        last.then_inc(vT_ready, 1)
                    if s.valid(STEPS):
                        values(g, s.par)

                run_steps(pe, -1, STEPS - 1, LO, HI, phase1, settle)
                pe.wait_ge(vT_sb, done(b * STEPS + (STEPS - 1)))

                def phase2(s):
                    g = b * (2 * STEPS) + (s.index + STEPS)
                    if s.valid(STEPS):
                        pe.wait_ge(staged, st_of(b, s) * 2 + (2 + CREDIT))
                        scores(g, s.par)
                    q = s.plus(-1)
                    if q.valid(STEPS):
                        pe.wait_ge(o_sb, done(g - 1))
                        pe.wait_ge(oT_done, freed(st_of(b, q), 1))
                        for c in range(KC):
                            for t in range(TT):
                                last = nc.tensor.transpose(ps_p[0][:, ST * c + P * t:ST * c + P * t + P],
                                                           o2[:, q.par, t, P * c:P * c + P], ident[:, :])
                        last.then_inc(oT_ready, 1)
                    if s.valid(STEPS):
                        weights_T(g)
                    if q.valid(STEPS):
                        pe.wait_ge(oT_done, done(st_of(b, q)))
                        pe.wait_ge(x2_ready, freed(st_of(b, q), 1))
                        for t in range(TT):
                            for c in range(KC):
                                last = nc.tensor.matmul(ps_p[1][:, C * t:C * t + C], oT_sb[:, c, P * t:P * t + P],
                                                        wo_sb[:, c, :], start=(c == 0), stop=(c == KC - 1))
                        last.then_inc(y_ready, 1)
                    q = s.plus(-2)
                    if q.valid(STEPS):
                        pe.wait_ge(hn_ready, done(st_of(b, q)))
                        pe.wait_ge(hT_done, freed(st_of(b, q), 1))
                        for c in range(KC):
                            for t in range(TT):
                                last = nc.tensor.transpose(ps_p[2][:, ST * c + P * t:ST * c + P * t + P],
                                                           hn[:, q.par, t, P * c:P * c + P], ident[:, :])
                        last.then_inc(hT_ready, 1)
                    if s.valid(STEPS):
                        pe.wait_ge(v_load[s.par], half_of(b, s) * 32 + 32)
                        values(g, s.par)
                    if q.valid(STEPS):
                        pe.wait_ge(hT_done, done(st_of(b, q)))
                        pe.wait_ge(lg_ready, freed(st_of(b, q), 1))
                        for t in range(TT):
                            for c in range(KC):
                                last = nc.tensor.matmul(ps_p[3][:, E * t:E * t + E], hT_sb[:, c, P * t:P * t + P],
                                                        gw_sb[:, c, :], start=(c == 0), stop=(c == KC - 1))
                        last.then_inc(g_ready, 1)

                run_steps(pe, 0, STEPS + 1, LO, HI, phase2, settle)
                pe.wait_ge(lg_ready, done(b * STEPS + (STEPS - 1)))

                pe.wait_ge(r_chain, b * R_CHAIN + R_TOTALS)
                nc.tensor.matmul(ps_p[0][:, 0:E], upper[:, :], r_tot[:, :], start=True, stop=True)
                nc.tensor.matmul(ps_p[1][:, 0:E], ones[:, :], r_tot[:, :], start=True, stop=True).then_inc(r_pe, 1)
                pe.wait_ge(r_chain, (b + 1) * R_CHAIN)

            def transposes(n):
                pe.wait_ge(fn_ready, done(n))
                pe.wait_ge(fT_done, freed(n, 1))
                for c in range(KC):
                    for i in range(CT):
                        last = nc.tensor.transpose(ps_p[c][:, P * i:P * i + P], fn[:, i, P * c:P * c + P],
                                                   ident[:, :])
                last.then_inc(fT_ready, 1)

            transposes(0)
            with pe.Fori(0, E // 2) as pair:
                for par in range(2):
                    pe.wait_ge(w_load[par], pair * 64 + 64)
                    settle(pe)
                    with pe.Fori(0, CHUNKS) as j:
                        n = pair * (2 * CHUNKS) + (j + par * CHUNKS)
                        pe.wait_ge(fT_done, done(n))
                        for f in range(FB):
                            pe.wait_ge(relu_done, n * FB + (f + 1))
                            for c in range(KC):
                                last = nc.tensor.matmul(ps_s[:, f % 2, :], w1_sb[par][:, c, P * f:P * f + P],
                                                        fT_sb[:, c, :], start=(c == 0), stop=(c == KC - 1))
                            last.then_inc(h_ready, 1)
                        transposes(n + 1)
                        pe.wait_ge(y_taken, freed(n, 1))
                        for i in range(CT):
                            for f in range(FB):
                                if i == 0:
                                    pe.wait_ge(relu_done, n * FB + (f + 1 + CREDIT))
                                last = nc.tensor.matmul(ps_t[:, C * i:C * i + C], hm_sb[:, f, P * i:P * i + P],
                                                        w2_sb[par][:, f, :], start=(f == 0), stop=(f == FB - 1))
                        last.then_inc(f_ready, 1)

        @block.scalar
        def _(act):
            for s_ in (xnT_sb_ready, q_sb, vT_sb, e_ready, eT_sb, hT_done, fT_done, relu_done):
                act.sem_inc(s_, CREDIT)
            act.wait_ge(consts, 16 * CONST_DMAS)
            act.wait_ge(made, 5)

            def exps(g):
                act.wait_ge(sub_done, done(g))
                act.wait_ge(eT_ready, freed(g, 1))
                nc.scalar.activation(ex_sb[:, :, :], sc_sb[:, :, :], ACT.Exp).then_inc(e_ready, 1)

            def take_weights_T(g):
                act.wait_ge(eT_ready, done(g))
                act.wait_ge(o_ready, freed(g, 1))
                nc.scalar.activation(exT_sb[:, :, :].rearrange("p k q -> p (k q)"), ps_t[:, :], ACT.Copy
                                     ).then_inc(eT_sb, 1)

            with act.Fori(0, IMGS) as b:
                act.wait_ge(tap1, b * (TAPS * STEPS // 2) + 1)

                def phase1(s):
                    g = b * (2 * STEPS) + s.index
                    q = s.plus(1)
                    n = st_of(b, q)
                    if q.valid(STEPS):
                        act.wait_ge(xT_ready, done(n))
                        act.wait_ge(v_ready, freed(n, 1))
                        nc.scalar.activation(xnT[:, :, :].rearrange("p c t -> p (c t)"), ps_p[0][:, :], ACT.Copy
                                             ).then_inc(xnT_sb_ready, 1)
                    if s.valid(STEPS):
                        exps(g)
                    if q.valid(STEPS):
                        act.wait_ge(q_ready, done(n))
                        act.wait_ge(qk_stored[q.par], half_of(b, q) * 32 + 32)
                        act.wait_ge(s_ready, freed(b * (2 * STEPS) + q.index, 2))
                        for c in range(KC):
                            last = nc.scalar.activation(q_st[:, q.par, c, :], ps_p[1][:, ST * c:ST * c + ST],
                                                        ACT.Identity, bias=bq_sb[:, c:c + 1])
                        last.then_inc(q_sb, 1)
                    if s.valid(STEPS):
                        take_weights_T(g)
                    if q.valid(STEPS):
                        act.wait_ge(vT_ready, done(n))
                        rows = bass.ds(q.index * LINES + PAD, LINES)
                        nc.scalar.activation(v_pad[:, :, rows, PAD:PAD + W],
                                             ps_p[0][:, :].rearrange("p (c r w) -> p c r w", c=KC, w=W),
                                             ACT.Copy).then_inc(vT_sb, 1)

                run_steps(act, -1, STEPS - 1, LO, HI, phase1, settle)

                def phase2(s):
                    g = b * (2 * STEPS) + (s.index + STEPS)
                    if s.valid(STEPS):
                        exps(g)
                        take_weights_T(g)
                    q = s.plus(-2)
                    if q.valid(STEPS):
                        act.wait_ge(hT_ready, done(st_of(b, q)))
                        act.wait_ge(g_ready, freed(st_of(b, q), 1))
                        nc.scalar.activation(hT_sb[:, :, :].rearrange("p c t -> p (c t)"), ps_p[2][:, :], ACT.Copy
                                             ).then_inc(hT_done, 1)

                run_steps(act, 0, STEPS + 1, LO, HI, phase2, settle)
                act.wait_ge(r_chain, b * R_CHAIN + 2)
                nc.scalar.activation(rp[:, :, :], rl[:, :, :], ACT.Exp).then_inc(r_exp, 1)

            def take_fT(n):
                act.wait_ge(fT_ready, done(n))
                for c in range(KC):
                    last = nc.scalar.activation(fT_sb[:, c, :], ps_p[c][:, :], ACT.Copy)
                last.then_inc(fT_done, 1)

            take_fT(0)
            with act.Fori(0, E // 2) as pair:
                for par in range(2):
                    act.wait_ge(w_load[par], pair * 64 + 64)
                    settle(act)
                    with act.Fori(0, CHUNKS) as j:
                        n = pair * (2 * CHUNKS) + (j + par * CHUNKS)
                        act.wait_ge(f_ready, freed(n, 1))
                        for f in range(FB):
                            act.wait_ge(h_ready, n * FB + (f + 1 + CREDIT))
                            nc.scalar.activation(hm_sb[:, f, :], ps_s[:, f % 2, :], ACT.Relu,
                                                 bias=b1_sb[par][:, f:f + 1]).then_inc(relu_done, 1)
                        take_fT(n + 1)

        @block.vector
        def _(dve):
            nc.disable_value_cache = True
            for s_ in (stat1, xn_ready, k_sb, v_sb, sm_done, mx_done, sub_done, rec_done, o_sb,
                       oT_done, x2_ready, stat2, hn_ready, lg_ready, fn_ready, y_taken, yo_ready):
                dve.sem_inc(s_, CREDIT)
            dve.sem_inc(tap1, 1)
            nc.vector.memset(ones[:, :], 1.0).then_inc(made, 1)
            nc.vector.memset(r_run[:, :], 0.0)
            nc.vector.memset(half[:, :], -0.5)
            nc.vector.memset(r_reset[:, :, 1:RT], 1.0)
            nc.vector.memset(r_reset[:, :, 0], 0.0)
            nc.vector.memset(r_cum[:, :, 0], 0.0)
            nc.vector.memset(v_st[:, :, :, :, :], 1.0)
            nc.vector.memset(v1_st[:, :, :, :, :], 1.0)
            nc.vector.memset(v_pad[:, :, :, :], 0.0).then_inc(made, 1)
            dve.wait_ge(consts, 16 * CONST_DMAS)
            dve.wait_ge(made, 5)
            dve.wait_ge(r_ready, 5)
            dve.wait_ge(table_cleared, 16 * CLEAR_DMAS)

            def soft1(g, m):
                dve.wait_ge(s_ready, done(g))
                dve.wait_ge(e_ready, freed(g, 1))
                nc.vector.tensor_tensor(
                    sc_sb[:, :, :].rearrange("p (a r) k -> p a r k", r=LINES),
                    ps_s[:, :, :].rearrange("p i (c r k) -> p (i c) r k", c=KC, k=64),
                    masks[:, m, :, :].unsqueeze(2).broadcast_to([P, 4, LINES, 64]), ALU.add).then_inc(sm_done, 1)
                dve.wait_ge(sm_done, done(g))
                nc.vector.tensor_reduce(mx_sb[:, :], sc_sb[:, :, :], AX_X, ALU.max).then_inc(mx_done, 1)
                dve.wait_ge(mx_done, done(g))
                nc.vector.tensor_tensor(sc_sb[:, :, :], sc_sb[:, :, :],
                                        mx_sb[:, :].unsqueeze(2).broadcast_to([P, 16, 64]), ALU.subtract
                                        ).then_inc(sub_done, 1)

            def normalised(g, dst):
                dve.wait_ge(o_ready, done(g))
                nc.vector.reciprocal(rec_sb[:, :].rearrange("p (t n) -> p t n", t=TT), ps_o[:, :, :, KEY_DIM]
                                     ).then_inc(rec_done, 1)
                dve.wait_ge(rec_done, done(g))
                nc.vector.tensor_tensor(
                    dst, ps_o[:, :, :, 0:KEY_DIM],
                    rec_sb[:, :].rearrange("p (t n) -> p t n", t=TT).unsqueeze(3).broadcast_to(
                        [P, TT, HEADS, KEY_DIM]), ALU.mult).then_inc(o_sb, 1)

            def conv(cnt, c, chain, rows, cols, out_view, first, last_):
                for k in range(first, last_):
                    src = v_pad[:, c, rows(k // 5), cols(k % 5)]
                    if k == 0:
                        nc.vector.tensor_scalar(out_view, src, wl_sb[:, c, 0:1], bl_sb[:, c:c + 1],
                                                ALU.mult, ALU.add).then_inc(chain, 1)
                    else:
                        dve.wait_ge(chain, cnt + k)
                        nc.vector.scalar_tensor_tensor(out_view, src, wl_sb[:, c, k:k + 1], out_view,
                                                       ALU.mult, ALU.add).then_inc(chain, 1)

            def stats(src, sp_, tiles, n, st_sem, out_sem):
                for t in range(tiles):
                    last = nc.vector.bn_stats(stat[:, sp_, t, :], src[:, t, :])
                last.then_inc(st_sem, 1)
                dve.wait_ge(st_sem, n + 1)
                settle(dve)
                for t in range(tiles):
                    last = nc.vector.bn_aggr(mv[:, sp_, t, :], stat[:, sp_, t, :])
                last.then_inc(out_sem, 1)

            def centred(dst, src, sp_, tiles, ready):
                for t in range(tiles):
                    last = nc.vector.tensor_scalar(dst[:, t, :], src[:, t, :], mv[:, sp_, t, 0:1],
                                                   rstd[:, sp_, t:t + 1], ALU.subtract, ALU.mult)
                last.then_inc(ready, 1)

            def route(b):
                count = [0]

                def link(ins):
                    count[0] += 1
                    ins.then_inc(r_chain, 1)
                    dve.wait_ge(r_chain, b * R_CHAIN + count[0])

                v = nc.vector
                over_e = [P, RT, E]
                by_expert = "p t e -> p e t"
                dve.wait_ge(rl_load, b * 16 + 16)
                link(v.tensor_reduce(r_mx[:, :], rl[:, :, :], AX_X, ALU.max))
                link(v.tensor_tensor(rl[:, :, :], rl[:, :, :], r_mx[:, :].unsqueeze(2).broadcast_to(over_e),
                                     ALU.subtract))
                dve.wait_ge(r_exp, b + 1)
                link(v.tensor_reduce(r_sum[:, :], rp[:, :, :], AX_X, ALU.add))
                link(v.reciprocal(r_sum[:, :], r_sum[:, :]))
                link(v.tensor_tensor(rp[:, :, :], rp[:, :, :], r_sum[:, :].unsqueeze(2).broadcast_to(over_e),
                                     ALU.mult))
                link(v.tensor_reduce(r_mx[:, :], rp[:, :, :], AX_X, ALU.max))
                link(v.tensor_tensor(r_eq[:, :, :], rp[:, :, :], r_mx[:, :].unsqueeze(2).broadcast_to(over_e),
                                     ALU.is_equal))
                for e in range(1, E):
                    link(v.tensor_tensor(r_cum[:, :, e], r_cum[:, :, e - 1], r_eq[:, :, e - 1], ALU.add))
                link(v.scalar_tensor_tensor(r_oh[:, :, :], r_cum[:, :, :].rearrange(by_expert), 0.0,
                                            r_eq[:, :, :].rearrange(by_expert), ALU.is_equal, ALU.mult))
                flat = "p e t -> p (e t)"
                link(v.tensor_tensor_scan(r_pos[:, :, :].rearrange(flat), r_reset[:, :, :].rearrange(flat),
                                          r_oh[:, :, :].rearrange(flat), 0.0, ALU.mult, ALU.add))
                link(v.tensor_copy(r_tot[:, :], r_pos[:, :, RT - 1]))
                assert count[0] == R_TOTALS
                dve.wait_ge(r_pe, b + 1)
                link(v.tensor_tensor(r_base[:, :], ps_p[0][:, 0:E], r_run[:, :], ALU.add))
                link(v.tensor_tensor(r_run[:, :], ps_p[1][:, 0:E], r_run[:, :], ALU.add))
                link(v.tensor_tensor(r_pos[:, :, :], r_pos[:, :, :],
                                     r_base[:, :].unsqueeze(2).broadcast_to([P, E, RT]), ALU.add))
                link(v.tensor_scalar(r_big[:, :, :], r_pos[:, :, :], float(CAP), float(NO_TOKEN),
                                     ALU.is_gt, ALU.mult))
                link(v.tensor_tensor(r_pos[:, :, :], r_pos[:, :, :],
                                     r_first[:, :].unsqueeze(2).broadcast_to([P, E, RT]), ALU.add))
                link(v.tensor_tensor(r_pos[:, :, :], r_pos[:, :, :], r_big[:, :, :], ALU.add))
                link(v.tensor_tensor(r_pos[:, :, :], r_pos[:, :, :], r_oh[:, :, :], ALU.mult))
                link(v.tensor_reduce(r_slot[:, :], r_pos[:, :, :].rearrange("p e t -> p t e"), AX_X, ALU.add))
                dve.wait_ge(r_free, b + 1)
                link(v.tensor_scalar(r_slot_i[:, :], r_slot[:, :], -1.0, None, ALU.add))
                link(v.tensor_copy(r_pair[:, :, 0], r_tok[:, :]))
                link(v.tensor_copy(r_pair[:, :, 1:2].bitcast(F32), r_mx[:, :].unsqueeze(2)))
                link(v.tensor_scalar(r_tok[:, :], r_tok[:, :], float(IMG_TOK), None, ALU.add))
                assert count[0] == R_CHAIN

            SPLIT = (0, 4, 8, 13), (13, 17, 21, 25)

            with dve.Fori(0, IMGS) as b:
                def phase1(s):
                    g = b * (2 * STEPS) + s.index

                    def taps(k):
                        j = s.half - 1
                        if not (s.inside or 0 <= j < STEPS // 2):
                            return
                        if k == 0 and s.par == 0:
                            top = s.half * 2 if (s.inside or s.half < STEPS // 2) else STEPS - 1
                            dve.wait_ge(vT_sb, done(b * STEPS + top))
                        conv(b * (TAPS * STEPS // 2) + j * TAPS, 0, tap0,
                             lambda kh: bass.ds(j * (2 * LINES) + kh, 2 * LINES), lambda kw: slice(kw, kw + W),
                             lepe[:, 0, bass.ds(j * (2 * LINES), 2 * LINES), :], SPLIT[s.par][k], SPLIT[s.par][k + 1])

                    if s.valid(STEPS):
                        soft1(g, 0)
                    taps(0)
                    q = s.plus(1)
                    n = st_of(b, q)
                    if q.valid(STEPS):
                        dve.wait_ge(k_ready, done(n))
                        dve.wait_ge(qk_stored[q.par], half_of(b, q) * 32 + 32)
                        dve.wait_ge(s_ready, freed(b * (2 * STEPS) + q.index, 2))
                        for c in range(KC):
                            last = nc.vector.tensor_scalar(k_st[:, q.par, c, :], ps_p[2][:, ST * c:ST * c + ST],
                                                           bk_sb[:, c:c + 1], SCALING, ALU.add, ALU.mult)
                        last.then_inc(k_sb, 1)
                        dve.wait_ge(v_ready, done(n))
                        dve.wait_ge(o_ready, freed(b * (2 * STEPS) + q.index, 2))
                        nc.vector.tensor_tensor(
                            v_st[:, q.par, :, 0:KEY_DIM, :].rearrange("p t d n -> p t (d n)"),
                            ps_p[3][:, :].rearrange("p (t c) -> p t c", t=TT),
                            bv_sb[:, :].unsqueeze(1).broadcast_to([P, TT, C]), ALU.add).then_inc(v_sb, 1)
                    taps(1)
                    q = s.plus(2)
                    n = st_of(b, q)
                    if q.valid(STEPS):
                        dve.wait_ge(x_load[q.par], half_of(b, q) * 16 + 16)
                        stats(x_in[:, q.par], 0, TT, n, st_c, stat1)
                        dve.wait_ge(rstd1, n + 1)
                        dve.wait_ge(xT_ready, freed(n, 2))
                        centred(xn[:, q.par], x_in[:, q.par], 0, TT, xn_ready)
                    taps(2)
                    if s.valid(STEPS):
                        dve.wait_ge(v1_stored[s.par], half_of(b, s) * 16 + 16)
                        normalised(g, v1_st[:, s.par, :, 0:KEY_DIM, :].rearrange("p t d n -> p t n d"))

                run_steps(dve, -2, STEPS + 1, LO, HI, phase1, settle)

                def phase2(s):
                    g = b * (2 * STEPS) + (s.index + STEPS)

                    def taps(k):
                        j = s.half + s.par
                        if not (s.inside or 0 <= j < STEPS // 2):
                            return
                        cols = j * (2 * LINES)
                        sp_ = SPLIT[1 - s.par]
                        conv(b * (TAPS * STEPS // 2) + (j * TAPS + 1), 1, tap1,
                             lambda kh: slice(kh, kh + H), lambda kw: bass.ds(cols + kw, 2 * LINES),
                             lepe[:, 1, :, bass.ds(cols, 2 * LINES)], sp_[k], sp_[k + 1])

                    if s.valid(STEPS):
                        soft1(g, 1)
                    q = s.plus(-1)
                    n = st_of(b, q)
                    if q.valid(STEPS):
                        dve.wait_ge(oT_ready, done(n))
                        dve.wait_ge(y_ready, freed(n, 1))
                        dve.wait_ge(tap0, (b + 1) * (TAPS * STEPS // 2))
                        dve.wait_ge(tap1, b * (TAPS * STEPS // 2) + (q.half * TAPS + (TAPS + 1)))
                        cols = bass.ds(q.index * LINES, LINES)
                        for c in range(KC):
                            last = nc.vector.tensor_tensor(
                                oT_sb[:, c, :].rearrange("p (w h) -> p w h", h=H),
                                ps_p[0][:, ST * c:ST * c + ST].rearrange("p (w h) -> p w h", h=H),
                                lepe[:, c, :, cols].rearrange("p h w -> p w h"), ALU.add)
                        last.then_inc(oT_done, 1)
                    taps(0)
                    if q.valid(STEPS):
                        dve.wait_ge(y_ready, done(n))
                        dve.wait_ge(xb_ready, n + 1)
                        dve.wait_ge(x2_stored[q.par], half_of(b, q) * 64 + 64)
                        nc.vector.tensor_tensor(x2_st[:, q.par].rearrange("p t c -> p (t c)"), ps_p[1][:, :],
                                                x_r[:, q.par].rearrange("p t c -> p (t c)"), ALU.add
                                                ).then_inc(x2_ready, 1)
                        dve.wait_ge(x2_ready, done(n))
                        stats(x2_st[:, q.par], 1, TT, n, st_c2, stat2)
                    taps(1)
                    if q.valid(STEPS):
                        dve.wait_ge(rstd2, n + 1)
                        dve.wait_ge(hT_ready, freed(n, 2))
                        centred(hn[:, q.par], x2_st[:, q.par], 1, TT, hn_ready)
                    taps(2)
                    q = s.plus(-2)
                    n = st_of(b, q)
                    if s.valid(STEPS):
                        dve.wait_ge(oT_ready, freed(st_of(b, s), 2))
                        normalised(g, o2[:, s.par].rearrange("p t (d n) -> p t n d", n=HEADS))
                    if q.valid(STEPS):
                        dve.wait_ge(g_ready, done(n))
                        dve.wait_ge(lg_stored[q.par], half_of(b, q) * 32 + 32)
                        nc.vector.tensor_tensor(
                            lg_st[:, q.par], ps_p[3][:, 0:TT * E].rearrange("p (t e) -> p t e", t=TT),
                            gb_sb[:, :].unsqueeze(1).broadcast_to([P, TT, E]), ALU.add).then_inc(lg_ready, 1)

                run_steps(dve, -1, STEPS + 1, LO, HI, phase2, settle)
                route(b)

            def prepare(n, par):
                dve.wait_ge(gathered[par], n[1] * (16 * CT) + 16 * CT)
                n = n[0]
                for i in range(CT):
                    last = nc.vector.bn_stats(stat[:, 0, i, :], xg[par][:, i, :])
                last.then_inc(f_stat, 1)
                dve.wait_ge(f_stat, n + 1)
                settle(dve)
                for i in range(CT):
                    last = nc.vector.bn_aggr(mv[:, 0, i, :], stat[:, 0, i, :])
                last.then_inc(f_aggr, 1)
                dve.wait_ge(f_rstd, n + 1)
                dve.wait_ge(fT_ready, freed(n, 1))
                centred(fn, xg[par], 0, CT, fn_ready)

            prepare((0, 0), 0)
            with dve.Fori(0, E // 2) as pair:
                for epar in range(2):
                    dve.wait_ge(w_load[epar], pair * 64 + 64)
                    settle(dve)
                    with dve.Fori(0, CHUNKS // 2) as jj:
                        for par in range(2):
                            h = pair * CHUNKS + (jj + epar * (CHUNKS // 2))
                            n = h * 2 + par
                            prepare((n + 1, h + par), 1 - par)
                            dve.wait_ge(f_ready, done(n))
                            nc.vector.tensor_tensor(
                                y_sb, ps_t[:, :].rearrange("p (i c) -> p i c", i=CT),
                                b2_sb[epar].unsqueeze(1).broadcast_to([P, CT, C]), ALU.add).then_inc(y_taken, 1)
                            dve.wait_ge(y_taken, done(n))
                            prob = tok_g[:, par, :, 1:2].bitcast(F32).broadcast_to([P, CT, C])
                            links = [0]

                            def link(ins, n=n, links=links):
                                links[0] += 1
                                ins.then_inc(y_chain, 1)
                                dve.wait_ge(y_chain, n * 7 + links[0])

                            link(nc.vector.tensor_tensor(y_sb, y_sb, prob, ALU.mult))
                            link(nc.vector.tensor_scalar(r_sb, y_sb, -1e4, 1e4, ALU.max, ALU.min))
                            link(nc.vector.tensor_tensor(m_sb, y_sb, y_sb, ALU.is_equal))
                            link(nc.vector.tensor_tensor(r_sb, r_sb, m_sb, ALU.mult))
                            link(nc.vector.tensor_scalar(m_sb, y_sb, -FLT_MAX, FLT_MAX, ALU.max, ALU.min))
                            link(nc.vector.tensor_tensor(m_sb.bitcast(U32), m_sb, y_sb, ALU.is_equal))
                            settle(dve)
                            link(nc.vector.copy_predicated(r_sb, m_sb.bitcast(U32), y_sb))
                            nc.vector.tensor_tensor(yo[par], r_sb, xg[par], ALU.add).then_inc(yo_ready, 1)

        @block.gpsimd
        def _(pool):
            pool.sem_inc(staged, CREDIT)
            pool.sem_inc(r_free, 1)
            nc.gpsimd.memset(ident[:, :], 0.0).then_inc(made, 1)
            nc.gpsimd.iota(r_pair[:, :, :], pattern=[[0, 2 * RT]], base=NO_TOKEN, channel_multiplier=0
                           ).then_inc(r_ready, 1)
            pool.wait_ge(made, 3)
            nc.gpsimd.affine_select(out=ident[:, :], in_=ident[:, :], compare_op=ALU.not_equal, fill=1.0,
                                    base=0, pattern=[[-1, P]], channel_multiplier=1).then_inc(made, 1)
            nc.gpsimd.affine_select(out=upper[:, :], in_=ones[:, :], compare_op=ALU.is_gt, fill=0.0,
                                    base=0, pattern=[[1, P]], channel_multiplier=-1).then_inc(made, 1)
            nc.gpsimd.iota(r_slot_i[:, :], pattern=[[1, RT]], base=0, channel_multiplier=RT).then_inc(r_ready, 1)
            nc.gpsimd.iota(tok_g[:, 0, 0:CT, 0:2], pattern=[[CAP, E]], base=0, channel_multiplier=0
                           ).then_inc(r_ready, 1)
            pool.wait_ge(r_ready, 3)
            nc.gpsimd.tensor_copy(r_tok[:, :], r_slot_i[:, :]).then_inc(r_ready, 1)
            nc.gpsimd.tensor_copy(r_first[:, :], tok_g[:, 0, 0:CT, 0:2].rearrange("p a b -> p (a b)")
                                  ).then_inc(r_ready, 1)
            rows = (SLOTS + CHUNK) // P
            for top in range(0, rows, RT):
                k = min(RT, rows - top)
                pool.dma_start(slot_t[P * top:P * (top + k), :].rearrange("(p k) c -> p k c", p=P),
                               r_pair[:, 0:k, :]).then_inc(table_cleared, 16)
            pool.wait_ge(table_cleared, 16 * CLEAR_DMAS)
            pool.wait_ge(consts, 16 * CONST_DMAS)

            def inverse_deviation(k, tiles, seen, n, eps, eps_sem, out_sem):
                pool.wait_ge(seen, done(n))
                settle(pool)
                nc.gpsimd.tensor_scalar(veps[:, k, 0:tiles], mv[:, k, 0:tiles, 1], eps, None, ALU.add
                                        ).then_inc(eps_sem, 1)
                pool.wait_ge(eps_sem, n + 1)
                nc.gpsimd.tensor_tensor(rstd[:, k, 0:tiles], veps[:, k, 0:tiles], half[:, 0:tiles], ALU.pow
                                        ).then_inc(out_sem, 1)

            with pool.Fori(0, IMGS) as b:
                def phase1(s):
                    q = s.plus(2)
                    if q.valid(STEPS):
                        inverse_deviation(0, TT, stat1, st_of(b, q), 1e-6, eps1, rstd1)

                run_steps(pool, -2, STEPS - 3, LO, HI, phase1, settle)
                for n in range(2):
                    pool.wait_ge(qk_stored[n], b * (16 * STEPS) + (16 * STEPS + 32))
                    settle(pool)

                def phase2(s):
                    q = s.plus(1)
                    if q.valid(STEPS):
                        pool.wait_ge(s_ready, freed(b * (2 * STEPS) + (q.index + STEPS), 2))
                        settle(pool)
                        cols = bass.ds(q.index * LINES, LINES)
                        for dst, src in ((q_st, q_img), (k_st, k_img)):
                            nc.gpsimd.tensor_copy(
                                dst[:, q.par].rearrange("p c (w h) -> p c w h", h=H),
                                src[:, :, :].rearrange("p c (h w) -> p c w h", w=W)[:, :, cols, :]
                            ).then_inc(staged, 1)
                    if s.valid(STEPS):
                        pool.wait_ge(xr_load[s.par], half_of(b, s) * 32 + 32)
                        nc.gpsimd.tensor_tensor(x_r[:, s.par], x_r[:, s.par],
                                                bo_sb[:, :].unsqueeze(1).broadcast_to([P, TT, C]), ALU.add
                                                ).then_inc(xb_ready, 1)
                    q = s.plus(-1)
                    if q.valid(STEPS):
                        inverse_deviation(1, TT, stat2, st_of(b, q), 1e-5, eps2, rstd2)

                run_steps(pool, -1, STEPS, LO, HI, phase2, settle)
                pool.wait_ge(r_chain, (b + 1) * R_CHAIN)
                settle(pool)
                for t in range(RT):
                    nc.gpsimd.indirect_dma_start(
                        out=slot_t, out_offset=bass.IndirectOffsetOnAxis(ap=r_slot_i[:, t:t + 1], axis=0),
                        in_=r_pair[:, t, :], in_offset=None, bounds_check=SLOTS - 1, oob_is_err=False
                    ).then_inc(r_scattered, 16)
                pool.wait_ge(r_scattered, b * (16 * RT) + 16 * RT)
                pool.sem_inc(r_free, 1)

            for n in range(2):
                pool.wait_ge(x2_stored[n], 32 * IMGS * STEPS + 64)
                settle(pool)

            def gather(slots, n, h, par):
                pool.dma_start(tok_g[:, par, :, :], slot_t[slots, :].rearrange("(p i) c -> p i c", i=CT)
                               ).then_inc(tok_load[par], 16)
                pool.wait_ge(tok_load[par], h * 16 + 16)
                settle(pool)
                for i in range(CT):
                    nc.gpsimd.indirect_dma_start(
                        out=xg[par][:, i, :], out_offset=None, in_=x2_t,
                        in_offset=bass.IndirectOffsetOnAxis(ap=tok_g[:, par, i, 0:1], axis=0),
                        bounds_check=TOK - 1, oob_is_err=False).then_inc(gathered[par], 16)
                pool.wait_ge(f_aggr, n + 1)
                settle(pool)
                nc.gpsimd.tensor_scalar(veps[:, 0, :], mv[:, 0, :, 1], 1e-5, None, ALU.add).then_inc(f_eps, 1)
                pool.wait_ge(f_eps, n + 1)
                nc.gpsimd.tensor_tensor(rstd[:, 0, :], veps[:, 0, :], half[:, :], ALU.pow).then_inc(f_rstd, 1)

            gather(slice(0, CHUNK), 0, 0, 0)
            with pool.Fori(0, E * CHUNKS // 2) as h:
                for par in range(2):
                    n = h * 2 + par
                    gather(bass.ds((n + 1) * CHUNK, CHUNK), n + 1, h + par, 1 - par)
                    pool.wait_ge(yo_ready, done(n))
                    settle(pool)
                    for i in range(CT):
                        nc.gpsimd.indirect_dma_start(
                            out=out_t, out_offset=bass.IndirectOffsetOnAxis(ap=tok_g[:, par, i, 0:1], axis=0),
                            in_=yo[par][:, i, :], in_offset=None, bounds_check=TOK - 1, oob_is_err=False
                        ).then_inc(scattered[par], 16)
                    pool.wait_ge(scattered[par], h * (16 * CT) + 16 * CT)
                    settle(pool)


_INS = ["x", "mask_h", "mask_w", "wqT", "bq", "wkT", "bk", "wvT", "bv", "wlepe", "blepe", "woT", "bo",
        "gate_w", "gate_b", "w1", "b1", "w2", "b2"]


def kernel(x, L0_conv_mask_h, L0_conv_mask_w, L0_conv_Wq, L0_conv_bq, L0_conv_Wk, L0_conv_bk, L0_conv_Wv,
           L0_conv_bv, L0_conv_Wlepe, L0_conv_blepe, L0_conv_Wo, L0_conv_bo, L0_ffn_gate_w, L0_ffn_gate_b,
           L0_ffn_w1, L0_ffn_b1, L0_ffn_w2, L0_ffn_b2):
    import concourse.bacc as bacc
    from concourse.bass_utils import run_bass_kernel_spmd

    def rows(a):
        return np.ascontiguousarray(a)

    channels = np.shape(x)[-1]
    experts, width = np.shape(L0_ffn_b1)

    def by_value(a):
        split = np.reshape(a, np.shape(a)[:-1] + (HEADS, KEY_DIM))
        return np.ascontiguousarray(np.reshape(np.swapaxes(split, -1, -2), np.shape(a)))

    data = {
        "x": rows(x), "mask_h": rows(L0_conv_mask_h), "mask_w": rows(L0_conv_mask_w),
        "wqT": rows(np.transpose(L0_conv_Wq)), "bq": rows(L0_conv_bq),
        "wkT": rows(np.transpose(L0_conv_Wk)), "bk": rows(L0_conv_bk),
        "wvT": by_value(np.transpose(L0_conv_Wv)), "bv": by_value(L0_conv_bv),
        "wlepe": rows(np.transpose(by_value(np.reshape(L0_conv_Wlepe, (TAPS, channels))))),
        "blepe": by_value(L0_conv_blepe),
        "woT": rows(np.transpose(by_value(L0_conv_Wo))), "bo": rows(L0_conv_bo),
        "gate_w": rows(L0_ffn_gate_w), "gate_b": rows(L0_ffn_gate_b),
        "w1": rows(L0_ffn_w1),
        "b1": rows(np.reshape(np.transpose(np.reshape(L0_ffn_b1, (experts, width // P, P)), (2, 0, 1)), (P, -1))),
        "w2": rows(L0_ffn_w2), "b2": rows(L0_ffn_b2),
    }
    nc = bacc.Bacc("TRN2", target_bir_lowering=False, num_devices=1)
    arrays, args = {}, []
    for name in _INS:
        a = data[name]
        arrays[f"in_{name}"] = a
        args.append(nc.dram_tensor(f"in_{name}", a.shape, mybir.dt.from_np(a.dtype), kind="ExternalInput").ap())
    out = nc.dram_tensor("out_0", data["x"].shape, F32, kind="ExternalOutput").ap()
    metaformer_kernel(nc, *args, out)
    result = run_bass_kernel_spmd(nc, [arrays], core_ids=[0])
    return result.results[0]["out_0"]
```

```python
import math
from contextlib import ExitStack

import numpy as np
import concourse.bass as bass
from concourse import mybir
from concourse.alu_op_type import AluOpType as ALU

F32 = mybir.dt.float32
I32 = mybir.dt.int32
U32 = mybir.dt.uint32
ACT = mybir.ActivationFunctionType
AX_X = mybir.AxisListType.X

P = 128
HEADS = 8
KEY_DIM = 32
VCOLS = KEY_DIM + 1
LINES = 4
PAD = 2
TAPS = 25
CREDIT = 2
CHUNK = 512
FLT_MAX = 3.4028234663852886e38
NO_TOKEN = 1 << 20


class Step:

    def __init__(self, half, par, inside):
        self.half, self.par, self.inside = half, par, inside

    def plus(self, off):
        total = self.par + off
        return Step(self.half + total // 2, total % 2, self.inside)

    @property
    def index(self):
        return self.half * 2 + self.par

    def valid(self, count):
        return self.inside or 0 <= self.index < count


def run_steps(eng, first, last, lo, hi, emit, before_loop):
    for s in range(first, lo):
        emit(Step(s // 2, s % 2, False))
    before_loop(eng)
    with eng.Fori(lo // 2, hi // 2) as half:
        for par in range(2):
            emit(Step(half, par, True))
    for s in range(hi, last + 1):
        emit(Step(s // 2, s % 2, False))


def done(n):
    return n + (1 + CREDIT)


def freed(n, buffers):
    return n + (1 + CREDIT - buffers)


def metaformer_kernel(nc, x, mask_h, mask_w, wqT, bq, wkT, bk, wvT, bv, wlepe, blepe, woT, bo,
                      gate_w, gate_b, w1, b1, w2, b2, out):
    IMGS, H, W, C = x.shape
    E, _, F = w1.shape
    TOK = IMGS * H * W
    IMG_TOK = H * W
    KC = C // P
    DC = P // HEADS
    STEPS = H // LINES
    ST = LINES * W
    TT = ST // P
    CAP = math.ceil(1.25 * TOK / E)
    CHUNKS = CAP // CHUNK
    SLOTS = E * CAP
    FB = F // P
    CT = CHUNK // P
    PW = W + 2 * PAD
    VROW = HEADS * VCOLS
    RT = IMG_TOK // P
    SCALING = float(KEY_DIM) ** -0.5
    assert H == W == 64 and C == 256 and CAP % (2 * CHUNK) == 0 and E % 2 == 0
    LO, HI = 4, 12

    x_t = x.rearrange("b h w c -> (b h w) c")
    out_t = out.rearrange("b h w c -> (b h w) c")
    v1_t = nc.dram_tensor("v1_rows", [TOK, VROW], F32).ap()
    x2_t = nc.dram_tensor("x2_rows", [TOK, C], F32).ap()
    lg_t = nc.dram_tensor("gate_logits", [TOK, E], F32).ap()
    slot_t = nc.dram_tensor("slot_table", [SLOTS + 2 * CHUNK, 2], I32).ap()

    with ExitStack() as ctx:
        def sb(name, shape, dt=F32):
            return ctx.enter_context(nc.sbuf_tensor(name, shape, dt))

        def sem(name):
            return ctx.enter_context(nc.semaphore(name))

        q_img = sb("q_img", [P, KC, IMG_TOK])
        k_img = sb("k_img", [P, KC, IMG_TOK])
        v_pad = sb("v_pad", [P, KC, H + 2 * PAD, PW])
        lepe = sb("lepe", [P, KC, H, W])
        q_st = sb("q_st", [P, 2, KC, ST])
        k_st = sb("k_st", [P, 2, KC, ST])
        v_st = sb("v_st", [P, 2, TT, VCOLS, HEADS])
        sc_sb = sb("sc_sb", [P, 4 * LINES, 64])
        ex_sb = sb("ex_sb", [P, 4 * LINES, 64])
        exT_sb = sb("exT_sb", [P, 8, P])
        mx_sb = sb("mx_sb", [P, 16])
        rec_sb = sb("rec_sb", [P, 16])
        v1_st = sb("v1_st", [P, 2, TT, VCOLS, HEADS])
        x_in = sb("x_in", [P, 2, TT, C])
        xn = sb("xn", [P, 2, TT, C])
        xnT = sb("xnT", [P, KC, ST])
        oT_sb = sb("oT_sb", [P, KC, ST])
        o2 = sb("o2", [P, 2, TT, C])
        x_r, hn = x_in, xn
        x2_st = sb("x2_st", [P, 2, TT, C])
        hT_sb = sb("hT_sb", [P, KC, ST])
        lg_st = sb("lg_st", [P, 2, TT, E])
        masks = sb("masks", [P, 2, 4, 64])
        wq_sb, wk_sb, wv_sb, wo_sb = (sb(n, [P, KC, C]) for n in ("wq_sb", "wk_sb", "wv_sb", "wo_sb"))
        gw_sb = sb("gw_sb", [P, KC, E])
        gb_sb = sb("gb_sb", [P, E])
        bq_sb = sb("bq_sb", [P, KC])
        bk_sb = sb("bk_sb", [P, KC])
        bv_sb = sb("bv_sb", [P, C])
        bo_sb = sb("bo_sb", [P, C])
        wl_sb = sb("wl_sb", [P, KC, TAPS])
        bl_sb = sb("bl_sb", [P, KC])
        ident = sb("ident", [P, P])
        upper = sb("upper", [P, P])
        ones = sb("ones", [P, P])
        stat = sb("stat", [P, 2, 4, 6])
        mv = sb("mv", [P, 2, 4, 2])
        veps = sb("veps", [P, 2, 4])
        rstd = sb("rstd", [P, 2, 4])
        half = sb("half", [P, 4])
        q_flat = q_img[:, :, :].rearrange("p c t -> p (c t)")
        k_flat = k_img[:, :, :].rearrange("p c t -> p (c t)")
        W1N, W2N = KC * F, FB * C
        w1_sb = [(q_flat, k_flat)[h][:, 0:W1N].rearrange("p (c f) -> p c f", c=KC) for h in range(2)]
        w2_sb = [(q_flat, k_flat)[h][:, W1N:W1N + W2N].rearrange("p (c f) -> p c f", c=FB) for h in range(2)]
        b1_sb = [(q_flat, k_flat)[h][:, W1N + W2N:W1N + W2N + FB] for h in range(2)]
        b2_sb = [(q_flat, k_flat)[h][:, W1N + W2N + FB:W1N + W2N + FB + C] for h in range(2)]
        l_flat = lepe[:, :, :, :].rearrange("p c h w -> p (c h w)")
        hm_sb = l_flat[:, 0:FB * CHUNK].rearrange("p (f t) -> p f t", f=FB)
        fT_sb = l_flat[:, FB * CHUNK:FB * CHUNK + KC * CHUNK].rearrange("p (c t) -> p c t", c=KC)
        v_flat = v_pad[:, :, :, :].rearrange("p c h w -> p (c h w)")
        CN = CT * C
        xg = [v_flat[:, n * CN:(n + 1) * CN].rearrange("p (i c) -> p i c", i=CT) for n in range(2)]
        fn = v_flat[:, 2 * CN:3 * CN].rearrange("p (i c) -> p i c", i=CT)
        y_sb = v_flat[:, 3 * CN:4 * CN].rearrange("p (i c) -> p i c", i=CT)
        r_sb = v_flat[:, 4 * CN:5 * CN].rearrange("p (i c) -> p i c", i=CT)
        m_sb = v_flat[:, 5 * CN:6 * CN].rearrange("p (i c) -> p i c", i=CT)
        yo = [v_flat[:, (6 + n) * CN:(7 + n) * CN].rearrange("p (i c) -> p i c", i=CT) for n in range(2)]
        tok_g = sb("tok_g", [P, 2, CT, 2], I32)
        tok_s = sb("tok_s", [P, 2, CT], I32)
        prob_s = sb("prob_s", [P, 2, CT])
        rl = sb("rl", [P, RT, E])
        rp = sb("rp", [P, RT, E])
        r_eq = sb("r_eq", [P, RT, E])
        r_cum = sb("r_cum", [P, RT, E])
        r_oh = sb("r_oh", [P, E, RT])
        r_pos = sb("r_pos", [P, E, RT])
        r_big = sb("r_big", [P, E, RT])
        r_mx = sb("r_mx", [P, RT])
        r_sum = sb("r_sum", [P, RT])
        r_slot = sb("r_slot", [P, RT])
        r_slot_i = sb("r_slot_i", [P, RT], I32)
        r_tok = sb("r_tok", [P, RT])
        r_pair = sb("r_pair", [P, RT, 2], I32)
        r_reset = sb("r_reset", [P, E, RT])
        r_run = sb("r_run", [P, E])
        r_tot = sb("r_tot", [P, E])
        r_base = sb("r_base", [P, E])
        r_first = sb("r_first", [P, E])

        ps_s = ctx.enter_context(nc.psum_tensor("ps_s", [P, 2, 512], F32))
        ps_t = ctx.enter_context(nc.psum_tensor("ps_t", [P, 1024], F32))
        ps_p = [ctx.enter_context(nc.psum_tensor(f"ps_p{n}", [P, 512], F32)) for n in range(4)]
        ps_o = ps_t[:, :].rearrange("p (t n) -> p t n", t=TT)[:, :, 0:VROW].rearrange(
            "p t (n d) -> p t n d", n=HEADS)

        consts = sem("consts_loaded")
        made = sem("constants_made")
        bk_scaled = sem("bk_scaled")
        x_load = [sem(f"x_load{n}") for n in range(2)]
        qk_stored = [sem(f"qk_stored{n}") for n in range(2)]
        v1_stored = [sem(f"v1_stored{n}") for n in range(2)]
        v_load = [sem(f"v_load{n}") for n in range(2)]
        xr_load = [sem(f"xr_load{n}") for n in range(2)]
        x2_stored = [sem(f"x2_stored{n}") for n in range(2)]
        lg_stored = [sem(f"lg_stored{n}") for n in range(2)]
        stat1, eps1, rstd1, xn_ready = sem("stat1"), sem("eps1"), sem("rstd1"), sem("xn_ready")
        xT_ready, xnT_sb_ready = sem("xT_ready"), sem("xnT_sb_ready")
        q_ready, k_ready, v_ready = sem("q_ready"), sem("k_ready"), sem("v_ready")
        q_sb, k_sb, v_sb = sem("q_sb"), sem("k_sb"), sem("v_sb")
        vT_ready, vT_sb = sem("vT_ready"), sem("vT_sb")
        conv_done = sem("conv_done")
        chain = sem("vector_chain")
        s_ready, sub_done = sem("s_ready"), sem("sub_done")
        e_ready, eT_ready, eT_sb = sem("e_ready"), sem("eT_ready"), sem("eT_sb")
        o_ready, o_sb = sem("o_ready"), sem("o_sb")
        staged, xb_ready = sem("staged"), sem("xb_ready")
        oT_ready, oT_done, y_ready, x2_ready = sem("oT_ready"), sem("oT_done"), sem("y_ready"), sem("x2_ready")
        stat2, eps2, rstd2, hn_ready = sem("stat2"), sem("eps2"), sem("rstd2"), sem("hn_ready")
        hT_ready, hT_done, g_ready, lg_ready = sem("hT_ready"), sem("hT_done"), sem("g_ready"), sem("lg_ready")
        passed = sem("passed")
        table_cleared = sem("table_cleared")
        r_free = sem("r_free")
        rl_load, r_chain, r_exp, r_pe, r_ready, r_scattered = (
            sem(n) for n in ("rl_load", "r_chain", "r_exp", "r_pe", "r_ready", "r_scattered"))
        w_load = [sem(f"w_load{n}") for n in range(2)]
        tok_load = [sem(f"tok_load{n}") for n in range(2)]
        gathered = [sem(f"gathered{n}") for n in range(2)]
        scattered = [sem(f"scattered{n}") for n in range(2)]
        f_aggr, f_eps, f_rstd, fn_ready = (sem(n) for n in ("f_aggr", "f_eps", "f_rstd", "fn_ready"))
        tok_taken, yo_free = sem("tok_taken"), sem("yo_free")
        fT_ready, fT_done, h_ready, relu_done, f_ready, y_taken, yo_ready = (
            sem(n) for n in ("fT_ready", "fT_done", "h_ready", "relu_done", "f_ready", "y_taken", "yo_ready"))

        CONST_DMAS = 5 + 3 + 3 + 1 + 8

        R_TOTALS = 7 + (E - 1) + 3
        R_CHAIN = R_TOTALS + 12
        CLEAR_DMAS = math.ceil((SLOTS + 2 * CHUNK) / P / RT)

        block = ctx.enter_context(nc.Block())

        def settle(eng):
            eng.sem_inc(passed, 1)

        def st_of(b, s):
            return b * STEPS + s.index

        def half_of(b, s):
            return b * (STEPS // 2) + s.half

        def tokens_rows(dram, b, s):
            return dram[bass.ds(b * IMG_TOK + s.index * ST, ST), :].rearrange("(t p) c -> p t c", p=P)

        def tokens_cols(dram, b, s, s2):
            img = dram[bass.ds(b * IMG_TOK, IMG_TOK), :].rearrange("(h w) c -> h w c", w=W)
            cols = img[:, bass.ds(s.index * LINES, LINES), :].rearrange("h (t s2) c -> h t s2 c", s2=2)
            return cols[:, :, s2, :]

        @block.sync
        def _(sp):
            for dst, src in ((wq_sb, wqT), (wk_sb, wkT), (wv_sb, wvT), (wo_sb, woT), (gw_sb, gate_w)):
                sp.dma_start(dst[:, :, :], src.rearrange("(c p) n -> p c n", p=P)).then_inc(consts, 16)
            for dst, src in ((bq_sb, bq), (bk_sb, bk), (bl_sb, blepe)):
                sp.dma_start(dst[:, :], src.rearrange("(c p) -> p c", p=P),
                             allow_slow_non_contiguous=True).then_inc(consts, 16)
            for dst, src in ((bv_sb, bv), (bo_sb, bo), (gb_sb, gate_b)):
                sp.dma_start(dst[:, :], src.partition_broadcast(P)).then_inc(consts, 16)
            sp.dma_start(wl_sb[:, :, :], wlepe.rearrange("(c p) k -> p c k", p=P)).then_inc(consts, 16)
            for m, mask in enumerate((mask_w, mask_h)):
                by_head = mask.rearrange("(c i e) q k -> e i q c k", i=2, e=2)
                for e in range(2):
                    for i in range(2):
                        sp.dma_start(masks[64 * e:64 * e + 64, m, 2 * i:2 * i + 2, :],
                                     by_head[e, i]).then_inc(consts, 16)
            for n in range(2):
                sp.sem_inc(v1_stored[n], 16)
                sp.sem_inc(qk_stored[n], 32)
                sp.sem_inc(x2_stored[n], 64)
                sp.sem_inc(lg_stored[n], 32)

            with sp.Fori(0, IMGS) as b:
                def phase1(s):
                    q = s.plus(3)
                    if q.valid(STEPS):
                        sp.wait_ge(xn_ready, freed(st_of(b, q), 2))
                        sp.dma_start(x_in[:, q.par], tokens_rows(x_t, b, q)).then_inc(x_load[q.par], 16)
                    q = s.plus(1)
                    if q.valid(STEPS):
                        if not q.inside and q.index == 0:
                            sp.wait_ge(staged, b * (2 * STEPS) + CREDIT)
                        cols = bass.ds(q.index * ST, ST)
                        sp.wait_ge(q_sb, done(st_of(b, q)))
                        sp.dma_start(q_img[:, :, cols], q_st[:, q.par]).then_inc(qk_stored[q.par], 16)
                        sp.wait_ge(k_sb, done(st_of(b, q)))
                        settle(sp)
                        sp.dma_start(k_img[:, :, cols], k_st[:, q.par]).then_inc(qk_stored[q.par], 16)
                    q = s.plus(-1)
                    if q.valid(STEPS):
                        sp.wait_ge(o_sb, done(b * (2 * STEPS) + q.index))
                        sp.dma_start(tokens_rows(v1_t, b, q),
                                     v1_st[:, q.par].rearrange("p t d n -> p t (d n)")).then_inc(v1_stored[q.par], 16)

                run_steps(sp, -3, STEPS, LO, HI, phase1, settle)
                for n in range(2):
                    sp.wait_ge(v1_stored[n], b * (8 * STEPS) + (8 * STEPS + 16))
                    settle(sp)

                def phase2(s):
                    q = s.plus(1)
                    if q.valid(STEPS):
                        sp.wait_ge(o_ready, freed(b * (2 * STEPS) + (q.index + STEPS), 2))
                        for s2 in range(2):
                            sp.dma_start(v_st[64 * s2:64 * s2 + 64, q.par].rearrange("p t d n -> p t (d n)"),
                                         tokens_cols(v1_t, b, q, s2)).then_inc(v_load[q.par], 16)
                    if s.valid(STEPS):
                        sp.wait_ge(x2_ready, freed(st_of(b, s), 2))
                        for s2 in range(2):
                            sp.dma_start(x_r[64 * s2:64 * s2 + 64, s.par], tokens_cols(x_t, b, s, s2)
                                         ).then_inc(xr_load[s.par], 16)
                    q = s.plus(-2)
                    if q.valid(STEPS):
                        sp.wait_ge(x2_ready, done(st_of(b, q)))
                        for s2 in range(2):
                            for dram in (x2_t, out_t):
                                sp.dma_start(tokens_cols(dram, b, q, s2), x2_st[64 * s2:64 * s2 + 64, q.par]
                                             ).then_inc(x2_stored[q.par], 16)
                    q = s.plus(-3)
                    if q.valid(STEPS):
                        sp.wait_ge(lg_ready, done(st_of(b, q)))
                        for s2 in range(2):
                            sp.dma_start(tokens_cols(lg_t, b, q, s2), lg_st[64 * s2:64 * s2 + 64, q.par]
                                         ).then_inc(lg_stored[q.par], 16)

                run_steps(sp, -1, STEPS + 2, LO, HI, phase2, settle)
                for n in range(2):
                    sp.wait_ge(lg_stored[n], b * (16 * STEPS) + (16 * STEPS + 32))
                    settle(sp)
                sp.dma_start(rl[:, :, :], lg_t[bass.ds(b * IMG_TOK, IMG_TOK), :].rearrange(
                    "(p t) e -> p t e", t=RT)).then_inc(rl_load, 16)

            w1_rows = w1.rearrange("e d f -> (e d) f")
            w2_rows = w2.rearrange("e f d -> (e f) d")

            def weights(e, par):
                for dst, src in ((w1_sb[par], w1_rows[bass.ds(e * C, C), :]),
                                 (w2_sb[par], w2_rows[bass.ds(e * F, F), :])):
                    sp.dma_start(dst, src.rearrange("(c p) n -> p c n", p=P)).then_inc(w_load[par], 16)
                sp.dma_start(b1_sb[par], b1[:, bass.ds(e * FB, FB)]).then_inc(w_load[par], 16)
                sp.dma_start(b2_sb[par], b2[bass.ds(e, 1), :].rearrange("a c -> (a c)").partition_broadcast(P)
                             ).then_inc(w_load[par], 16)

            def tokens(slots, par):
                sp.dma_start(tok_g[:, par, :, :], slot_t[slots, :].rearrange("(p i) c -> p i c", i=CT)
                             ).then_inc(tok_load[par], 16)

            sp.wait_ge(r_free, IMGS + 1)
            settle(sp)
            for par in range(2):
                tokens(slice(par * CHUNK, (par + 1) * CHUNK), par)
            sp.wait_ge(staged, 2 * IMGS * STEPS + CREDIT)
            settle(sp)
            weights(0, 0)
            weights(1, 1)

            def tokens_of_expert(pair, epar):
                with sp.Fori(0, CHUNKS // 2) as jj:
                    for par in range(2):
                        n = (pair * CHUNKS + (jj + epar * (CHUNKS // 2))) * 2 + par
                        sp.wait_ge(tok_taken, done(n))
                        settle(sp)
                        tokens(bass.ds((n + 2) * CHUNK, CHUNK), par)

            with sp.Fori(0, E // 2 - 1) as pair:
                for epar in range(2):
                    tokens_of_expert(pair, epar)
                    sp.wait_ge(y_taken, pair * (2 * CHUNKS) + ((epar + 1) * CHUNKS + CREDIT))
                    settle(sp)
                    weights(pair * 2 + (epar + 2), epar)
            for epar in range(2):
                tokens_of_expert(E // 2 - 1, epar)
            for par in range(2):
                sp.wait_ge(tok_load[par], 16 * (E * CHUNKS // 2 + 1))
            for n in range(2):
                sp.wait_ge(x2_stored[n], 32 * IMGS * STEPS + 64)
                sp.wait_ge(scattered[n], 16 * CT * (E * CHUNKS // 2))

        @block.tensor
        def _(pe):
            for s_ in (xT_ready, q_ready, k_ready, v_ready, vT_ready, s_ready, eT_ready, o_ready,
                       oT_ready, y_ready, hT_ready, g_ready, fT_ready, f_ready):
                pe.sem_inc(s_, CREDIT)
            pe.sem_inc(h_ready, CREDIT)
            pe.wait_ge(consts, 16 * CONST_DMAS)
            pe.wait_ge(made, 5)

            def scores(g, par):
                pe.wait_ge(sub_done, freed(g, 1))
                for c in range(KC):
                    for r in range(LINES):
                        for a in range(4):
                            i, e = a // 2, a % 2
                            rows = slice(32 * a, 32 * a + 32)
                            line = slice(64 * r, 64 * r + 64)
                            col = 256 * c + 64 * r
                            last = nc.tensor.matmul(ps_s[64 * e:64 * e + 64, i, col:col + 64],
                                                    q_st[rows, par, c, line], k_st[rows, par, c, line],
                                                    start=True, stop=True)
                last.then_inc(s_ready, 1)

            def weights_T(g):
                pe.wait_ge(e_ready, done(g))
                pe.wait_ge(o_sb, freed(g, 1))
                for k in range(8):
                    ic, rp_ = k // 2, k % 2
                    src = ex_sb[:, LINES * ic + 2 * rp_:LINES * ic + 2 * rp_ + 2, :].rearrange("p r k -> p (r k)")
                    last = nc.tensor.transpose(ps_t[:, P * k:P * k + P], src, ident[:, :])
                last.then_inc(eT_ready, 1)

            def values(g, par):
                pe.wait_ge(eT_sb, done(g))
                settle(pe)
                for t in range(TT):
                    for c in range(KC):
                        for i in range(2):
                            for e in range(2):
                                for r in range(2):
                                    n = 4 * c + 2 * i + e
                                    rows = slice(64 * r, 64 * r + 64)
                                    last = nc.tensor.matmul(
                                        ps_o[rows, t, n, :], exT_sb[rows, 2 * (2 * i + c) + t, 64 * e:64 * e + 64],
                                        v_st[rows, par, t, :, n], start=True, stop=True)
                last.then_inc(o_ready, 1)

            with pe.Fori(0, IMGS) as b:
                def phase1(s):
                    g = b * (2 * STEPS) + s.index
                    q = s.plus(-1)
                    if q.valid(STEPS):
                        weights_T(g - 1)
                    if s.valid(STEPS):
                        pe.wait_ge(q_sb, done(st_of(b, s)))
                        pe.wait_ge(k_sb, done(st_of(b, s)))
                        scores(g, s.par)
                        pe.wait_ge(v_sb, done(st_of(b, s)))
                        for c in range(KC):
                            for t in range(TT):
                                last = nc.tensor.transpose(ps_p[1][:, ST * c + P * t:ST * c + P * t + P],
                                                           v_st[:, s.par, t, DC * c:DC * c + DC, :].rearrange("p d n -> p (d n)"),
                                                           ident[:, :])
                        last.then_inc(vT_ready, 1)
                    q = s.plus(1)
                    n = st_of(b, q)
                    if q.valid(STEPS):
                        pe.wait_ge(xn_ready, done(n))
                        for c in range(KC):
                            for t in range(TT):
                                last = nc.tensor.transpose(ps_p[0][:, ST * c + P * t:ST * c + P * t + P],
                                                           xn[:, q.par, t, P * c:P * c + P], ident[:, :])
                        last.then_inc(xT_ready, 1)
                    if s.plus(-1).valid(STEPS):
                        values(g - 1, s.plus(-1).par)
                    if q.valid(STEPS):
                        pe.wait_ge(xnT_sb_ready, done(n))
                        pe.wait_ge(vT_sb, freed(n, 1))
                        for bank, wt, taken, ready in ((1, wq_sb, q_sb, q_ready), (2, wk_sb, k_sb, k_ready)):
                            pe.wait_ge(taken, freed(n, 1))
                            for m in range(KC):
                                for c in range(KC):
                                    last = nc.tensor.matmul(ps_p[bank][:, ST * m:ST * m + ST],
                                                            wt[:, c, P * m:P * m + P], xnT[:, c, :],
                                                            start=(c == 0), stop=(c == KC - 1))
                            last.then_inc(ready, 1)
                        pe.wait_ge(v_sb, freed(n, 1))
                        for t in range(TT):
                            for c in range(KC):
                                last = nc.tensor.matmul(ps_p[3][:, C * t:C * t + C], xnT[:, c, P * t:P * t + P],
                                                        wv_sb[:, c, :], start=(c == 0), stop=(c == KC - 1))
                        last.then_inc(v_ready, 1)

                run_steps(pe, -1, STEPS, LO, HI, phase1, settle)
                pe.wait_ge(vT_sb, done(b * STEPS + (STEPS - 1)))

                def phase2(s):
                    g = b * (2 * STEPS) + (s.index + STEPS)
                    q1, q2, q3 = s.plus(-1), s.plus(-2), s.plus(-3)
                    if q1.valid(STEPS):
                        weights_T(g - 1)
                    if s.valid(STEPS):
                        pe.wait_ge(staged, st_of(b, s) * 2 + (2 + CREDIT))
                        scores(g, s.par)
                    if q2.valid(STEPS):
                        pe.wait_ge(o_sb, done(g - 2))
                        pe.wait_ge(oT_done, freed(st_of(b, q2), 1))
                        for c in range(KC):
                            for t in range(TT):
                                last = nc.tensor.transpose(ps_p[0][:, ST * c + P * t:ST * c + P * t + P],
                                                           o2[:, q2.par, t, P * c:P * c + P], ident[:, :])
                        last.then_inc(oT_ready, 1)
                    if q3.valid(STEPS):
                        pe.wait_ge(hn_ready, done(st_of(b, q3)))
                        pe.wait_ge(hT_done, freed(st_of(b, q3), 1))
                        for c in range(KC):
                            for t in range(TT):
                                last = nc.tensor.transpose(ps_p[2][:, ST * c + P * t:ST * c + P * t + P],
                                                           hn[:, q3.par, t, P * c:P * c + P], ident[:, :])
                        last.then_inc(hT_ready, 1)
                    if q1.valid(STEPS):
                        pe.wait_ge(v_load[q1.par], half_of(b, q1) * 32 + 32)
                        values(g - 1, q1.par)
                    if q2.valid(STEPS):
                        pe.wait_ge(oT_done, done(st_of(b, q2)))
                        pe.wait_ge(x2_ready, freed(st_of(b, q2), 1))
                        for t in range(TT):
                            for c in range(KC):
                                last = nc.tensor.matmul(ps_p[1][:, C * t:C * t + C], oT_sb[:, c, P * t:P * t + P],
                                                        wo_sb[:, c, :], start=(c == 0), stop=(c == KC - 1))
                        last.then_inc(y_ready, 1)
                    if q3.valid(STEPS):
                        pe.wait_ge(hT_done, done(st_of(b, q3)))
                        pe.wait_ge(lg_ready, freed(st_of(b, q3), 1))
                        for t in range(TT):
                            for c in range(KC):
                                last = nc.tensor.matmul(ps_p[3][:, E * t:E * t + E], hT_sb[:, c, P * t:P * t + P],
                                                        gw_sb[:, c, :], start=(c == 0), stop=(c == KC - 1))
                        last.then_inc(g_ready, 1)

                run_steps(pe, 0, STEPS + 2, LO, HI, phase2, settle)
                pe.wait_ge(lg_ready, done(b * STEPS + (STEPS - 1)))

                pe.wait_ge(r_chain, b * R_CHAIN + R_TOTALS)
                nc.tensor.matmul(ps_p[0][:, 0:E], upper[:, :], r_tot[:, :], start=True, stop=True)
                nc.tensor.matmul(ps_p[1][:, 0:E], ones[:, :], r_tot[:, :], start=True, stop=True).then_inc(r_pe, 1)
                pe.wait_ge(r_chain, (b + 1) * R_CHAIN)

            def transposes(n):
                pe.wait_ge(fn_ready, done(n))
                pe.wait_ge(fT_done, freed(n, 1))
                for c in range(KC):
                    for i in range(CT):
                        last = nc.tensor.transpose(ps_p[c][:, P * i:P * i + P], fn[:, i, P * c:P * c + P],
                                                   ident[:, :])
                last.then_inc(fT_ready, 1)

            transposes(0)
            with pe.Fori(0, E // 2) as pair:
                for par in range(2):
                    pe.wait_ge(w_load[par], pair * 64 + 64)
                    settle(pe)
                    with pe.Fori(0, CHUNKS) as j:
                        n = pair * (2 * CHUNKS) + (j + par * CHUNKS)
                        pe.wait_ge(fT_done, done(n))
                        for f in range(FB):
                            pe.wait_ge(relu_done, n * FB + (f + 1))
                            for c in range(KC):
                                last = nc.tensor.matmul(ps_s[:, f % 2, :], w1_sb[par][:, c, P * f:P * f + P],
                                                        fT_sb[:, c, :], start=(c == 0), stop=(c == KC - 1))
                            last.then_inc(h_ready, 1)
                        pe.wait_ge(y_taken, freed(n, 1))
                        for i in range(CT):
                            if i == 2:
                                transposes(n + 1)
                            for f in range(FB):
                                if i == 0:
                                    pe.wait_ge(relu_done, n * FB + (f + 1 + CREDIT))
                                last = nc.tensor.matmul(ps_t[:, C * i:C * i + C], hm_sb[:, f, P * i:P * i + P],
                                                        w2_sb[par][:, f, :], start=(f == 0), stop=(f == FB - 1))
                        last.then_inc(f_ready, 1)

        @block.scalar
        def _(act):
            for s_ in (xnT_sb_ready, q_sb, k_sb, vT_sb, e_ready, eT_sb, hT_done, fT_done, relu_done):
                act.sem_inc(s_, CREDIT)
            act.wait_ge(consts, 16 * CONST_DMAS)
            act.wait_ge(made, 5)
            act.wait_ge(bk_scaled, 1)

            def exps(g):
                act.wait_ge(sub_done, done(g))
                act.wait_ge(eT_ready, freed(g, 1))
                nc.scalar.activation(ex_sb[:, :, :], sc_sb[:, :, :], ACT.Exp).then_inc(e_ready, 1)

            def take_weights_T(g):
                act.wait_ge(eT_ready, done(g))
                act.wait_ge(o_ready, freed(g, 1))
                nc.scalar.activation(exT_sb[:, :, :].rearrange("p k q -> p (k q)"), ps_t[:, :], ACT.Copy
                                     ).then_inc(eT_sb, 1)

            with act.Fori(0, IMGS) as b:
                act.wait_ge(conv_done, b + 1)

                def phase1(s):
                    g = b * (2 * STEPS) + s.index
                    if s.plus(-1).valid(STEPS):
                        take_weights_T(g - 1)
                    if s.valid(STEPS):
                        act.wait_ge(vT_ready, done(st_of(b, s)))
                        rows = bass.ds(s.index * LINES + PAD, LINES)
                        nc.scalar.activation(v_pad[:, :, rows, PAD:PAD + W],
                                             ps_p[1][:, :].rearrange("p (c r w) -> p c r w", c=KC, w=W),
                                             ACT.Copy).then_inc(vT_sb, 1)
                    q = s.plus(1)
                    n = st_of(b, q)
                    if q.valid(STEPS):
                        act.wait_ge(xT_ready, done(n))
                        act.wait_ge(v_ready, freed(n, 1))
                        nc.scalar.activation(xnT[:, :, :].rearrange("p c t -> p (c t)"), ps_p[0][:, :], ACT.Copy
                                             ).then_inc(xnT_sb_ready, 1)
                    if s.valid(STEPS):
                        exps(g)
                    if q.valid(STEPS):
                        act.wait_ge(q_ready, done(n))
                        act.wait_ge(qk_stored[q.par], half_of(b, q) * 32 + 32)
                        act.wait_ge(s_ready, freed(b * (2 * STEPS) + q.index, 2))
                        for c in range(KC):
                            last = nc.scalar.activation(q_st[:, q.par, c, :], ps_p[1][:, ST * c:ST * c + ST],
                                                        ACT.Identity, bias=bq_sb[:, c:c + 1])
                        last.then_inc(q_sb, 1)
                        act.wait_ge(k_ready, done(n))
                        for c in range(KC):
                            last = nc.scalar.activation(k_st[:, q.par, c, :], ps_p[2][:, ST * c:ST * c + ST],
                                                        ACT.Identity, bias=bk_sb[:, c:c + 1], scale=SCALING)
                        last.then_inc(k_sb, 1)

                run_steps(act, -1, STEPS, LO, HI, phase1, settle)

                def phase2(s):
                    g = b * (2 * STEPS) + (s.index + STEPS)
                    if s.plus(-1).valid(STEPS):
                        take_weights_T(g - 1)
                    q = s.plus(-3)
                    if q.valid(STEPS):
                        act.wait_ge(hT_ready, done(st_of(b, q)))
                        act.wait_ge(g_ready, freed(st_of(b, q), 1))
                        nc.scalar.activation(hT_sb[:, :, :].rearrange("p c t -> p (c t)"), ps_p[2][:, :], ACT.Copy
                                             ).then_inc(hT_done, 1)
                    if s.valid(STEPS):
                        exps(g)

                run_steps(act, 0, STEPS + 2, LO, HI, phase2, settle)
                act.wait_ge(r_chain, b * R_CHAIN + 2)
                nc.scalar.activation(rp[:, :, :], rl[:, :, :], ACT.Exp).then_inc(r_exp, 1)

            def take_fT(n):
                act.wait_ge(fT_ready, done(n))
                for c in range(KC):
                    last = nc.scalar.activation(fT_sb[:, c, :], ps_p[c][:, :], ACT.Copy)
                last.then_inc(fT_done, 1)

            take_fT(0)
            with act.Fori(0, E // 2) as pair:
                for par in range(2):
                    act.wait_ge(w_load[par], pair * 64 + 64)
                    settle(act)
                    with act.Fori(0, CHUNKS) as j:
                        n = pair * (2 * CHUNKS) + (j + par * CHUNKS)
                        act.wait_ge(f_ready, freed(n, 1))
                        for f in range(FB):
                            act.wait_ge(h_ready, n * FB + (f + 1 + CREDIT))
                            nc.scalar.activation(hm_sb[:, f, :], ps_s[:, f % 2, :], ACT.Relu,
                                                 bias=b1_sb[par][:, f:f + 1]).then_inc(relu_done, 1)
                        take_fT(n + 1)

        @block.vector
        def _(dve):
            nc.disable_value_cache = True
            for s_ in (stat1, xn_ready, v_sb, sub_done, o_sb,
                       oT_done, x2_ready, stat2, hn_ready, lg_ready, fn_ready, y_taken, yo_ready, tok_taken):
                dve.sem_inc(s_, CREDIT)
            dve.sem_inc(conv_done, 1)
            nc.vector.memset(ones[:, :], 1.0).then_inc(made, 1)
            nc.vector.memset(r_run[:, :], 0.0)
            nc.vector.memset(half[:, :], -0.5)
            nc.vector.memset(r_reset[:, :, 1:RT], 1.0)
            nc.vector.memset(r_reset[:, :, 0], 0.0)
            nc.vector.memset(r_cum[:, :, 0], 0.0)
            nc.vector.memset(v_st[:, :, :, :, :], 1.0)
            nc.vector.memset(v1_st[:, :, :, :, :], 1.0)
            nc.vector.memset(v_pad[:, :, :, :], 0.0).then_inc(made, 1)
            dve.wait_ge(consts, 16 * CONST_DMAS)
            nc.vector.tensor_scalar(bk_sb[:, :], bk_sb[:, :], SCALING, None, ALU.mult).then_inc(bk_scaled, 1)
            dve.wait_ge(made, 5)
            dve.wait_ge(r_ready, 5)
            dve.wait_ge(table_cleared, 16 * CLEAR_DMAS)

            links = [0]

            def linked():
                links[0] += 1
                return links[0]

            def chain_restarts():
                if links[0]:
                    dve.wait_ge(chain, links[0])
                    dve.sem_clear(chain)
                links[0] = 0

            def soft1(g, m, taps):
                dve.wait_ge(s_ready, done(g))
                nc.vector.tensor_tensor(
                    sc_sb[:, :, :].rearrange("p (a r) k -> p a r k", r=LINES),
                    ps_s[:, :, :].rearrange("p i (c r k) -> p (i c) r k", c=KC, k=64),
                    masks[:, m, :, :].unsqueeze(2).broadcast_to([P, 4, LINES, 64]), ALU.add).then_inc(chain, 1)
                masked = linked()
                taps(1)
                dve.wait_ge(chain, masked)
                nc.vector.tensor_reduce(mx_sb[:, :], sc_sb[:, :, :], AX_X, ALU.max).then_inc(chain, 1)
                greatest = linked()
                taps(1)
                dve.wait_ge(chain, greatest)
                nc.vector.tensor_tensor(sc_sb[:, :, :], sc_sb[:, :, :],
                                        mx_sb[:, :].unsqueeze(2).broadcast_to([P, 16, 64]), ALU.subtract
                                        ).then_inc(sub_done, 1)

            def normalised(g, dst, taps):
                dve.wait_ge(o_ready, done(g))
                nc.vector.reciprocal(rec_sb[:, :].rearrange("p (t n) -> p t n", t=TT), ps_o[:, :, :, KEY_DIM]
                                     ).then_inc(chain, 1)
                inverted = linked()
                taps(1)
                dve.wait_ge(chain, inverted)
                nc.vector.tensor_tensor(
                    dst, ps_o[:, :, :, 0:KEY_DIM],
                    rec_sb[:, :].rearrange("p (t n) -> p t n", t=TT).unsqueeze(3).broadcast_to(
                        [P, TT, HEADS, KEY_DIM]), ALU.mult).then_inc(o_sb, 1)

            def convolution(c, window, out_view, first, count):
                at = [first, 0]

                def taps(k):
                    for tap in range(at[0], min(at[0] + k, first + count)):
                        src = v_pad[:, c, window(tap // 5, tap % 5)[0], window(tap // 5, tap % 5)[1]]
                        if at[1]:
                            dve.wait_ge(chain, at[1])
                        if tap == 0:
                            nc.vector.tensor_scalar(out_view, src, wl_sb[:, c, 0:1], bl_sb[:, c:c + 1],
                                                    ALU.mult, ALU.add).then_inc(chain, 1)
                        else:
                            nc.vector.scalar_tensor_tensor(out_view, src, wl_sb[:, c, tap:tap + 1], out_view,
                                                           ALU.mult, ALU.add).then_inc(chain, 1)
                        at[:] = tap + 1, linked()

                return taps

            def no_taps(k):
                pass

            def stats(src, sp_, tiles, out_sem, taps):
                for t in range(tiles):
                    last = nc.vector.bn_stats(stat[:, sp_, t, :], src[:, t, :])
                last.then_inc(chain, 1)
                counted = linked()
                taps(1)
                dve.wait_ge(chain, counted)
                for t in range(tiles):
                    last = nc.vector.bn_aggr(mv[:, sp_, t, :], stat[:, sp_, t, :])
                last.then_inc(out_sem, 1)

            def centred(dst, src, sp_, tiles, ready):
                for t in range(tiles):
                    last = nc.vector.tensor_scalar(dst[:, t, :], src[:, t, :], mv[:, sp_, t, 0:1],
                                                   rstd[:, sp_, t:t + 1], ALU.subtract, ALU.mult)
                last.then_inc(ready, 1)

            def route(b):
                count = [0]

                def link(ins):
                    count[0] += 1
                    ins.then_inc(r_chain, 1)
                    dve.wait_ge(r_chain, b * R_CHAIN + count[0])

                v = nc.vector
                over_e = [P, RT, E]
                by_expert = "p t e -> p e t"
                dve.wait_ge(rl_load, b * 16 + 16)
                link(v.tensor_reduce(r_mx[:, :], rl[:, :, :], AX_X, ALU.max))
                link(v.tensor_tensor(rl[:, :, :], rl[:, :, :], r_mx[:, :].unsqueeze(2).broadcast_to(over_e),
                                     ALU.subtract))
                dve.wait_ge(r_exp, b + 1)
                link(v.tensor_reduce(r_sum[:, :], rp[:, :, :], AX_X, ALU.add))
                link(v.reciprocal(r_sum[:, :], r_sum[:, :]))
                link(v.tensor_tensor(rp[:, :, :], rp[:, :, :], r_sum[:, :].unsqueeze(2).broadcast_to(over_e),
                                     ALU.mult))
                link(v.tensor_reduce(r_mx[:, :], rp[:, :, :], AX_X, ALU.max))
                link(v.tensor_tensor(r_eq[:, :, :], rp[:, :, :], r_mx[:, :].unsqueeze(2).broadcast_to(over_e),
                                     ALU.is_equal))
                for e in range(1, E):
                    link(v.tensor_tensor(r_cum[:, :, e], r_cum[:, :, e - 1], r_eq[:, :, e - 1], ALU.add))
                link(v.scalar_tensor_tensor(r_oh[:, :, :], r_cum[:, :, :].rearrange(by_expert), 0.0,
                                            r_eq[:, :, :].rearrange(by_expert), ALU.is_equal, ALU.mult))
                flat = "p e t -> p (e t)"
                link(v.tensor_tensor_scan(r_pos[:, :, :].rearrange(flat), r_reset[:, :, :].rearrange(flat),
                                          r_oh[:, :, :].rearrange(flat), 0.0, ALU.mult, ALU.add))
                link(v.tensor_copy(r_tot[:, :], r_pos[:, :, RT - 1]))
                assert count[0] == R_TOTALS
                dve.wait_ge(r_pe, b + 1)
                link(v.tensor_tensor(r_base[:, :], ps_p[0][:, 0:E], r_run[:, :], ALU.add))
                link(v.tensor_tensor(r_run[:, :], ps_p[1][:, 0:E], r_run[:, :], ALU.add))
                link(v.tensor_tensor(r_pos[:, :, :], r_pos[:, :, :],
                                     r_base[:, :].unsqueeze(2).broadcast_to([P, E, RT]), ALU.add))
                link(v.tensor_scalar(r_big[:, :, :], r_pos[:, :, :], float(CAP), float(NO_TOKEN),
                                     ALU.is_gt, ALU.mult))
                link(v.tensor_tensor(r_pos[:, :, :], r_pos[:, :, :],
                                     r_first[:, :].unsqueeze(2).broadcast_to([P, E, RT]), ALU.add))
                link(v.tensor_tensor(r_pos[:, :, :], r_pos[:, :, :], r_big[:, :, :], ALU.add))
                link(v.tensor_tensor(r_pos[:, :, :], r_pos[:, :, :], r_oh[:, :, :], ALU.mult))
                link(v.tensor_reduce(r_slot[:, :], r_pos[:, :, :].rearrange("p e t -> p t e"), AX_X, ALU.add))
                dve.wait_ge(r_free, b + 1)
                link(v.tensor_scalar(r_slot_i[:, :], r_slot[:, :], -1.0, None, ALU.add))
                link(v.tensor_copy(r_pair[:, :, 0], r_tok[:, :]))
                link(v.tensor_copy(r_pair[:, :, 1:2].bitcast(F32), r_mx[:, :].unsqueeze(2)))
                link(v.tensor_scalar(r_tok[:, :], r_tok[:, :], float(IMG_TOK), None, ALU.add))
                assert count[0] == R_CHAIN

            PAIRS = STEPS // 2
            with dve.Fori(0, IMGS) as b:
                def phase1(s):
                    g = b * (2 * STEPS) + s.index
                    taps = no_taps
                    j = s.half - 1
                    if 0 <= j < PAIRS:
                        if s.par == 0:
                            dve.wait_ge(vT_sb, done(b * STEPS + min(2 * s.half, STEPS - 1)))
                        taps = convolution(
                            0, lambda kh, kw: (slice(2 * LINES * j + kh, 2 * LINES * (j + 1) + kh), slice(kw, kw + W)),
                            lepe[:, 0, 2 * LINES * j:2 * LINES * (j + 1), :], (0, 13)[s.par], (13, 12)[s.par])
                    if s.valid(STEPS):
                        soft1(g, 0, taps)
                    taps(2)
                    q = s.plus(-1)
                    if q.valid(STEPS):
                        dve.wait_ge(v1_stored[q.par], half_of(b, q) * 16 + 16)
                        normalised(g - 1, v1_st[:, q.par, :, 0:KEY_DIM, :].rearrange("p t d n -> p t n d"), taps)
                    q = s.plus(2)
                    n = st_of(b, q)
                    if q.valid(STEPS):
                        dve.wait_ge(x_load[q.par], half_of(b, q) * 16 + 16)
                        stats(x_in[:, q.par], 0, TT, stat1, taps)
                        taps(2)
                    taps(2)
                    q = s.plus(1)
                    n = st_of(b, q)
                    if q.valid(STEPS):
                        dve.wait_ge(v_ready, done(n))
                        nc.vector.tensor_tensor(
                            v_st[:, q.par, :, 0:KEY_DIM, :].rearrange("p t d n -> p t (d n)"),
                            ps_p[3][:, :].rearrange("p (t c) -> p t c", t=TT),
                            bv_sb[:, :].unsqueeze(1).broadcast_to([P, TT, C]), ALU.add).then_inc(v_sb, 1)
                    q = s.plus(2)
                    n = st_of(b, q)
                    if q.valid(STEPS):
                        dve.wait_ge(rstd1, n + 1)
                        centred(xn[:, q.par], x_in[:, q.par], 0, TT, xn_ready)
                    taps(TAPS)
                    chain_restarts()

                for s in range(-2, STEPS + 2):
                    phase1(Step(s // 2, s % 2, False))

                def phase2(s):
                    g = b * (2 * STEPS) + (s.index + STEPS)
                    taps = no_taps
                    j = s.half + s.par
                    if 0 <= j < PAIRS:
                        taps = convolution(
                            1, lambda kh, kw: (slice(kh, kh + H), slice(2 * LINES * j + kw, 2 * LINES * (j + 1) + kw)),
                            lepe[:, 1, :, 2 * LINES * j:2 * LINES * (j + 1)], (13, 0)[s.par], (12, 13)[s.par])
                    if s.valid(STEPS):
                        soft1(g, 1, taps)
                    taps(1)
                    q = s.plus(-2)
                    n = st_of(b, q)
                    if q.valid(STEPS):
                        dve.wait_ge(oT_ready, done(n))
                        cols = slice(q.index * LINES, q.index * LINES + LINES)
                        for c in range(KC):
                            last = nc.vector.tensor_tensor(
                                oT_sb[:, c, :].rearrange("p (w h) -> p w h", h=H),
                                ps_p[0][:, ST * c:ST * c + ST].rearrange("p (w h) -> p w h", h=H),
                                lepe[:, c, :, cols].rearrange("p h w -> p w h"), ALU.add)
                        last.then_inc(oT_done, 1)
                    taps(3)
                    q = s.plus(-1)
                    if q.valid(STEPS):
                        normalised(g - 1, o2[:, q.par].rearrange("p t (d n) -> p t n d", n=HEADS), taps)
                    q = s.plus(-2)
                    if q.valid(STEPS):
                        dve.wait_ge(xb_ready, n + 1)
                        dve.wait_ge(x2_stored[q.par], half_of(b, q) * 64 + 64)
                        dve.wait_ge(y_ready, done(n))
                        nc.vector.tensor_tensor(x2_st[:, q.par].rearrange("p t c -> p (t c)"), ps_p[1][:, :],
                                                x_r[:, q.par].rearrange("p t c -> p (t c)"), ALU.add
                                                ).then_inc(x2_ready, 1)
                        taps(1)
                        dve.wait_ge(x2_ready, done(n))
                        stats(x2_st[:, q.par], 1, TT, stat2, taps)
                        taps(2)
                    q = s.plus(-3)
                    if q.valid(STEPS):
                        dve.wait_ge(g_ready, done(n - 1))
                        dve.wait_ge(lg_stored[q.par], half_of(b, q) * 32 + 32)
                        nc.vector.tensor_tensor(
                            lg_st[:, q.par], ps_p[3][:, 0:TT * E].rearrange("p (t e) -> p t e", t=TT),
                            gb_sb[:, :].unsqueeze(1).broadcast_to([P, TT, E]), ALU.add).then_inc(lg_ready, 1)
                    q = s.plus(-2)
                    if q.valid(STEPS):
                        dve.wait_ge(rstd2, n + 1)
                        centred(hn[:, q.par], x2_st[:, q.par], 1, TT, hn_ready)
                    taps(TAPS)
                    chain_restarts()
                    if s.index == 2 * PAIRS - 2:
                        dve.sem_inc(conv_done, 1)

                for s in range(-1, STEPS + 3):
                    phase2(Step(s // 2, s % 2, False))
                route(b)

            def prepare(n, par):
                dve.wait_ge(gathered[par], n[1] * (16 * CT) + 16 * CT)
                n = n[0]
                stats(xg[par], 0, CT, f_aggr, no_taps)
                dve.wait_ge(f_rstd, n + 1)
                dve.wait_ge(fT_ready, freed(n, 1))
                centred(fn, xg[par], 0, CT, fn_ready)

            prepare((0, 0), 0)
            chain_restarts()
            with dve.Fori(0, E // 2) as pair:
                for epar in range(2):
                    dve.wait_ge(w_load[epar], pair * 64 + 64)
                    settle(dve)
                    with dve.Fori(0, CHUNKS // 2) as jj:
                        for par in range(2):
                            h = pair * CHUNKS + (jj + epar * (CHUNKS // 2))
                            n = h * 2 + par
                            prepare((n + 1, h + par), 1 - par)
                            dve.wait_ge(yo_free, freed(n, 2))
                            nc.vector.tensor_copy(tok_s[:, par], tok_g[:, par, :, 0])
                            nc.vector.tensor_copy(prob_s[:, par].unsqueeze(2), tok_g[:, par, :, 1:2].bitcast(F32)
                                                  ).then_inc(tok_taken, 1)
                            dve.wait_ge(f_ready, done(n))
                            nc.vector.tensor_tensor(
                                y_sb, ps_t[:, :].rearrange("p (i c) -> p i c", i=CT),
                                b2_sb[epar].unsqueeze(1).broadcast_to([P, CT, C]), ALU.add).then_inc(y_taken, 1)
                            dve.wait_ge(y_taken, done(n))
                            dve.wait_ge(tok_taken, done(n))
                            prob = prob_s[:, par].unsqueeze(2).broadcast_to([P, CT, C])

                            def link(ins):
                                ins.then_inc(chain, 1)
                                dve.wait_ge(chain, linked())

                            link(nc.vector.tensor_tensor(y_sb, y_sb, prob, ALU.mult))
                            link(nc.vector.tensor_scalar(r_sb, y_sb, -1e4, 1e4, ALU.max, ALU.min))
                            link(nc.vector.tensor_tensor(m_sb, y_sb, y_sb, ALU.is_equal))
                            link(nc.vector.tensor_tensor(r_sb, r_sb, m_sb, ALU.mult))
                            link(nc.vector.tensor_scalar(m_sb, y_sb, 0.0, 0.0, ALU.mult, ALU.is_equal))
                            settle(dve)
                            link(nc.vector.copy_predicated(r_sb, m_sb.bitcast(U32), y_sb))
                            nc.vector.tensor_tensor(yo[par], r_sb, xg[par], ALU.add).then_inc(yo_ready, 1)
                            chain_restarts()

        @block.gpsimd
        def _(pool):
            pool.sem_inc(staged, CREDIT)
            pool.sem_inc(yo_free, CREDIT)
            pool.sem_inc(r_free, 1)
            nc.gpsimd.memset(ident[:, :], 0.0).then_inc(made, 1)
            nc.gpsimd.iota(r_pair[:, :, :], pattern=[[0, 2 * RT]], base=NO_TOKEN, channel_multiplier=0
                           ).then_inc(r_ready, 1)
            pool.wait_ge(made, 3)
            nc.gpsimd.affine_select(out=ident[:, :], in_=ident[:, :], compare_op=ALU.not_equal, fill=1.0,
                                    base=0, pattern=[[-1, P]], channel_multiplier=1).then_inc(made, 1)
            nc.gpsimd.affine_select(out=upper[:, :], in_=ones[:, :], compare_op=ALU.is_gt, fill=0.0,
                                    base=0, pattern=[[1, P]], channel_multiplier=-1).then_inc(made, 1)
            nc.gpsimd.iota(r_slot_i[:, :], pattern=[[1, RT]], base=0, channel_multiplier=RT).then_inc(r_ready, 1)
            nc.gpsimd.iota(tok_g[:, 0, 0:CT, 0:2], pattern=[[CAP, E]], base=0, channel_multiplier=0
                           ).then_inc(r_ready, 1)
            pool.wait_ge(r_ready, 3)
            nc.gpsimd.tensor_copy(r_tok[:, :], r_slot_i[:, :]).then_inc(r_ready, 1)
            nc.gpsimd.tensor_copy(r_first[:, :], tok_g[:, 0, 0:CT, 0:2].rearrange("p a b -> p (a b)")
                                  ).then_inc(r_ready, 1)
            rows = (SLOTS + 2 * CHUNK) // P
            for top in range(0, rows, RT):
                k = min(RT, rows - top)
                pool.dma_start(slot_t[P * top:P * (top + k), :].rearrange("(p k) c -> p k c", p=P),
                               r_pair[:, 0:k, :]).then_inc(table_cleared, 16)
            pool.wait_ge(table_cleared, 16 * CLEAR_DMAS)
            pool.wait_ge(consts, 16 * CONST_DMAS)

            def inverse_deviation(k, tiles, seen, n, eps, eps_sem, out_sem):
                pool.wait_ge(seen, done(n))
                settle(pool)
                nc.gpsimd.tensor_scalar(veps[:, k, 0:tiles], mv[:, k, 0:tiles, 1], eps, None, ALU.add
                                        ).then_inc(eps_sem, 1)
                pool.wait_ge(eps_sem, n + 1)
                nc.gpsimd.tensor_tensor(rstd[:, k, 0:tiles], veps[:, k, 0:tiles], half[:, 0:tiles], ALU.pow
                                        ).then_inc(out_sem, 1)

            with pool.Fori(0, IMGS) as b:
                def phase1(s):
                    q = s.plus(2)
                    if q.valid(STEPS):
                        inverse_deviation(0, TT, stat1, st_of(b, q), 1e-6, eps1, rstd1)

                run_steps(pool, -2, STEPS - 3, LO, HI, phase1, settle)
                for n in range(2):
                    pool.wait_ge(qk_stored[n], b * (16 * STEPS) + (16 * STEPS + 32))
                    settle(pool)

                def phase2(s):
                    q = s.plus(1)
                    if q.valid(STEPS):
                        pool.wait_ge(s_ready, freed(b * (2 * STEPS) + (q.index + STEPS), 2))
                        settle(pool)
                        cols = bass.ds(q.index * LINES, LINES)
                        for dst, src in ((q_st, q_img), (k_st, k_img)):
                            nc.gpsimd.tensor_copy(
                                dst[:, q.par].rearrange("p c (w h) -> p c w h", h=H),
                                src[:, :, :].rearrange("p c (h w) -> p c w h", w=W)[:, :, cols, :]
                            ).then_inc(staged, 1)
                    q = s.plus(-2)
                    if q.valid(STEPS):
                        inverse_deviation(1, TT, stat2, st_of(b, q), 1e-5, eps2, rstd2)
                    if s.valid(STEPS):
                        pool.wait_ge(xr_load[s.par], half_of(b, s) * 32 + 32)
                        nc.gpsimd.tensor_tensor(x_r[:, s.par], x_r[:, s.par],
                                                bo_sb[:, :].unsqueeze(1).broadcast_to([P, TT, C]), ALU.add
                                                ).then_inc(xb_ready, 1)

                run_steps(pool, -1, STEPS + 1, LO, HI, phase2, settle)
                pool.wait_ge(r_chain, (b + 1) * R_CHAIN)
                settle(pool)
                for t in range(RT):
                    nc.gpsimd.indirect_dma_start(
                        out=slot_t, out_offset=bass.IndirectOffsetOnAxis(ap=r_slot_i[:, t:t + 1], axis=0),
                        in_=r_pair[:, t, :], in_offset=None, bounds_check=SLOTS - 1, oob_is_err=False
                    ).then_inc(r_scattered, 16)
                pool.wait_ge(r_scattered, b * (16 * RT) + 16 * RT)
                pool.sem_inc(r_free, 1)

            for n in range(2):
                pool.wait_ge(x2_stored[n], 32 * IMGS * STEPS + 64)
                settle(pool)

            def gather(h, par):
                pool.wait_ge(tok_load[par], h * 16 + 16)
                settle(pool)
                for i in range(CT):
                    nc.gpsimd.indirect_dma_start(
                        out=xg[par][:, i, :], out_offset=None, in_=x2_t,
                        in_offset=bass.IndirectOffsetOnAxis(ap=tok_g[:, par, i, 0:1], axis=0),
                        bounds_check=TOK - 1, oob_is_err=False).then_inc(gathered[par], 16)

            def scatter(h, par):
                for i in range(CT):
                    nc.gpsimd.indirect_dma_start(
                        out=out_t, out_offset=bass.IndirectOffsetOnAxis(ap=tok_s[:, par, i:i + 1], axis=0),
                        in_=yo[par][:, i, :], in_offset=None, bounds_check=TOK - 1, oob_is_err=False
                    ).then_inc(scattered[par], 16)

            def scatter_landed(h, par):
                pool.wait_ge(scattered[par], h * (16 * CT) + 16 * CT)
                pool.sem_inc(yo_free, 1)

            def inverse_deviations(n):
                pool.wait_ge(f_aggr, n + 1)
                settle(pool)
                nc.gpsimd.tensor_scalar(veps[:, 0, :], mv[:, 0, :, 1], 1e-5, None, ALU.add).then_inc(f_eps, 1)
                pool.wait_ge(f_eps, n + 1)
                nc.gpsimd.tensor_tensor(rstd[:, 0, :], veps[:, 0, :], half[:, :], ALU.pow).then_inc(f_rstd, 1)

            for par in range(2):
                gather(0, par)
            for n in range(2):
                inverse_deviations(n)

            def turn(h, par):
                pool.wait_ge(yo_ready, done(h * 2 + par))
                settle(pool)
                gather(h + 1, par)
                scatter(h, par)

            with pool.Fori(0, E * CHUNKS // 2 - 1) as h:
                for par in range(2):
                    turn(h, par)
                    inverse_deviations(h * 2 + (par + 2))
                    scatter_landed(h, par)
            h = E * CHUNKS // 2 - 1
            turn(h, 0)
            inverse_deviations(2 * h + 2)
            scatter_landed(h, 0)
            pool.wait_ge(yo_ready, done(h * 2 + 1))
            scatter(h, 1)
            scatter_landed(h, 1)


_INS = ["x", "mask_h", "mask_w", "wqT", "bq", "wkT", "bk", "wvT", "bv", "wlepe", "blepe", "woT", "bo",
        "gate_w", "gate_b", "w1", "b1", "w2", "b2"]


def kernel(x, L0_conv_mask_h, L0_conv_mask_w, L0_conv_Wq, L0_conv_bq, L0_conv_Wk, L0_conv_bk, L0_conv_Wv,
           L0_conv_bv, L0_conv_Wlepe, L0_conv_blepe, L0_conv_Wo, L0_conv_bo, L0_ffn_gate_w, L0_ffn_gate_b,
           L0_ffn_w1, L0_ffn_b1, L0_ffn_w2, L0_ffn_b2):
    import concourse.bacc as bacc
    from concourse.bass_utils import run_bass_kernel_spmd

    def rows(a):
        return np.ascontiguousarray(a)

    channels = np.shape(x)[-1]
    experts, width = np.shape(L0_ffn_b1)

    def by_value(a):
        split = np.reshape(a, np.shape(a)[:-1] + (HEADS, KEY_DIM))
        return np.ascontiguousarray(np.reshape(np.swapaxes(split, -1, -2), np.shape(a)))

    data = {
        "x": rows(x), "mask_h": rows(L0_conv_mask_h), "mask_w": rows(L0_conv_mask_w),
        "wqT": rows(np.transpose(L0_conv_Wq)), "bq": rows(L0_conv_bq),
        "wkT": rows(np.transpose(L0_conv_Wk)), "bk": rows(L0_conv_bk),
        "wvT": by_value(np.transpose(L0_conv_Wv)), "bv": by_value(L0_conv_bv),
        "wlepe": rows(np.transpose(by_value(np.reshape(L0_conv_Wlepe, (TAPS, channels))))),
        "blepe": by_value(L0_conv_blepe),
        "woT": rows(np.transpose(by_value(L0_conv_Wo))), "bo": rows(L0_conv_bo),
        "gate_w": rows(L0_ffn_gate_w), "gate_b": rows(L0_ffn_gate_b),
        "w1": rows(L0_ffn_w1),
        "b1": rows(np.reshape(np.transpose(np.reshape(L0_ffn_b1, (experts, width // P, P)), (2, 0, 1)), (P, -1))),
        "w2": rows(L0_ffn_w2), "b2": rows(L0_ffn_b2),
    }
    nc = bacc.Bacc("TRN2", target_bir_lowering=False, num_devices=1)
    arrays, args = {}, []
    for name in _INS:
        a = data[name]
        arrays[f"in_{name}"] = a
        args.append(nc.dram_tensor(f"in_{name}", a.shape, mybir.dt.from_np(a.dtype), kind="ExternalInput").ap())
    out = nc.dram_tensor("out_0", data["x"].shape, F32, kind="ExternalOutput").ap()
    metaformer_kernel(nc, *args, out)
    result = run_bass_kernel_spmd(nc, [arrays], core_ids=[0])
    return result.results[0]["out_0"]
```

```python
import math
from contextlib import ExitStack

import numpy as np
import concourse.bass as bass
from concourse import mybir
from concourse.alu_op_type import AluOpType as ALU

F32 = mybir.dt.float32
F32R = mybir.dt.float32r
I32 = mybir.dt.int32
U32 = mybir.dt.uint32
ACT = mybir.ActivationFunctionType
AX_X = mybir.AxisListType.X

P = 128
HEADS = 8
KEY_DIM = 32
VCOLS = KEY_DIM + 1
LINES = 4
PAD = 2
TAPS = 25
CREDIT = 2
CHUNK = 512
RING = 4
NO_TOKEN = 1 << 20


class Step:

    def __init__(self, half, par, inside):
        self.half, self.par, self.inside = half, par, inside

    def plus(self, off):
        total = self.par + off
        return Step(self.half + total // 2, total % 2, self.inside)

    @property
    def index(self):
        return self.half * 2 + self.par

    def valid(self, count):
        return self.inside or 0 <= self.index < count


def run_steps(eng, first, last, lo, hi, emit, before_loop):
    for s in range(first, lo):
        emit(Step(s // 2, s % 2, False))
    before_loop(eng)
    with eng.Fori(lo // 2, hi // 2) as half:
        for par in range(2):
            emit(Step(half, par, True))
    for s in range(hi, last + 1):
        emit(Step(s // 2, s % 2, False))


def done(n):
    return n + (1 + CREDIT)


def freed(n, buffers):
    return n + (1 + CREDIT - buffers)


def metaformer_kernel(nc, x, mask_h, mask_w, wqT, bq, wkT, bk, wvT, bv, wlepe, blepe, woT, bo,
                      gate_w, gate_b, w1, b1, w2, b2, out):
    IMGS, H, W, C = x.shape
    E, _, F = w1.shape
    TOK = IMGS * H * W
    IMG_TOK = H * W
    KC = C // P
    DC = P // HEADS
    STEPS = H // LINES
    ST = LINES * W
    TT = ST // P
    CAP = math.ceil(1.25 * TOK / E)
    CHUNKS = CAP // CHUNK
    SLOTS = E * CAP
    FB = F // P
    CT = CHUNK // P
    PW = W + 2 * PAD
    VROW = HEADS * VCOLS
    RT = IMG_TOK // P
    SCALING = float(KEY_DIM) ** -0.5
    assert H == W == 64 and C == 256 and CAP % CHUNK == 0 and 2 * CHUNKS % RING == 0 and E % 2 == 0
    LO, HI = 4, 12

    x_t = x.rearrange("b h w c -> (b h w) c")
    out_t = out.rearrange("b h w c -> (b h w) c")
    v1_t = nc.dram_tensor("v1_rows", [TOK, VROW], F32).ap()
    x2_t = nc.dram_tensor("x2_rows", [TOK, C], F32).ap()
    lg_t = nc.dram_tensor("gate_logits", [TOK, E], F32).ap()
    slot_t = nc.dram_tensor("slot_table", [SLOTS + RING * CHUNK, 2], I32).ap()

    with ExitStack() as ctx:
        def sb(name, shape, dt=F32):
            return ctx.enter_context(nc.sbuf_tensor(name, shape, dt))

        def sem(name):
            return ctx.enter_context(nc.semaphore(name))

        ident = sb("ident", [P, P])
        stat = sb("stat", [P, 2, 4, 6])
        mv = sb("mv", [P, 2, 4, 2])
        veps = sb("veps", [P, 2, 4])
        rstd = sb("rstd", [P, 2, 4])
        half = sb("half", [P, 4])
        tok_g = sb("tok_g", [P, RING, CT, 2], I32)
        tok_s = sb("tok_s", [P, 2, CT], I32)
        prob_s = sb("prob_s", [P, 2, CT])
        rl = sb("rl", [P, RT, E])
        rp = sb("rp", [P, RT, E])
        r_eq = sb("r_eq", [P, RT, E])
        r_cum = sb("r_cum", [P, RT, E])
        r_oh = sb("r_oh", [P, E, RT])
        r_pos = sb("r_pos", [P, E, RT])
        r_big = sb("r_big", [P, E, RT])
        r_mx = sb("r_mx", [P, RT])
        r_sum = sb("r_sum", [P, RT])
        r_slot = sb("r_slot", [P, RT])
        r_slot_i = sb("r_slot_i", [P, RT], I32)
        r_tok = sb("r_tok", [P, RT])
        r_pair = sb("r_pair", [P, RT, 2], I32)
        r_reset = sb("r_reset", [P, E, RT])
        r_run = sb("r_run", [P, E])
        r_tot = sb("r_tot", [P, E])
        r_base = sb("r_base", [P, E])
        r_first = sb("r_first", [P, E])
        with ExitStack() as attention:
            def sba(name, shape, dt=F32):
                return attention.enter_context(nc.sbuf_tensor(name, shape, dt))

            q_img = sba("q_img", [P, KC, IMG_TOK])
            k_img = sba("k_img", [P, KC, IMG_TOK])
            v_pad = sba("v_pad", [P, KC, H + 2 * PAD, PW])
            lepe = sba("lepe", [P, KC, H, W])
            q_st = sba("q_st", [P, 2, KC, ST])
            k_st = sba("k_st", [P, 2, KC, ST])
            v_st = sba("v_st", [P, 2, TT, VCOLS, HEADS])
            sc_sb = sba("sc_sb", [P, 4 * LINES, 64])
            ex_sb = sba("ex_sb", [P, 4 * LINES, 64])
            exT_sb = sba("exT_sb", [P, 8, P])
            mx_sb = sba("mx_sb", [P, 16])
            rec_sb = sba("rec_sb", [P, 16])
            v1_st = sba("v1_st", [P, 2, TT, VCOLS, HEADS])
            x_in = sba("x_in", [P, 2, TT, C])
            xn = sba("xn", [P, 2, TT, C])
            xnT = sba("xnT", [P, KC, ST])
            oT_sb = sba("oT_sb", [P, KC, ST])
            o2 = sba("o2", [P, 2, TT, C])
            x_r, hn = x_in, xn
            x2_st = sba("x2_st", [P, 2, TT, C])
            hT_sb = sba("hT_sb", [P, KC, ST])
            lg_st = sba("lg_st", [P, 2, TT, E])
            masks = sba("masks", [P, 2, 4, 64])
            wq_sb, wk_sb, wv_sb, wo_sb = (sba(n, [P, KC, C]) for n in ("wq_sb", "wk_sb", "wv_sb", "wo_sb"))
            gw_sb = sba("gw_sb", [P, KC, E])
            gb_sb = sba("gb_sb", [P, E])
            bq_sb = sba("bq_sb", [P, KC])
            bk_sb = sba("bk_sb", [P, KC])
            bv_sb = sba("bv_sb", [P, C])
            bo_sb = sba("bo_sb", [P, C])
            wl_sb = sba("wl_sb", [P, KC, TAPS])
            bl_sb = sba("bl_sb", [P, KC])
            upper = sba("upper", [P, P])
            ones = sba("ones", [P, P])
        w1_raw, w2_raw = sb("w1_raw", [P, KC, F]), sb("w2_raw", [P, FB, C])
        w1_hl = [[sb(f"w1_{part}{n}", [P, KC, F], F32R) for part in ("high", "low")] for n in range(2)]
        w2_hl = [[sb(f"w2_{part}{n}", [P, FB, C], F32R) for part in ("high", "low")] for n in range(2)]
        b1_sb = [sb(f"b1_{n}", [P, FB]) for n in range(2)]
        b2_sb = [sb(f"b2_{n}", [P, C]) for n in range(2)]
        xg = [sb(f"xg{n}", [P, CT, C]) for n in range(RING)]
        fn = sb("fn", [P, CT, C])
        fT_high, fT_low = sb("fT_high", [P, KC, CHUNK], F32R), sb("fT_low", [P, KC, CHUNK], F32R)
        h_raw = sb("h_raw", [P, FB, CHUNK])
        h_high, h_low = sb("h_high", [P, FB, CHUNK], F32R), sb("h_low", [P, FB, CHUNK], F32R)
        y_sb, r_sb, m_sb = (sb(n, [P, CT, C]) for n in ("y_sb", "r_sb", "m_sb"))
        yo = [sb(f"yo{n}", [P, CT, C]) for n in range(2)]

        ps_s = ctx.enter_context(nc.psum_tensor("ps_s", [P, 2, 512], F32))
        ps_t = ctx.enter_context(nc.psum_tensor("ps_t", [P, 1024], F32))
        ps_p = [ctx.enter_context(nc.psum_tensor(f"ps_p{n}", [P, 512], F32)) for n in range(4)]
        ps_o = ps_t[:, :].rearrange("p (t n) -> p t n", t=TT)[:, :, 0:VROW].rearrange(
            "p t (n d) -> p t n d", n=HEADS)

        consts = sem("consts_loaded")
        made = sem("constants_made")
        bk_scaled = sem("bk_scaled")
        x_load = [sem(f"x_load{n}") for n in range(2)]
        qk_stored = [sem(f"qk_stored{n}") for n in range(2)]
        v1_stored = [sem(f"v1_stored{n}") for n in range(2)]
        v_load = [sem(f"v_load{n}") for n in range(2)]
        xr_load = [sem(f"xr_load{n}") for n in range(2)]
        x2_stored = [sem(f"x2_stored{n}") for n in range(2)]
        lg_stored = [sem(f"lg_stored{n}") for n in range(2)]
        stat1, eps1, rstd1, xn_ready = sem("stat1"), sem("eps1"), sem("rstd1"), sem("xn_ready")
        xT_ready, xnT_sb_ready = sem("xT_ready"), sem("xnT_sb_ready")
        q_ready, k_ready, v_ready = sem("q_ready"), sem("k_ready"), sem("v_ready")
        q_sb, k_sb, v_sb = sem("q_sb"), sem("k_sb"), sem("v_sb")
        vT_ready, vT_sb = sem("vT_ready"), sem("vT_sb")
        conv_done = sem("conv_done")
        chain = sem("vector_chain")
        s_ready, mx_done = sem("s_ready"), sem("mx_done")
        e_ready, eT_ready, eT_sb = sem("e_ready"), sem("eT_ready"), sem("eT_sb")
        o_ready, o_sb = sem("o_ready"), sem("o_sb")
        staged, xb_ready = sem("staged"), sem("xb_ready")
        oT_ready, oT_done, y_ready, x2_ready = sem("oT_ready"), sem("oT_done"), sem("y_ready"), sem("x2_ready")
        stat2, eps2, rstd2, hn_ready = sem("stat2"), sem("eps2"), sem("rstd2"), sem("hn_ready")
        hT_ready, hT_done, g_ready, lg_ready = sem("hT_ready"), sem("hT_done"), sem("g_ready"), sem("lg_ready")
        passed = sem("passed")
        table_cleared = sem("table_cleared")
        r_free = sem("r_free")
        rl_load, r_shifted, r_exp, r_totals, r_pe, r_sums_taken, r_slots_ready, r_ready, r_scattered = (
            sem(n) for n in ("rl_load", "r_shifted", "r_exp", "r_totals", "r_pe", "r_sums_taken",
                             "r_slots_ready", "r_ready", "r_scattered"))
        attention_over, xg_cleared = sem("attention_over"), sem("xg_cleared")
        w_load, w_high_done, w_split = sem("w_load"), sem("w_high_done"), sem("w_split")
        b_load = [sem(f"b_load{n}") for n in range(2)]
        tok_load = [sem(f"tok_load{n}") for n in range(RING)]
        gathered = [sem(f"gathered{n}") for n in range(RING)]
        fT_high_done, h_high_done, h_low_done = sem("fT_high_done"), sem("h_high_done"), sem("h_low_done")
        scattered = [sem(f"scattered{n}") for n in range(2)]
        f_aggr, f_eps, f_rstd, fn_ready = (sem(n) for n in ("f_aggr", "f_eps", "f_rstd", "fn_ready"))
        tok_taken, yo_free = sem("tok_taken"), sem("yo_free")
        fT_ready, fT_done, h_ready, relu_done, f_ready, y_taken, yo_ready = (
            sem(n) for n in ("fT_ready", "fT_done", "h_ready", "relu_done", "f_ready", "y_taken", "yo_ready"))

        CONST_DMAS = 5 + 3 + 3 + 1 + 8
        SCATTER_STEPS = (2, 3, 12, 13, 14, 15, 16, 17)
        CLEAR_DMAS = math.ceil((SLOTS + RING * CHUNK) / P / RT)

        block = ctx.enter_context(nc.Block())

        last_step = Step((STEPS - 1) // 2, (STEPS - 1) % 2, False)

        def settle(eng):
            eng.sem_inc(passed, 1)

        def expert_chunks(eng, pair, epar, emit):
            base = pair * (2 * CHUNKS // RING)
            first, end = epar * CHUNKS, (epar + 1) * CHUNKS
            turn, turns_end = -(-first // RING), end // RING
            for c in range(first, turn * RING):
                emit(base + c // RING, c % RING)
            settle(eng)
            with eng.Fori(turn, turns_end) as h:
                for ring in range(RING):
                    emit(base + h, ring)
            for c in range(turns_end * RING, end):
                emit(base + c // RING, c % RING)

        def st_of(b, s):
            return b * STEPS + s.index

        def half_of(b, s):
            return b * (STEPS // 2) + s.half

        def tokens_rows(dram, b, s):
            return dram[bass.ds(b * IMG_TOK + s.index * ST, ST), :].rearrange("(t p) c -> p t c", p=P)

        def tokens_cols(dram, b, s, s2):
            img = dram[bass.ds(b * IMG_TOK, IMG_TOK), :].rearrange("(h w) c -> h w c", w=W)
            cols = img[:, bass.ds(s.index * LINES, LINES), :].rearrange("h (t s2) c -> h t s2 c", s2=2)
            return cols[:, :, s2, :]

        @block.sync
        def _(sp):
            for dst, src in ((wq_sb, wqT), (wk_sb, wkT), (wv_sb, wvT), (wo_sb, woT), (gw_sb, gate_w)):
                sp.dma_start(dst[:, :, :], src.rearrange("(c p) n -> p c n", p=P)).then_inc(consts, 16)
            for dst, src in ((bq_sb, bq), (bk_sb, bk), (bl_sb, blepe)):
                sp.dma_start(dst[:, :], src.rearrange("(c p) -> p c", p=P),
                             allow_slow_non_contiguous=True).then_inc(consts, 16)
            for dst, src in ((bv_sb, bv), (bo_sb, bo), (gb_sb, gate_b)):
                sp.dma_start(dst[:, :], src.partition_broadcast(P)).then_inc(consts, 16)
            sp.dma_start(wl_sb[:, :, :], wlepe.rearrange("(c p) k -> p c k", p=P)).then_inc(consts, 16)
            for m, mask in enumerate((mask_w, mask_h)):
                by_head = mask.rearrange("(c i e) q k -> e i q c k", i=2, e=2)
                for e in range(2):
                    for i in range(2):
                        sp.dma_start(masks[64 * e:64 * e + 64, m, 2 * i:2 * i + 2, :],
                                     by_head[e, i]).then_inc(consts, 16)
            for n in range(2):
                sp.sem_inc(v1_stored[n], 16)
                sp.sem_inc(qk_stored[n], 32)
                sp.sem_inc(x2_stored[n], 64)
                sp.sem_inc(lg_stored[n], 32)

            def store_logits(i, q):
                sp.wait_ge(lg_ready, done(st_of(i, q)))
                for s2 in range(2):
                    sp.dma_start(tokens_cols(lg_t, i, q, s2), lg_st[64 * s2:64 * s2 + 64, q.par]
                                 ).then_inc(lg_stored[q.par], 16)

            def load_logits(i):
                for n in range(2):
                    sp.wait_ge(lg_stored[n], i * (16 * STEPS) + (16 * STEPS + 32))
                    settle(sp)
                sp.dma_start(rl[:, :, :], lg_t[bass.ds(i * IMG_TOK, IMG_TOK), :].rearrange(
                    "(p t) e -> p t e", t=RT)).then_inc(rl_load, 16)

            def image(b, routing):
                def phase1(s):
                    if routing and not s.inside and s.index == -1:
                        store_logits(b - 1, last_step)
                    if routing and not s.inside and s.index == 1:
                        load_logits(b - 1)
                    q = s.plus(3)
                    if q.valid(STEPS):
                        sp.wait_ge(xn_ready, freed(st_of(b, q), 2))
                        sp.dma_start(x_in[:, q.par], tokens_rows(x_t, b, q)).then_inc(x_load[q.par], 16)
                    q = s.plus(1)
                    if q.valid(STEPS):
                        if not q.inside and q.index == 0:
                            sp.wait_ge(staged, b * (2 * STEPS) + CREDIT)
                        cols = bass.ds(q.index * ST, ST)
                        sp.wait_ge(q_sb, done(st_of(b, q)))
                        sp.dma_start(q_img[:, :, cols], q_st[:, q.par]).then_inc(qk_stored[q.par], 16)
                        sp.wait_ge(k_sb, done(st_of(b, q)))
                        settle(sp)
                        sp.dma_start(k_img[:, :, cols], k_st[:, q.par]).then_inc(qk_stored[q.par], 16)
                    q = s.plus(-1)
                    if q.valid(STEPS):
                        sp.wait_ge(o_sb, done(b * (2 * STEPS) + q.index))
                        sp.dma_start(tokens_rows(v1_t, b, q),
                                     v1_st[:, q.par].rearrange("p t d n -> p t (d n)")).then_inc(v1_stored[q.par], 16)

                run_steps(sp, -3, STEPS, LO, HI, phase1, settle)
                for n in range(2):
                    sp.wait_ge(v1_stored[n], b * (8 * STEPS) + (8 * STEPS + 16))
                    settle(sp)

                def phase2(s):
                    q = s.plus(1)
                    if q.valid(STEPS):
                        sp.wait_ge(o_ready, freed(b * (2 * STEPS) + (q.index + STEPS), 2))
                        for s2 in range(2):
                            sp.dma_start(v_st[64 * s2:64 * s2 + 64, q.par].rearrange("p t d n -> p t (d n)"),
                                         tokens_cols(v1_t, b, q, s2)).then_inc(v_load[q.par], 16)
                    if s.valid(STEPS):
                        sp.wait_ge(x2_ready, freed(st_of(b, s), 2))
                        for s2 in range(2):
                            sp.dma_start(x_r[64 * s2:64 * s2 + 64, s.par], tokens_cols(x_t, b, s, s2)
                                         ).then_inc(xr_load[s.par], 16)
                    q = s.plus(-2)
                    if q.valid(STEPS):
                        sp.wait_ge(x2_ready, done(st_of(b, q)))
                        for s2 in range(2):
                            for dram in (x2_t, out_t):
                                sp.dma_start(tokens_cols(dram, b, q, s2), x2_st[64 * s2:64 * s2 + 64, q.par]
                                             ).then_inc(x2_stored[q.par], 16)
                    q = s.plus(-3)
                    if q.valid(STEPS):
                        store_logits(b, q)

                run_steps(sp, -1, STEPS + 1, LO, HI, phase2, settle)
            image(0, False)
            with sp.Fori(1, IMGS) as b:
                image(b, True)
            store_logits(IMGS - 1, last_step)
            load_logits(IMGS - 1)

            w1_rows = w1.rearrange("e d f -> (e d) f")
            w2_rows = w2.rearrange("e f d -> (e f) d")

            def weights(e):
                for dst, src in ((w1_raw, w1_rows[bass.ds(e * C, C), :]), (w2_raw, w2_rows[bass.ds(e * F, F), :])):
                    sp.dma_start(dst[:, :, :], src.rearrange("(c p) n -> p c n", p=P)).then_inc(w_load, 16)

            def biases(e, par):
                sp.dma_start(b1_sb[par][:, :], b1[:, bass.ds(e * FB, FB)]).then_inc(b_load[par], 16)
                sp.dma_start(b2_sb[par][:, :], b2[bass.ds(e, 1), :].rearrange("a c -> (a c)").partition_broadcast(P)
                             ).then_inc(b_load[par], 16)

            def tokens(slots, ring):
                sp.dma_start(tok_g[:, ring, :, :], slot_t[slots, :].rearrange("(p i) c -> p i c", i=CT)
                             ).then_inc(tok_load[ring], 16)

            def tokens_of_expert(pair, epar):
                def load(h, ring):
                    sp.wait_ge(tok_taken, done(h * RING + ring))
                    settle(sp)
                    tokens(bass.ds((h * RING + (ring + RING)) * CHUNK, CHUNK), ring)

                expert_chunks(sp, pair, epar, load)

            sp.wait_ge(staged, 2 * IMGS * STEPS + CREDIT)
            settle(sp)
            weights(0)
            sp.wait_ge(attention_over, 1)
            for ring in range(RING):
                tokens(slice(ring * CHUNK, (ring + 1) * CHUNK), ring)
            for par in range(2):
                biases(par, par)
            sp.wait_ge(w_split, 1)
            weights(1)
            with sp.Fori(0, E // 2 - 1) as pair:
                for epar in range(2):
                    sp.wait_ge(w_split, pair * 2 + (epar + 2))
                    settle(sp)
                    weights(pair * 2 + (epar + 2))
                    tokens_of_expert(pair, epar)
                    sp.wait_ge(y_taken, pair * (2 * CHUNKS) + ((epar + 1) * CHUNKS + CREDIT))
                    settle(sp)
                    biases(pair * 2 + (epar + 2), epar)
            for epar in range(2):
                tokens_of_expert(E // 2 - 1, epar)
            for ring in range(RING):
                sp.wait_ge(tok_load[ring], 16 * (E * CHUNKS // RING + 1))
            for n in range(2):
                sp.wait_ge(x2_stored[n], 32 * IMGS * STEPS + 64)
                sp.wait_ge(scattered[n], 16 * CT * (E * CHUNKS // 2))

        @block.tensor
        def _(pe):
            for s_ in (xT_ready, q_ready, k_ready, v_ready, vT_ready, s_ready, eT_ready, o_ready,
                       oT_ready, y_ready, hT_ready, g_ready, fT_ready, f_ready):
                pe.sem_inc(s_, CREDIT)
            pe.sem_inc(h_ready, CREDIT)
            pe.wait_ge(consts, 16 * CONST_DMAS)
            pe.wait_ge(made, 5)

            def scores(g, par):
                pe.wait_ge(mx_done, freed(g, 1))
                for c in range(KC):
                    for r in range(LINES):
                        for a in range(4):
                            i, e = a // 2, a % 2
                            rows = slice(32 * a, 32 * a + 32)
                            line = slice(64 * r, 64 * r + 64)
                            col = 256 * c + 64 * r
                            last = nc.tensor.matmul(ps_s[64 * e:64 * e + 64, i, col:col + 64],
                                                    q_st[rows, par, c, line], k_st[rows, par, c, line],
                                                    start=True, stop=True)
                last.then_inc(s_ready, 1)

            def weights_T(g):
                pe.wait_ge(e_ready, done(g))
                pe.wait_ge(o_sb, freed(g, 1))
                for k in range(8):
                    ic, rp_ = k // 2, k % 2
                    src = ex_sb[:, LINES * ic + 2 * rp_:LINES * ic + 2 * rp_ + 2, :].rearrange("p r k -> p (r k)")
                    last = nc.tensor.transpose(ps_t[:, P * k:P * k + P], src, ident[:, :])
                last.then_inc(eT_ready, 1)

            def values(g, par):
                pe.wait_ge(eT_sb, done(g))
                settle(pe)
                for t in range(TT):
                    for c in range(KC):
                        for i in range(2):
                            for e in range(2):
                                for r in range(2):
                                    n = 4 * c + 2 * i + e
                                    rows = slice(64 * r, 64 * r + 64)
                                    last = nc.tensor.matmul(
                                        ps_o[rows, t, n, :], exT_sb[rows, 2 * (2 * i + c) + t, 64 * e:64 * e + 64],
                                        v_st[rows, par, t, :, n], start=True, stop=True)
                last.then_inc(o_ready, 1)

            def expert_sums(i):
                pe.wait_ge(r_totals, i + 1)
                nc.tensor.matmul(ps_p[0][:, 0:E], upper[:, :], r_tot[:, :], start=True, stop=True)
                nc.tensor.matmul(ps_p[1][:, 0:E], ones[:, :], r_tot[:, :], start=True, stop=True).then_inc(r_pe, 1)

            def image(b, routing):
                def phase1(s):
                    g = b * (2 * STEPS) + s.index
                    q = s.plus(-1)
                    if q.valid(STEPS):
                        weights_T(g - 1)
                    if s.valid(STEPS):
                        pe.wait_ge(q_sb, done(st_of(b, s)))
                        pe.wait_ge(k_sb, done(st_of(b, s)))
                        scores(g, s.par)
                        pe.wait_ge(v_sb, done(st_of(b, s)))
                        for c in range(KC):
                            for t in range(TT):
                                last = nc.tensor.transpose(ps_p[1][:, ST * c + P * t:ST * c + P * t + P],
                                                           v_st[:, s.par, t, DC * c:DC * c + DC, :].rearrange("p d n -> p (d n)"),
                                                           ident[:, :])
                        last.then_inc(vT_ready, 1)
                    q = s.plus(1)
                    n = st_of(b, q)
                    if q.valid(STEPS):
                        pe.wait_ge(xn_ready, done(n))
                        for c in range(KC):
                            for t in range(TT):
                                last = nc.tensor.transpose(ps_p[0][:, ST * c + P * t:ST * c + P * t + P],
                                                           xn[:, q.par, t, P * c:P * c + P], ident[:, :])
                        last.then_inc(xT_ready, 1)
                    if s.plus(-1).valid(STEPS):
                        values(g - 1, s.plus(-1).par)
                    if q.valid(STEPS):
                        pe.wait_ge(xnT_sb_ready, done(n))
                        pe.wait_ge(vT_sb, freed(n, 1))
                        for bank, wt, taken, ready in ((1, wq_sb, q_sb, q_ready), (2, wk_sb, k_sb, k_ready)):
                            pe.wait_ge(taken, freed(n, 1))
                            for m in range(KC):
                                for c in range(KC):
                                    last = nc.tensor.matmul(ps_p[bank][:, ST * m:ST * m + ST],
                                                            wt[:, c, P * m:P * m + P], xnT[:, c, :],
                                                            start=(c == 0), stop=(c == KC - 1))
                            last.then_inc(ready, 1)
                        pe.wait_ge(v_sb, freed(n, 1))
                        for t in range(TT):
                            for c in range(KC):
                                last = nc.tensor.matmul(ps_p[3][:, C * t:C * t + C], xnT[:, c, P * t:P * t + P],
                                                        wv_sb[:, c, :], start=(c == 0), stop=(c == KC - 1))
                        last.then_inc(v_ready, 1)

                run_steps(pe, -1, STEPS, LO, HI, phase1, settle)
                pe.wait_ge(vT_sb, done(b * STEPS + (STEPS - 1)))
                if routing:
                    expert_sums(b - 1)

                def phase2(s):
                    g = b * (2 * STEPS) + (s.index + STEPS)
                    q1, q2, q3 = s.plus(-1), s.plus(-2), s.plus(-3)
                    if q1.valid(STEPS):
                        weights_T(g - 1)
                    if s.valid(STEPS):
                        pe.wait_ge(staged, st_of(b, s) * 2 + (2 + CREDIT))
                        scores(g, s.par)
                    if routing and not s.inside and s.index == 2:
                        pe.wait_ge(r_sums_taken, b)
                    if q2.valid(STEPS):
                        pe.wait_ge(o_sb, done(g - 2))
                        pe.wait_ge(oT_done, freed(st_of(b, q2), 1))
                        for c in range(KC):
                            for t in range(TT):
                                last = nc.tensor.transpose(ps_p[0][:, ST * c + P * t:ST * c + P * t + P],
                                                           o2[:, q2.par, t, P * c:P * c + P], ident[:, :])
                        last.then_inc(oT_ready, 1)
                    if q3.valid(STEPS):
                        pe.wait_ge(hn_ready, done(st_of(b, q3)))
                        pe.wait_ge(hT_done, freed(st_of(b, q3), 1))
                        for c in range(KC):
                            for t in range(TT):
                                last = nc.tensor.transpose(ps_p[2][:, ST * c + P * t:ST * c + P * t + P],
                                                           hn[:, q3.par, t, P * c:P * c + P], ident[:, :])
                        last.then_inc(hT_ready, 1)
                    if q1.valid(STEPS):
                        pe.wait_ge(v_load[q1.par], half_of(b, q1) * 32 + 32)
                        values(g - 1, q1.par)
                    if q2.valid(STEPS):
                        pe.wait_ge(oT_done, done(st_of(b, q2)))
                        pe.wait_ge(x2_ready, freed(st_of(b, q2), 1))
                        for t in range(TT):
                            for c in range(KC):
                                last = nc.tensor.matmul(ps_p[1][:, C * t:C * t + C], oT_sb[:, c, P * t:P * t + P],
                                                        wo_sb[:, c, :], start=(c == 0), stop=(c == KC - 1))
                        last.then_inc(y_ready, 1)
                    if q3.valid(STEPS):
                        pe.wait_ge(hT_done, done(st_of(b, q3)))
                        pe.wait_ge(lg_ready, freed(st_of(b, q3), 1))
                        for t in range(TT):
                            for c in range(KC):
                                last = nc.tensor.matmul(ps_p[3][:, E * t:E * t + E], hT_sb[:, c, P * t:P * t + P],
                                                        gw_sb[:, c, :], start=(c == 0), stop=(c == KC - 1))
                        last.then_inc(g_ready, 1)

                run_steps(pe, 0, STEPS + 2, LO, HI, phase2, settle)
                pe.wait_ge(lg_ready, done(b * STEPS + (STEPS - 1)))

            image(0, False)
            with pe.Fori(1, IMGS) as b:
                image(b, True)
            expert_sums(IMGS - 1)

            def transposes(n):
                pe.wait_ge(fn_ready, done(n))
                pe.wait_ge(fT_done, freed(n, 1))
                for c in range(KC):
                    for i in range(CT):
                        last = nc.tensor.transpose(ps_p[c][:, P * i:P * i + P], fn[:, i, P * c:P * c + P],
                                                   ident[:, :])
                last.then_inc(fT_ready, 1)

            transposes(0)
            with pe.Fori(0, E // 2) as pair:
                for par in range(2):
                    pe.wait_ge(w_split, pair * 2 + (par + 1))
                    settle(pe)
                    with pe.Fori(0, CHUNKS) as j:
                        n = pair * (2 * CHUNKS) + (j + par * CHUNKS)
                        pe.wait_ge(fT_high_done, done(n))
                        for f in range(FB):
                            pe.wait_ge(relu_done, n * FB + (f + 1))
                            k = 0
                            for w_, x_ in ((0, fT_high), (1, fT_high), (0, fT_low)):
                                if f == 0 and x_ is fT_low:
                                    pe.wait_ge(fT_done, done(n))
                                for c in range(KC):
                                    last = nc.tensor.matmul(ps_s[:, f % 2, :], w1_hl[par][w_][:, c, P * f:P * f + P],
                                                            x_[:, c, :], start=(k == 0), stop=(k == 3 * KC - 1))
                                    k += 1
                            last.then_inc(h_ready, 1)
                        pe.wait_ge(y_taken, freed(n, 1))
                        for i in range(CT):
                            if i == 2:
                                transposes(n + 1)
                            rows = slice(P * i, P * i + P)
                            k = 0
                            for f in range(FB):
                                if i == 0:
                                    pe.wait_ge(h_low_done, n * FB + (f + 1 + CREDIT))
                                for x_, w_ in ((h_high, 0), (h_high, 1), (h_low, 0)):
                                    last = nc.tensor.matmul(ps_t[:, C * i:C * i + C], x_[:, f, rows],
                                                            w2_hl[par][w_][:, f, :], start=(k == 0),
                                                            stop=(k == 3 * FB - 1))
                                    k += 1
                        last.then_inc(f_ready, 1)

        @block.scalar
        def _(act):
            for s_ in (xnT_sb_ready, q_sb, k_sb, vT_sb, e_ready, eT_sb, hT_done, fT_high_done, relu_done):
                act.sem_inc(s_, CREDIT)
            act.wait_ge(consts, 16 * CONST_DMAS)
            act.wait_ge(made, 5)
            act.wait_ge(bk_scaled, 1)

            def exps(g):
                act.wait_ge(mx_done, done(g))
                act.wait_ge(eT_ready, freed(g, 1))
                for line in range(4 * LINES):
                    last = nc.scalar.activation(ex_sb[:, line, :], sc_sb[:, line, :], ACT.Exp,
                                                bias=mx_sb[:, line:line + 1])
                last.then_inc(e_ready, 1)

            def take_weights_T(g):
                act.wait_ge(eT_ready, done(g))
                act.wait_ge(o_ready, freed(g, 1))
                nc.scalar.activation(exT_sb[:, :, :].rearrange("p k q -> p (k q)"), ps_t[:, :], ACT.Copy
                                     ).then_inc(eT_sb, 1)

            def logit_exps(i):
                act.wait_ge(r_shifted, i + 1)
                nc.scalar.activation(rp[:, :, :], rl[:, :, :], ACT.Exp).then_inc(r_exp, 1)

            def image(b, routing):
                act.wait_ge(conv_done, b + 1)

                def phase1(s):
                    g = b * (2 * STEPS) + s.index
                    if s.plus(-1).valid(STEPS):
                        take_weights_T(g - 1)
                    if s.valid(STEPS):
                        act.wait_ge(vT_ready, done(st_of(b, s)))
                        rows = bass.ds(s.index * LINES + PAD, LINES)
                        nc.scalar.activation(v_pad[:, :, rows, PAD:PAD + W],
                                             ps_p[1][:, :].rearrange("p (c r w) -> p c r w", c=KC, w=W),
                                             ACT.Copy).then_inc(vT_sb, 1)
                    q = s.plus(1)
                    n = st_of(b, q)
                    if q.valid(STEPS):
                        act.wait_ge(xT_ready, done(n))
                        act.wait_ge(v_ready, freed(n, 1))
                        nc.scalar.activation(xnT[:, :, :].rearrange("p c t -> p (c t)"), ps_p[0][:, :], ACT.Copy
                                             ).then_inc(xnT_sb_ready, 1)
                    if s.valid(STEPS):
                        exps(g)
                    if routing and not s.inside and s.index == 3:
                        logit_exps(b - 1)
                    if q.valid(STEPS):
                        act.wait_ge(q_ready, done(n))
                        act.wait_ge(qk_stored[q.par], half_of(b, q) * 32 + 32)
                        act.wait_ge(s_ready, freed(b * (2 * STEPS) + q.index, 2))
                        for c in range(KC):
                            last = nc.scalar.activation(q_st[:, q.par, c, :], ps_p[1][:, ST * c:ST * c + ST],
                                                        ACT.Identity, bias=bq_sb[:, c:c + 1])
                        last.then_inc(q_sb, 1)
                        act.wait_ge(k_ready, done(n))
                        for c in range(KC):
                            last = nc.scalar.activation(k_st[:, q.par, c, :], ps_p[2][:, ST * c:ST * c + ST],
                                                        ACT.Identity, bias=bk_sb[:, c:c + 1], scale=SCALING)
                        last.then_inc(k_sb, 1)

                run_steps(act, -1, STEPS, LO, HI, phase1, settle)

                def phase2(s):
                    g = b * (2 * STEPS) + (s.index + STEPS)
                    if s.plus(-1).valid(STEPS):
                        take_weights_T(g - 1)
                    q = s.plus(-3)
                    if q.valid(STEPS):
                        act.wait_ge(hT_ready, done(st_of(b, q)))
                        act.wait_ge(g_ready, freed(st_of(b, q), 1))
                        nc.scalar.activation(hT_sb[:, :, :].rearrange("p c t -> p (c t)"), ps_p[2][:, :], ACT.Copy
                                             ).then_inc(hT_done, 1)
                    if s.valid(STEPS):
                        exps(g)

                run_steps(act, 0, STEPS + 2, LO, HI, phase2, settle)
            image(0, False)
            with act.Fori(1, IMGS) as b:
                image(b, True)
            logit_exps(IMGS - 1)

            def take_fT(n):
                act.wait_ge(fT_ready, done(n))
                for c in range(KC):
                    last = nc.scalar.activation(fT_high[:, c, :], ps_p[c][:, :], ACT.Copy)
                last.then_inc(fT_high_done, 1)

            def split_weights(e, par):
                act.wait_ge(w_load, e * 32 + 32)
                settle(act)
                for c in range(KC):
                    nc.scalar.activation(w1_hl[par][0][:, c, :], w1_raw[:, c, :], ACT.Copy).then_inc(w_high_done, 1)
                for c in range(0, FB, FB // 2):
                    nc.scalar.activation(w2_hl[par][0][:, c:c + FB // 2, :], w2_raw[:, c:c + FB // 2, :], ACT.Copy
                                         ).then_inc(w_high_done, 1)

            def hidden_of_expert(pair, par):
                act.wait_ge(b_load[par], pair * 32 + 32)
                settle(act)
                with act.Fori(0, CHUNKS) as j:
                    n = pair * (2 * CHUNKS) + (j + par * CHUNKS)
                    act.wait_ge(f_ready, freed(n, 1))
                    for f in range(FB):
                        act.wait_ge(h_ready, n * FB + (f + 1 + CREDIT))
                        nc.scalar.activation(h_raw[:, f, :], ps_s[:, f % 2, :], ACT.Relu,
                                             bias=b1_sb[par][:, f:f + 1]).then_inc(relu_done, 1)
                        act.wait_ge(relu_done, n * FB + (f + 1 + CREDIT))
                        nc.scalar.activation(h_high[:, f, :], h_raw[:, f, :], ACT.Copy).then_inc(h_high_done, 1)
                    take_fT(n + 1)

            split_weights(0, 0)
            act.wait_ge(attention_over, 1)
            take_fT(0)

            with act.Fori(0, E // 2 - 1) as pair:
                for par in range(2):
                    act.wait_ge(f_ready, pair * (2 * CHUNKS) + (par * CHUNKS + CREDIT))
                    split_weights(pair * 2 + (par + 1), 1 - par)
                    hidden_of_expert(pair, par)
            pair = E // 2 - 1
            act.wait_ge(f_ready, pair * (2 * CHUNKS) + CREDIT)
            split_weights(E - 1, 1)
            for par in range(2):
                hidden_of_expert(pair, par)

        @block.vector
        def _(dve):
            nc.disable_value_cache = True
            for s_ in (stat1, xn_ready, v_sb, mx_done, o_sb,
                       oT_done, x2_ready, stat2, hn_ready, lg_ready, fn_ready, y_taken, tok_taken,
                       fT_done, h_low_done):
                dve.sem_inc(s_, CREDIT)
            dve.sem_inc(conv_done, 1)
            dve.sem_inc(yo_ready, CREDIT - 1)
            nc.vector.memset(ones[:, :], 1.0).then_inc(made, 1)
            nc.vector.memset(r_run[:, :], 0.0)
            nc.vector.memset(half[:, :], -0.5)
            nc.vector.memset(r_reset[:, :, 1:RT], 1.0)
            nc.vector.memset(r_reset[:, :, 0], 0.0)
            nc.vector.memset(r_cum[:, :, 0], 0.0)
            nc.vector.memset(v_st[:, :, :, :, :], 1.0)
            nc.vector.memset(v1_st[:, :, :, :, :], 1.0)
            nc.vector.memset(v_pad[:, :, :, :], 0.0).then_inc(made, 1)
            dve.wait_ge(consts, 16 * CONST_DMAS)
            nc.vector.tensor_scalar(bk_sb[:, :], bk_sb[:, :], SCALING, None, ALU.mult).then_inc(bk_scaled, 1)
            dve.wait_ge(made, 5)
            dve.wait_ge(r_ready, 5)
            dve.wait_ge(table_cleared, 16 * CLEAR_DMAS)

            links = [0]

            def linked():
                links[0] += 1
                return links[0]

            def chain_restarts():
                if links[0]:
                    dve.wait_ge(chain, links[0])
                    dve.sem_clear(chain)
                links[0] = 0

            def soft1(g, m, taps):
                dve.wait_ge(s_ready, done(g))
                nc.vector.tensor_tensor(
                    sc_sb[:, :, :].rearrange("p (a r) k -> p a r k", r=LINES),
                    ps_s[:, :, :].rearrange("p i (c r k) -> p (i c) r k", c=KC, k=64),
                    masks[:, m, :, :].unsqueeze(2).broadcast_to([P, 4, LINES, 64]), ALU.add).then_inc(chain, 1)
                masked = linked()
                taps(1)
                dve.wait_ge(chain, masked)
                nc.vector.tensor_reduce(mx_sb[:, :], sc_sb[:, :, :], AX_X, ALU.max).then_inc(chain, 1)
                greatest = linked()
                taps(1)
                dve.wait_ge(chain, greatest)
                nc.vector.tensor_scalar(mx_sb[:, :], mx_sb[:, :], -1.0, None, ALU.mult).then_inc(mx_done, 1)

            def normalised(g, dst, taps):
                dve.wait_ge(o_ready, done(g))
                nc.vector.reciprocal(rec_sb[:, :].rearrange("p (t n) -> p t n", t=TT), ps_o[:, :, :, KEY_DIM]
                                     ).then_inc(chain, 1)
                inverted = linked()
                taps(1)
                dve.wait_ge(chain, inverted)
                nc.vector.tensor_tensor(
                    dst, ps_o[:, :, :, 0:KEY_DIM],
                    rec_sb[:, :].rearrange("p (t n) -> p t n", t=TT).unsqueeze(3).broadcast_to(
                        [P, TT, HEADS, KEY_DIM]), ALU.mult).then_inc(o_sb, 1)

            def logits(i, q):
                dve.wait_ge(g_ready, done(st_of(i, q)))
                dve.wait_ge(lg_stored[q.par], half_of(i, q) * 32 + 32)
                nc.vector.tensor_tensor(
                    lg_st[:, q.par], ps_p[3][:, 0:TT * E].rearrange("p (t e) -> p t e", t=TT),
                    gb_sb[:, :].unsqueeze(1).broadcast_to([P, TT, E]), ALU.add).then_inc(lg_ready, 1)

            def convolution(c, window, out_view, first, count):
                at = [first, 0]

                def taps(k):
                    for tap in range(at[0], min(at[0] + k, first + count)):
                        src = v_pad[:, c, window(tap // 5, tap % 5)[0], window(tap // 5, tap % 5)[1]]
                        if at[1]:
                            dve.wait_ge(chain, at[1])
                        if tap == 0:
                            nc.vector.tensor_scalar(out_view, src, wl_sb[:, c, 0:1], bl_sb[:, c:c + 1],
                                                    ALU.mult, ALU.add).then_inc(chain, 1)
                        else:
                            nc.vector.scalar_tensor_tensor(out_view, src, wl_sb[:, c, tap:tap + 1], out_view,
                                                           ALU.mult, ALU.add).then_inc(chain, 1)
                        at[:] = tap + 1, linked()

                return taps

            def no_taps(k):
                pass

            def stats(src, sp_, tiles, out_sem, taps):
                for t in range(tiles):
                    last = nc.vector.bn_stats(stat[:, sp_, t, :], src[:, t, :])
                last.then_inc(chain, 1)
                counted = linked()
                taps(1)
                dve.wait_ge(chain, counted)
                for t in range(tiles):
                    last = nc.vector.bn_aggr(mv[:, sp_, t, :], stat[:, sp_, t, :])
                last.then_inc(out_sem, 1)

            def centred(dst, src, sp_, tiles, ready):
                for t in range(tiles):
                    last = nc.vector.tensor_scalar(dst[:, t, :], src[:, t, :], mv[:, sp_, t, 0:1],
                                                   rstd[:, sp_, t:t + 1], ALU.subtract, ALU.mult)
                last.then_inc(ready, 1)

            def link(ins):
                ins.then_inc(chain, 1)
                dve.wait_ge(chain, linked())

            v = nc.vector
            over_e = [P, RT, E]

            def logits_shifted(i):
                dve.wait_ge(rl_load, i * 16 + 16)
                link(v.tensor_reduce(r_mx[:, :], rl[:, :, :], AX_X, ALU.max))
                v.tensor_tensor(rl[:, :, :], rl[:, :, :], r_mx[:, :].unsqueeze(2).broadcast_to(over_e),
                                ALU.subtract).then_inc(r_shifted, 1)

            def probabilities(i):
                dve.wait_ge(r_exp, i + 1)
                link(v.tensor_reduce(r_sum[:, :], rp[:, :, :], AX_X, ALU.add))
                link(v.reciprocal(r_sum[:, :], r_sum[:, :]))
                link(v.tensor_tensor(rp[:, :, :], rp[:, :, :], r_sum[:, :].unsqueeze(2).broadcast_to(over_e),
                                     ALU.mult))
                link(v.tensor_reduce(r_mx[:, :], rp[:, :, :], AX_X, ALU.max))
                link(v.tensor_tensor(r_eq[:, :, :], rp[:, :, :], r_mx[:, :].unsqueeze(2).broadcast_to(over_e),
                                     ALU.is_equal))

            def experts():
                by_expert = "p t e -> p e t"
                for e in range(1, E):
                    link(v.tensor_tensor(r_cum[:, :, e], r_cum[:, :, e - 1], r_eq[:, :, e - 1], ALU.add))
                link(v.scalar_tensor_tensor(r_oh[:, :, :], r_cum[:, :, :].rearrange(by_expert), 0.0,
                                            r_eq[:, :, :].rearrange(by_expert), ALU.is_equal, ALU.mult))

            def counts():
                flat = "p e t -> p (e t)"
                link(v.tensor_tensor_scan(r_pos[:, :, :].rearrange(flat), r_reset[:, :, :].rearrange(flat),
                                          r_oh[:, :, :].rearrange(flat), 0.0, ALU.mult, ALU.add))
                v.tensor_copy(r_tot[:, :], r_pos[:, :, RT - 1]).then_inc(r_totals, 1)

            def slots(i):
                dve.wait_ge(r_pe, i + 1)
                link(v.tensor_tensor(r_base[:, :], ps_p[0][:, 0:E], r_run[:, :], ALU.add))
                v.tensor_tensor(r_run[:, :], ps_p[1][:, 0:E], r_run[:, :], ALU.add).then_inc(r_sums_taken, 1)
                link(v.tensor_tensor(r_pos[:, :, :], r_pos[:, :, :],
                                     r_base[:, :].unsqueeze(2).broadcast_to([P, E, RT]), ALU.add))
                link(v.tensor_scalar(r_big[:, :, :], r_pos[:, :, :], float(CAP), float(NO_TOKEN),
                                     ALU.is_gt, ALU.mult))
                link(v.tensor_tensor(r_pos[:, :, :], r_pos[:, :, :],
                                     r_first[:, :].unsqueeze(2).broadcast_to([P, E, RT]), ALU.add))
                link(v.tensor_tensor(r_pos[:, :, :], r_pos[:, :, :], r_big[:, :, :], ALU.add))
                link(v.tensor_tensor(r_pos[:, :, :], r_pos[:, :, :], r_oh[:, :, :], ALU.mult))
                link(v.tensor_reduce(r_slot[:, :], r_pos[:, :, :].rearrange("p e t -> p t e"), AX_X, ALU.add))
                dve.wait_ge(r_free, i + 1)
                link(v.tensor_scalar(r_slot_i[:, :], r_slot[:, :], -1.0, None, ALU.add))
                link(v.tensor_copy(r_pair[:, :, 0], r_tok[:, :]))
                v.tensor_copy(r_pair[:, :, 1:2].bitcast(F32), r_mx[:, :].unsqueeze(2)).then_inc(r_slots_ready, 1)
                link(v.tensor_scalar(r_tok[:, :], r_tok[:, :], float(IMG_TOK), None, ALU.add))

            PAIRS = STEPS // 2
            def image(b, routing):
                def phase1(s):
                    g = b * (2 * STEPS) + s.index
                    taps = no_taps
                    j = s.half - 1
                    if 0 <= j < PAIRS:
                        if s.par == 0:
                            dve.wait_ge(vT_sb, done(b * STEPS + min(2 * s.half, STEPS - 1)))
                        taps = convolution(
                            0, lambda kh, kw: (slice(2 * LINES * j + kh, 2 * LINES * (j + 1) + kh), slice(kw, kw + W)),
                            lepe[:, 0, 2 * LINES * j:2 * LINES * (j + 1), :], (0, 13)[s.par], (13, 12)[s.par])
                    if s.valid(STEPS):
                        soft1(g, 0, taps)
                    if routing and s.index == -1:
                        logits(b - 1, last_step)
                    if routing and s.index == 3:
                        logits_shifted(b - 1)
                    if routing and s.index == 5:
                        probabilities(b - 1)
                    if routing and s.index == 7:
                        experts()
                    if routing and s.index == 9:
                        counts()
                    taps(2)
                    q = s.plus(-1)
                    if q.valid(STEPS):
                        dve.wait_ge(v1_stored[q.par], half_of(b, q) * 16 + 16)
                        normalised(g - 1, v1_st[:, q.par, :, 0:KEY_DIM, :].rearrange("p t d n -> p t n d"), taps)
                    q = s.plus(2)
                    n = st_of(b, q)
                    if q.valid(STEPS):
                        dve.wait_ge(x_load[q.par], half_of(b, q) * 16 + 16)
                        stats(x_in[:, q.par], 0, TT, stat1, taps)
                        taps(2)
                    taps(2)
                    q = s.plus(1)
                    n = st_of(b, q)
                    if q.valid(STEPS):
                        dve.wait_ge(v_ready, done(n))
                        nc.vector.tensor_tensor(
                            v_st[:, q.par, :, 0:KEY_DIM, :].rearrange("p t d n -> p t (d n)"),
                            ps_p[3][:, :].rearrange("p (t c) -> p t c", t=TT),
                            bv_sb[:, :].unsqueeze(1).broadcast_to([P, TT, C]), ALU.add).then_inc(v_sb, 1)
                    q = s.plus(2)
                    n = st_of(b, q)
                    if q.valid(STEPS):
                        dve.wait_ge(rstd1, n + 1)
                        centred(xn[:, q.par], x_in[:, q.par], 0, TT, xn_ready)
                    taps(TAPS)
                    chain_restarts()

                for s in range(-2, STEPS + 2):
                    phase1(Step(s // 2, s % 2, False))

                def phase2(s):
                    g = b * (2 * STEPS) + (s.index + STEPS)
                    taps = no_taps
                    j = s.half
                    if 0 <= j < PAIRS:
                        taps = convolution(
                            1, lambda kh, kw: (slice(kh, kh + H), slice(2 * LINES * j + kw, 2 * LINES * (j + 1) + kw)),
                            lepe[:, 1, :, 2 * LINES * j:2 * LINES * (j + 1)], (0, 13)[s.par], (13, 12)[s.par])
                    if s.valid(STEPS):
                        soft1(g, 1, taps)
                    if routing and s.index == 0:
                        slots(b - 1)
                    taps(1)
                    q = s.plus(-2)
                    n = st_of(b, q)
                    if q.valid(STEPS):
                        dve.wait_ge(oT_ready, done(n))
                        cols = slice(q.index * LINES, q.index * LINES + LINES)
                        for c in range(KC):
                            last = nc.vector.tensor_tensor(
                                oT_sb[:, c, :].rearrange("p (w h) -> p w h", h=H),
                                ps_p[0][:, ST * c:ST * c + ST].rearrange("p (w h) -> p w h", h=H),
                                lepe[:, c, :, cols].rearrange("p h w -> p w h"), ALU.add)
                        last.then_inc(oT_done, 1)
                    taps(3)
                    q = s.plus(-1)
                    if q.valid(STEPS):
                        normalised(g - 1, o2[:, q.par].rearrange("p t (d n) -> p t n d", n=HEADS), taps)
                    q = s.plus(-2)
                    if q.valid(STEPS):
                        dve.wait_ge(xb_ready, n + 1)
                        dve.wait_ge(x2_stored[q.par], half_of(b, q) * 64 + 64)
                        dve.wait_ge(y_ready, done(n))
                        nc.vector.tensor_tensor(x2_st[:, q.par].rearrange("p t c -> p (t c)"), ps_p[1][:, :],
                                                x_r[:, q.par].rearrange("p t c -> p (t c)"), ALU.add
                                                ).then_inc(x2_ready, 1)
                        taps(1)
                        dve.wait_ge(x2_ready, done(n))
                        stats(x2_st[:, q.par], 1, TT, stat2, taps)
                        taps(2)
                    q = s.plus(-3)
                    if q.valid(STEPS):
                        logits(b, q)
                    q = s.plus(-2)
                    if q.valid(STEPS):
                        dve.wait_ge(rstd2, n + 1)
                        centred(hn[:, q.par], x2_st[:, q.par], 1, TT, hn_ready)
                    taps(TAPS)
                    chain_restarts()
                    if s.index == 2 * PAIRS - 1:
                        dve.sem_inc(conv_done, 1)

                for s in range(-1, STEPS + 2):
                    phase2(Step(s // 2, s % 2, False))

            image(0, False)
            with dve.Fori(1, IMGS) as b:
                image(b, True)
            i = IMGS - 1
            logits(i, last_step)
            logits_shifted(i)
            probabilities(i)
            experts()
            counts()
            slots(i)
            chain_restarts()

            def stats_of(h, ring):
                dve.wait_ge(gathered[ring], h * (16 * CT) + 16 * CT)
                settle(dve)
                stats(xg[ring], ring % 2, CT, f_aggr, no_taps)

            def low_fT(n):
                dve.wait_ge(fT_high_done, done(n))
                for c in range(KC):
                    last = nc.vector.tensor_tensor(fT_low[:, c, :], ps_p[c][:, :], fT_high[:, c, :].bitcast(F32),
                                                   ALU.subtract)
                last.then_inc(fT_done, 1)

            def low_weights(e, par):
                k = 0
                for (high, low), raw, step in ((w1_hl[par], w1_raw, 1), (w2_hl[par], w2_raw, FB // 2)):
                    for c in range(0, raw.shape[1], step):
                        k += 1
                        dve.wait_ge(w_high_done, e * 4 + k)
                        last = nc.vector.tensor_tensor(low[:, c:c + step, :], raw[:, c:c + step, :],
                                                       high[:, c:c + step, :].bitcast(F32), ALU.subtract)
                last.then_inc(w_split, 1)

            def finish(par):
                prob = prob_s[:, par].unsqueeze(2).broadcast_to([P, CT, C])

                link(nc.vector.tensor_tensor(y_sb[:, :, :], y_sb[:, :, :], prob, ALU.mult))
                link(nc.vector.tensor_scalar(r_sb[:, :, :], y_sb[:, :, :], -1e4, 1e4, ALU.max, ALU.min))
                link(nc.vector.tensor_tensor(m_sb[:, :, :], y_sb[:, :, :], y_sb[:, :, :], ALU.is_equal))
                link(nc.vector.tensor_tensor(r_sb[:, :, :], r_sb[:, :, :], m_sb[:, :, :], ALU.mult))
                link(nc.vector.tensor_scalar(m_sb[:, :, :], y_sb[:, :, :], 0.0, 0.0, ALU.mult, ALU.is_equal))
                link(nc.vector.copy_predicated(r_sb[:, :, :], m_sb[:, :, :].bitcast(U32), y_sb[:, :, :]))

            def with_residual(par, ring):
                nc.vector.tensor_tensor(yo[par][:, :, :], r_sb[:, :, :], xg[ring][:, :, :], ALU.add
                                        ).then_inc(yo_ready, 1)

            def chunk(n, h, ring, epar):
                def low_hidden(first, count):
                    for f in range(first, first + count):
                        dve.wait_ge(h_high_done, f + 1)
                        if f == FB - 1:
                            dve.sem_clear(h_high_done)
                        nc.vector.tensor_tensor(h_low[:, f, :], h_raw[:, f, :], h_high[:, f, :].bitcast(F32),
                                                ALU.subtract).then_inc(h_low_done, 1)

                nxt = (ring + 1) % RING
                low_hidden(0, FB - 3)
                stats_of(h + (ring + 2) // RING, (ring + 2) % RING)
                low_hidden(FB - 3, 3)
                dve.wait_ge(f_rstd, n + 2)
                centred(fn, xg[nxt], nxt % 2, CT, fn_ready)
                finish((ring + 1) % 2)
                low_fT(n + 1)
                with_residual((ring + 1) % 2, (ring + RING - 1) % RING)
                dve.wait_ge(yo_free, n + CREDIT)
                nc.vector.tensor_copy(tok_s[:, ring % 2], tok_g[:, ring, :, 0])
                nc.vector.tensor_copy(prob_s[:, ring % 2].unsqueeze(2), tok_g[:, ring, :, 1:2].bitcast(F32)
                                      ).then_inc(tok_taken, 1)
                dve.wait_ge(f_ready, done(n))
                nc.vector.tensor_tensor(
                    y_sb[:, :, :], ps_t[:, :].rearrange("p (i c) -> p i c", i=CT),
                    b2_sb[epar][:, :].unsqueeze(1).broadcast_to([P, CT, C]), ALU.add).then_inc(y_taken, 1)
                chain_restarts()
                dve.wait_ge(tok_taken, done(n))
                dve.wait_ge(y_taken, done(n))
                settle(dve)

            low_weights(0, 0)
            dve.wait_ge(attention_over, 1)
            nc.vector.memset(y_sb[:, :, :], 0.0).then_inc(chain, 1)
            linked()
            nc.vector.memset(prob_s[:, :, :], 0.0).then_inc(chain, 1)
            linked()
            chain_restarts()
            dve.wait_ge(gathered[RING - 1], 16 * CT)
            stats_of(0, 0)
            stats_of(0, 1)
            dve.wait_ge(f_rstd, 1)
            centred(fn, xg[0], 0, CT, fn_ready)
            low_fT(0)
            chain_restarts()

            def chunks_of_expert(pair, epar):
                dve.wait_ge(b_load[epar], pair * 32 + 32)
                settle(dve)
                expert_chunks(dve, pair, epar, lambda h, ring: chunk(h * RING + ring, h, ring, epar))

            with dve.Fori(0, E // 2 - 1) as pair:
                for epar in range(2):
                    low_weights(pair * 2 + (epar + 1), 1 - epar)
                    chunks_of_expert(pair, epar)
            low_weights(E - 1, 1)
            for epar in range(2):
                chunks_of_expert(E // 2 - 1, epar)
            finish(1)
            stats_of(E * CHUNKS // RING, 2)
            with_residual(1, RING - 1)
            chain_restarts()

        @block.gpsimd
        def _(pool):
            pool.sem_inc(staged, CREDIT)
            pool.sem_inc(yo_free, CREDIT + 1)
            pool.sem_inc(r_free, 1)
            nc.gpsimd.memset(ident[:, :], 0.0).then_inc(made, 1)
            nc.gpsimd.iota(r_pair[:, :, :], pattern=[[0, 2 * RT]], base=NO_TOKEN, channel_multiplier=0
                           ).then_inc(r_ready, 1)
            pool.wait_ge(made, 3)
            nc.gpsimd.affine_select(out=ident[:, :], in_=ident[:, :], compare_op=ALU.not_equal, fill=1.0,
                                    base=0, pattern=[[-1, P]], channel_multiplier=1).then_inc(made, 1)
            nc.gpsimd.affine_select(out=upper[:, :], in_=ones[:, :], compare_op=ALU.is_gt, fill=0.0,
                                    base=0, pattern=[[1, P]], channel_multiplier=-1).then_inc(made, 1)
            nc.gpsimd.iota(r_slot_i[:, :], pattern=[[1, RT]], base=0, channel_multiplier=RT).then_inc(r_ready, 1)
            nc.gpsimd.iota(tok_g[:, 0, 0:CT, 0:2], pattern=[[CAP, E]], base=0, channel_multiplier=0
                           ).then_inc(r_ready, 1)
            pool.wait_ge(r_ready, 3)
            nc.gpsimd.tensor_copy(r_tok[:, :], r_slot_i[:, :]).then_inc(r_ready, 1)
            nc.gpsimd.tensor_copy(r_first[:, :], tok_g[:, 0, 0:CT, 0:2].rearrange("p a b -> p (a b)")
                                  ).then_inc(r_ready, 1)
            rows = (SLOTS + RING * CHUNK) // P
            for top in range(0, rows, RT):
                k = min(RT, rows - top)
                pool.dma_start(slot_t[P * top:P * (top + k), :].rearrange("(p k) c -> p k c", p=P),
                               r_pair[:, 0:k, :]).then_inc(table_cleared, 16)
            pool.wait_ge(table_cleared, 16 * CLEAR_DMAS)
            pool.wait_ge(consts, 16 * CONST_DMAS)

            def inverse_deviation(k, tiles, seen, n, eps, eps_sem, out_sem):
                pool.wait_ge(seen, done(n))
                settle(pool)
                nc.gpsimd.tensor_scalar(veps[:, k, 0:tiles], mv[:, k, 0:tiles, 1], eps, None, ALU.add
                                        ).then_inc(eps_sem, 1)
                pool.wait_ge(eps_sem, n + 1)
                nc.gpsimd.tensor_tensor(rstd[:, k, 0:tiles], veps[:, k, 0:tiles], half[:, 0:tiles], ALU.pow
                                        ).then_inc(out_sem, 1)

            def scatter_tokens(first, count):
                for t in range(first, first + count):
                    nc.gpsimd.indirect_dma_start(
                        out=slot_t, out_offset=bass.IndirectOffsetOnAxis(ap=r_slot_i[:, t:t + 1], axis=0),
                        in_=r_pair[:, t, :], in_offset=None, bounds_check=SLOTS - 1, oob_is_err=False
                    ).then_inc(r_scattered, 16)

            def slots_written(i):
                pool.wait_ge(r_scattered, i * (16 * RT) + 16 * RT)
                pool.sem_inc(r_free, 1)

            def image(b, routing):
                def phase1(s):
                    q = s.plus(2)
                    if q.valid(STEPS):
                        inverse_deviation(0, TT, stat1, st_of(b, q), 1e-6, eps1, rstd1)

                run_steps(pool, -2, STEPS - 3, LO, HI, phase1, settle)
                for n in range(2):
                    pool.wait_ge(qk_stored[n], b * (16 * STEPS) + (16 * STEPS + 32))
                    settle(pool)

                def phase2(s):
                    q = s.plus(1)
                    if q.valid(STEPS):
                        pool.wait_ge(s_ready, freed(b * (2 * STEPS) + (q.index + STEPS), 2))
                        settle(pool)
                        cols = bass.ds(q.index * LINES, LINES)
                        for dst, src in ((q_st, q_img), (k_st, k_img)):
                            nc.gpsimd.tensor_copy(
                                dst[:, q.par].rearrange("p c (w h) -> p c w h", h=H),
                                src[:, :, :].rearrange("p c (h w) -> p c w h", w=W)[:, :, cols, :]
                            ).then_inc(staged, 1)
                    q = s.plus(-2)
                    if q.valid(STEPS):
                        inverse_deviation(1, TT, stat2, st_of(b, q), 1e-5, eps2, rstd2)
                    if s.valid(STEPS):
                        pool.wait_ge(xr_load[s.par], half_of(b, s) * 32 + 32)
                        nc.gpsimd.tensor_tensor(x_r[:, s.par], x_r[:, s.par],
                                                bo_sb[:, :].unsqueeze(1).broadcast_to([P, TT, C]), ALU.add
                                                ).then_inc(xb_ready, 1)
                    if routing and not s.inside and s.index in SCATTER_STEPS:
                        if s.index == SCATTER_STEPS[0]:
                            pool.wait_ge(r_slots_ready, b)
                            settle(pool)
                        each = RT // len(SCATTER_STEPS)
                        scatter_tokens(SCATTER_STEPS.index(s.index) * each, each)

                run_steps(pool, -1, STEPS + 1, LO, HI, phase2, settle)
                if routing:
                    slots_written(b - 1)

            image(0, False)
            with pool.Fori(1, IMGS) as b:
                image(b, True)
            pool.wait_ge(r_slots_ready, IMGS)
            scatter_tokens(0, RT)
            slots_written(IMGS - 1)

            for n in range(2):
                pool.wait_ge(x2_stored[n], 32 * IMGS * STEPS + 64)
                settle(pool)

            pool.sem_inc(attention_over, 1)

            def gather(h, ring):
                pool.wait_ge(tok_load[ring], h * 16 + 16)
                settle(pool)
                for i in range(CT):
                    nc.gpsimd.indirect_dma_start(
                        out=xg[ring][:, i, :], out_offset=None, in_=x2_t,
                        in_offset=bass.IndirectOffsetOnAxis(ap=tok_g[:, ring, i, 0:1], axis=0),
                        bounds_check=TOK - 1, oob_is_err=False).then_inc(gathered[ring], 16)

            def inverse_deviations(n, par):
                pool.wait_ge(f_aggr, n + 1)
                settle(pool)
                nc.gpsimd.tensor_scalar(veps[:, par, :], mv[:, par, :, 1], 1e-5, None, ALU.add).then_inc(f_eps, 1)
                pool.wait_ge(f_eps, n + 1)
                nc.gpsimd.tensor_tensor(rstd[:, par, :], veps[:, par, :], half[:, :], ALU.pow).then_inc(f_rstd, 1)

            for ring in range(RING):
                nc.gpsimd.memset(xg[ring][:, :, :], 0.0).then_inc(xg_cleared, 1)
            pool.wait_ge(xg_cleared, RING)
            for ring in range(RING):
                gather(0, ring)
            for n in range(3):
                inverse_deviations(n, n % 2)
            with pool.Fori(0, E * CHUNKS // RING) as h:
                for ring in range(RING):
                    n = h * RING + ring
                    par = ring % 2
                    inverse_deviations(n + 3, 1 - par)
                    pool.wait_ge(yo_ready, done(n))
                    settle(pool)
                    gather(h + 1, ring)
                    for i in range(CT):
                        nc.gpsimd.indirect_dma_start(
                            out=out_t, out_offset=bass.IndirectOffsetOnAxis(ap=tok_s[:, par, i:i + 1], axis=0),
                            in_=yo[par][:, i, :], in_offset=None, bounds_check=TOK - 1, oob_is_err=False
                        ).then_inc(scattered[par], 16)
                    pool.wait_ge(scattered[par], h * (2 * 16 * CT) + (ring // 2 + 1) * (16 * CT))
                    pool.sem_inc(yo_free, 1)
            for ring in range(RING):
                pool.wait_ge(gathered[ring], (E * CHUNKS // RING + 1) * (16 * CT))


_INS = ["x", "mask_h", "mask_w", "wqT", "bq", "wkT", "bk", "wvT", "bv", "wlepe", "blepe", "woT", "bo",
        "gate_w", "gate_b", "w1", "b1", "w2", "b2"]


def kernel(x, L0_conv_mask_h, L0_conv_mask_w, L0_conv_Wq, L0_conv_bq, L0_conv_Wk, L0_conv_bk, L0_conv_Wv,
           L0_conv_bv, L0_conv_Wlepe, L0_conv_blepe, L0_conv_Wo, L0_conv_bo, L0_ffn_gate_w, L0_ffn_gate_b,
           L0_ffn_w1, L0_ffn_b1, L0_ffn_w2, L0_ffn_b2):
    import concourse.bacc as bacc
    from concourse.bass_utils import run_bass_kernel_spmd

    def rows(a):
        return np.ascontiguousarray(a)

    channels = np.shape(x)[-1]
    experts, width = np.shape(L0_ffn_b1)

    def by_value(a):
        split = np.reshape(a, np.shape(a)[:-1] + (HEADS, KEY_DIM))
        return np.ascontiguousarray(np.reshape(np.swapaxes(split, -1, -2), np.shape(a)))

    data = {
        "x": rows(x), "mask_h": rows(L0_conv_mask_h), "mask_w": rows(L0_conv_mask_w),
        "wqT": rows(np.transpose(L0_conv_Wq)), "bq": rows(L0_conv_bq),
        "wkT": rows(np.transpose(L0_conv_Wk)), "bk": rows(L0_conv_bk),
        "wvT": by_value(np.transpose(L0_conv_Wv)), "bv": by_value(L0_conv_bv),
        "wlepe": rows(np.transpose(by_value(np.reshape(L0_conv_Wlepe, (TAPS, channels))))),
        "blepe": by_value(L0_conv_blepe),
        "woT": rows(np.transpose(by_value(L0_conv_Wo))), "bo": rows(L0_conv_bo),
        "gate_w": rows(L0_ffn_gate_w), "gate_b": rows(L0_ffn_gate_b),
        "w1": rows(L0_ffn_w1),
        "b1": rows(np.reshape(np.transpose(np.reshape(L0_ffn_b1, (experts, width // P, P)), (2, 0, 1)), (P, -1))),
        "w2": rows(L0_ffn_w2), "b2": rows(L0_ffn_b2),
    }
    nc = bacc.Bacc("TRN2", target_bir_lowering=False, num_devices=1)
    arrays, args = {}, []
    for name in _INS:
        a = data[name]
        arrays[f"in_{name}"] = a
        args.append(nc.dram_tensor(f"in_{name}", a.shape, mybir.dt.from_np(a.dtype), kind="ExternalInput").ap())
    out = nc.dram_tensor("out_0", data["x"].shape, F32, kind="ExternalOutput").ap()
    metaformer_kernel(nc, *args, out)
    result = run_bass_kernel_spmd(nc, [arrays], core_ids=[0])
    return result.results[0]["out_0"]
```
